# Optimizing a Trainium2 kernel written in Bass

```python
import numpy as np
import jax
import jax.numpy as jnp

def _softmax(x, axis=-1):
    return jax.nn.softmax(x, axis=axis)

def _gelu(x):
    return jax.nn.gelu(x, approximate=True)

def _silu(x):
    return jax.nn.silu(x)

def _sigmoid(x):
    return jax.nn.sigmoid(x)

def _layernorm(x, axis=-1, eps=1e-05):
    m = jnp.mean(x, axis=axis, keepdims=True)
    v = jnp.var(x, axis=axis, keepdims=True)
    return (x - m) / jnp.sqrt(v + eps)

def _scatter_add(tgt, idx, src, axis=0):
    return tgt.at[idx].add(src)

def _segment_sum(src, seg, n):
    return jax.ops.segment_sum(src, seg, n)
kernel_name = 'mk_perceiver_d4_seqx_r4_fa06ec'

def setup_inputs(seed: int=0):
    np.random.seed(seed)
    _w = jnp.asarray

    def _rec_inputs():
        import jax
        import jax.numpy as jnp
        _rk = jax.random.key(seed)
        x = -0.000125 + 0.9999 * jax.random.normal(jax.random.fold_in(_rk, 1), (16, 64, 256), jnp.float32)
        _lenS = 64 - jax.random.randint(jax.random.fold_in(_rk, 7), (16,), 0, max(1, 64 // 4) + 1, jnp.int32)
        _lenS2 = 1024 - jax.random.randint(jax.random.fold_in(_rk, 8), (16,), 0, max(1, 1024 // 4) + 1, jnp.int32)
        _ctx_768P = jax.random.normal(jax.random.fold_in(_rk, 11), (16, 16, 192), jnp.float32)
        _ctx_768c = jax.random.dirichlet(jax.random.fold_in(_rk, 511), 0.3 * jnp.ones((16,), jnp.float32), (16, 1024))
        _ctx_768t = jnp.einsum('bsk,bkd->bsd', _ctx_768c, _ctx_768P)
        _ctx_768t = _ctx_768t * jax.lax.rsqrt(jnp.mean(jnp.square(_ctx_768t)) + 1e-12) * 0.953939
        ctx_768 = -5.15168e-05 + 0.999825 * (_ctx_768t + 0.3 * jax.random.normal(jax.random.fold_in(_rk, 611), (16, 1024, 192), jnp.float32))
        return (x, ctx_768)
    x, ctx_768 = _rec_inputs()

    def _L0_xattn_setup():
        import jax, jax.numpy as jnp
        import numpy as np
        Q_DIM, K_DIM, V_DIM, OUT_DIM = (256, 192, 192, 256)
        key = jax.random.key(seed)
        ks = jax.random.split(key, 9)
        s = lambda d: 1.0 / np.sqrt(d)
        return {'query': jax.random.normal(ks[0], (16, 512, Q_DIM), jnp.float32), 'key': jax.random.normal(ks[1], (16, 512, K_DIM), jnp.float32), 'value': jax.random.normal(ks[2], (16, 512, V_DIM), jnp.float32), 'Wq': jax.random.uniform(ks[3], (OUT_DIM, Q_DIM), jnp.float32, -s(Q_DIM), s(Q_DIM)), 'bq': jax.random.uniform(ks[4], (OUT_DIM,), jnp.float32, -s(Q_DIM), s(Q_DIM)), 'Wk': jax.random.uniform(ks[5], (OUT_DIM, K_DIM), jnp.float32, -s(K_DIM), s(K_DIM)), 'bk': jax.random.uniform(ks[6], (OUT_DIM,), jnp.float32, -s(K_DIM), s(K_DIM)), 'Wv': jax.random.uniform(ks[7], (OUT_DIM, V_DIM), jnp.float32, -s(V_DIM), s(V_DIM)), 'bv': jax.random.uniform(ks[8], (OUT_DIM,), jnp.float32, -s(V_DIM), s(V_DIM))}
    _L0_xattn_all = _L0_xattn_setup()
    _L0_xattn_in = {k: v for k, v in _L0_xattn_all.items() if k in ('Wq', 'bq', 'Wk', 'bk', 'Wv', 'bv')}
    del _L0_xattn_all

    def _L0_attn_setup():
        import jax, jax.numpy as jnp
        import numpy as np
        B, T, C = (4, 1024, 256)
        H = 16
        LS = 64
        EPS = 1e-06

        def rmsnorm(x, w):
            xf = x.astype(jnp.float32)
            y = xf * jax.lax.rsqrt(jnp.mean(xf * xf, axis=-1, keepdims=True) + EPS)
            return y.astype(x.dtype) * w
        key = jax.random.key(seed)
        k1, k2, k3 = jax.random.split(key, 3)
        x = jax.random.normal(k1, (B, T, C), dtype=jnp.float32)
        w_qkv = jax.random.normal(k2, (C, 3 * C), dtype=jnp.float32) * (1.0 / np.sqrt(C))
        ln_w = jnp.ones((C,), dtype=jnp.float32)
        w_proj = jax.random.normal(k3, (C, C), dtype=jnp.float32) * (1.0 / np.sqrt(C))
        return {'x': x, 'w_qkv': w_qkv, 'ln_w': ln_w, 'w_proj': w_proj}
    _L0_attn_all = _L0_attn_setup()
    _L0_attn_in = {k: v for k, v in _L0_attn_all.items() if k in ('w_qkv', 'ln_w', 'w_proj')}
    del _L0_attn_all

    def _L0_ffn_setup():
        import jax, jax.numpy as jnp
        import numpy as np
        DIM = 256
        HIDDEN = 1024
        E = 8
        K = 2

        def _ffn_hidden(h, multiple_of=64):
            h = int(2 * h / 3)
            return multiple_of * ((h + multiple_of - 1) // multiple_of)
        EXP_HID = _ffn_hidden(HIDDEN)
        SH_HID = _ffn_hidden(HIDDEN // 2)

        def _swiglu(t, a, b, c):
            return jax.nn.silu(t @ a) * (t @ c) @ b
        key = jax.random.key(seed)
        ks = jax.random.split(key, 8)

        def xavier(k, shape, fan_in, fan_out):
            lim = np.sqrt(6.0 / (fan_in + fan_out)).astype(np.float32)
            return jax.random.uniform(k, shape, jnp.float32, -lim, lim)
        return {'x': jax.random.normal(ks[0], (2, 512, DIM), jnp.float32), 'gate_w': xavier(ks[1], (E, DIM), DIM, E), 'w1': xavier(ks[2], (E, DIM, EXP_HID), DIM, EXP_HID), 'w2': xavier(ks[3], (E, EXP_HID, DIM), EXP_HID, DIM), 'w3': xavier(ks[4], (E, DIM, EXP_HID), DIM, EXP_HID), 'sw1': xavier(ks[5], (DIM, SH_HID), DIM, SH_HID), 'sw2': xavier(ks[6], (SH_HID, DIM), SH_HID, DIM), 'sw3': xavier(ks[7], (DIM, SH_HID), DIM, SH_HID)}
    _L0_ffn_all = _L0_ffn_setup()
    _L0_ffn_in = {k: v for k, v in _L0_ffn_all.items() if k in ('gate_w', 'w1', 'w2', 'w3', 'sw1', 'sw2', 'sw3')}
    del _L0_ffn_all

    def _L1_xattn_setup():
        import jax, jax.numpy as jnp
        import numpy as np
        N_HEADS = 16
        key = jax.random.key(seed)
        ks = jax.random.split(key, 8)
        b, l, m = (8, 256, 256)
        d_embed, d_cross = (256, 192)
        s_q = 1.0 / np.sqrt(d_embed)
        s_kv = 1.0 / np.sqrt(d_cross)
        return {'x': jax.random.normal(ks[0], (b, l, d_embed), jnp.float32), 'y': jax.random.normal(ks[1], (b, m, d_cross), jnp.float32), 'Wq': jax.random.normal(ks[2], (d_embed, d_embed), jnp.float32) * s_q, 'bq': jax.random.normal(ks[3], (d_embed,), jnp.float32) * 0.01, 'Wkv': jax.random.normal(ks[4], (2 * d_embed, d_cross), jnp.float32) * s_kv, 'bkv': jax.random.normal(ks[5], (2 * d_embed,), jnp.float32) * 0.01, 'Wo': jax.random.normal(ks[6], (d_embed, d_embed), jnp.float32) * s_q, 'bo': jax.random.normal(ks[7], (d_embed,), jnp.float32) * 0.01}
    _L1_xattn_all = _L1_xattn_setup()
    _L1_xattn_in = {k: v for k, v in _L1_xattn_all.items() if k in ('Wq', 'bq', 'Wkv', 'bkv', 'Wo', 'bo')}
    del _L1_xattn_all

    def _L1_attn_setup():
        import jax, jax.numpy as jnp
        import numpy as np
        EPS = 1e-05

        def _ln(x, g, b):
            m = jnp.mean(x, axis=-1, keepdims=True)
            v = jnp.mean((x - m) ** 2, axis=-1, keepdims=True)
            return (x - m) * jax.lax.rsqrt(v + EPS) * g + b

        def _forward(x, ln_attn_g, ln_attn_b, Wq, bq, Wk, bk, Wv, bv, ln_conv_g, ln_conv_b, conv_w, conv_b, ln_boom_g, ln_boom_b, Wb, bb, Wu, bu):
            B, S, D = x.shape
            K = conv_w.shape[-1]
            G = D // conv_w.shape[1]
            h = _ln(x, ln_conv_g, ln_conv_b)
            hc = jnp.transpose(h, (0, 2, 1))
            hc = jnp.pad(hc, ((0, 0), (0, 0), (K - 1, 0)))
            conv = jax.lax.conv_general_dilated(hc, conv_w, window_strides=(1,), padding='VALID', dimension_numbers=('NCH', 'OIH', 'NCH'), feature_group_count=G)
            conv = conv + conv_b[None, :, None]
            x = x + jnp.transpose(conv, (0, 2, 1))
            h = _ln(x, ln_attn_g, ln_attn_b)
            q = jnp.einsum('bsd,ed->bse', h, Wq) + bq
            k = jnp.einsum('bsd,ed->bse', h, Wk) + bk
            v = jnp.einsum('bsd,ed->bse', h, Wv) + bv
            scale = jnp.arange(1, S + 1, dtype=x.dtype)[None, :, None]
            pooled_q = jnp.cumsum(q, axis=1) / scale
            pooled_k = jnp.cumsum(pooled_q * k, axis=1) / scale
            x = x + pooled_k * v
            h = _ln(x, ln_boom_g, ln_boom_b)
            h = jax.nn.gelu(jnp.einsum('bsd,ed->bse', h, Wb) + bb, approximate=False)
            h = jnp.einsum('bse,de->bsd', h, Wu) + bu
            return x + h
        key = jax.random.key(seed)
        ks = jax.random.split(key, 8)
        B, S, D, K, G = (4, 512, 256, 4, 4)
        w = lambda k, shape: jax.random.normal(k, shape, jnp.float32) * 0.02
        return {'hidden_states': jax.random.normal(ks[0], (B, S, D), jnp.float32), 'attention_mask': jnp.ones((B, S), jnp.int32), 'ln_attn_g': jnp.ones((D,), jnp.float32), 'ln_attn_b': jnp.zeros((D,), jnp.float32), 'Wq': w(ks[1], (D, D)), 'bq': jnp.zeros((D,), jnp.float32), 'Wk': w(ks[2], (D, D)), 'bk': jnp.zeros((D,), jnp.float32), 'Wv': w(ks[3], (D, D)), 'bv': jnp.zeros((D,), jnp.float32), 'ln_conv_g': jnp.ones((D,), jnp.float32), 'ln_conv_b': jnp.zeros((D,), jnp.float32), 'conv_w': w(ks[4], (D, D // G, K)), 'conv_b': jnp.zeros((D,), jnp.float32), 'ln_boom_g': jnp.ones((D,), jnp.float32), 'ln_boom_b': jnp.zeros((D,), jnp.float32), 'Wb': w(ks[5], (4 * D, D)), 'bb': jnp.zeros((4 * D,), jnp.float32), 'Wu': w(ks[6], (D, 4 * D)), 'bu': jnp.zeros((D,), jnp.float32)}
    _L1_attn_all = _L1_attn_setup()
    _L1_attn_in = {k: v for k, v in _L1_attn_all.items() if k in ('attention_mask', 'ln_attn_g', 'ln_attn_b', 'Wq', 'bq', 'Wk', 'bk', 'Wv', 'bv', 'ln_conv_g', 'ln_conv_b', 'conv_w', 'conv_b', 'ln_boom_g', 'ln_boom_b', 'Wb', 'bb', 'Wu', 'bu')}
    del _L1_attn_all

    def _L1_ffn_setup():
        import jax, jax.numpy as jnp
        import numpy as np
        D_MODEL = 256
        D_FF = 1024
        N_EXPERTS = 8
        INIT_SCALE = 0.1

        def _trunc_normal(key, shape, std):
            return std * jax.random.truncated_normal(key, -2.0, 2.0, shape, dtype=jnp.float32)
        key = jax.random.key(seed)
        ks = jax.random.split(key, 5)
        x = jax.random.normal(ks[0], (4, 256, D_MODEL), dtype=jnp.float32)
        router_W = _trunc_normal(ks[1], (D_MODEL, N_EXPERTS), INIT_SCALE / np.sqrt(D_MODEL))
        router_b = jnp.zeros((N_EXPERTS,), dtype=jnp.float32)
        W1 = _trunc_normal(ks[2], (N_EXPERTS, D_MODEL, D_FF), INIT_SCALE / np.sqrt(D_MODEL))
        b1 = jnp.zeros((N_EXPERTS, D_FF), dtype=jnp.float32)
        W2 = _trunc_normal(ks[3], (N_EXPERTS, D_FF, D_MODEL), INIT_SCALE / np.sqrt(D_FF))
        b2 = jnp.zeros((N_EXPERTS, D_MODEL), dtype=jnp.float32)
        return {'x': x, 'router_W': router_W, 'router_b': router_b, 'W1': W1, 'b1': b1, 'W2': W2, 'b2': b2}
    _L1_ffn_all = _L1_ffn_setup()
    _L1_ffn_in = {k: v for k, v in _L1_ffn_all.items() if k in ('router_W', 'router_b', 'W1', 'b1', 'W2', 'b2')}
    del _L1_ffn_all

    def _L2_xattn_setup():
        import jax, jax.numpy as jnp
        import numpy as np
        HEADS = 8
        DIM_HEAD = 64
        QUERY_DIM = 256
        CONTEXT_DIM = 192
        INNER = HEADS * DIM_HEAD
        key = jax.random.key(seed)
        ks = jax.random.split(key, 7)
        B, Sq, Skv = (4, 1024, 256)
        x = jax.random.normal(ks[0], (B, Sq, QUERY_DIM), dtype=jnp.float32)
        context = jax.random.normal(ks[1], (B, Skv, CONTEXT_DIM), dtype=jnp.float32)
        Wq = jax.random.normal(ks[2], (QUERY_DIM, INNER), dtype=jnp.float32) * QUERY_DIM ** (-0.5)
        Wk = jax.random.normal(ks[3], (CONTEXT_DIM, INNER), dtype=jnp.float32) * CONTEXT_DIM ** (-0.5)
        Wv = jax.random.normal(ks[4], (CONTEXT_DIM, INNER), dtype=jnp.float32) * CONTEXT_DIM ** (-0.5)
        Wo = jax.random.normal(ks[5], (INNER, QUERY_DIM), dtype=jnp.float32) * INNER ** (-0.5)
        bo = jax.random.normal(ks[6], (QUERY_DIM,), dtype=jnp.float32) * 0.01
        return {'x': x, 'context': context, 'Wq': Wq, 'Wk': Wk, 'Wv': Wv, 'Wo': Wo, 'bo': bo}
    _L2_xattn_all = _L2_xattn_setup()
    _L2_xattn_in = {k: v for k, v in _L2_xattn_all.items() if k in ('Wq', 'Wk', 'Wv', 'Wo', 'bo')}
    del _L2_xattn_all

    def _L2_attn_setup():
        import jax, jax.numpy as jnp
        import numpy as np
        B, L, D_OUT, D_HIDDEN = (16, 1024, 256, 128)
        MAX_PHASE = 6.28
        R_MIN, R_MAX = (0.9, 0.999)

        def _binop(q_i, q_j):
            A_i, b_i = q_i
            A_j, b_j = q_j
            return (A_j * A_i, A_j * b_i + b_j)

        def _reference_tuple_inner(x, theta_log, nu_log, gamma_log, B_re, B_im, C_re, C_im, D):
            diag_lambda = jnp.exp(-jnp.exp(nu_log) + 1j * jnp.exp(theta_log))
            B_norm = (B_re + 1j * B_im) * jnp.exp(gamma_log)[:, None]
            C = C_re + 1j * C_im
            Bu = jnp.einsum('hd,bld->blh', B_norm, x.astype(B_norm.dtype))
            Lam = jnp.broadcast_to(diag_lambda, Bu.shape)
            _, h = jax.lax.associative_scan(_binop, (Lam, Bu), axis=1)
            y = jnp.einsum('oh,blh->blo', C, h).real + D * x
            return (y, h[:, -1])
        key = jax.random.key(seed)
        ks = jax.random.split(key, 8)
        x = jax.random.normal(ks[0], (B, L, D_OUT), dtype=jnp.float32)
        u_th = jax.random.uniform(ks[1], (D_HIDDEN,), dtype=jnp.float32)
        theta_log = jnp.log(MAX_PHASE * u_th)
        u_nu = jax.random.uniform(ks[2], (D_HIDDEN,), dtype=jnp.float32)
        nu_log = jnp.log(-0.5 * jnp.log(u_nu * (R_MAX ** 2 - R_MIN ** 2) + R_MIN ** 2))
        diag_lambda = jnp.exp(-jnp.exp(nu_log) + 1j * jnp.exp(theta_log))
        gamma_log = jnp.log(jnp.sqrt(1.0 - jnp.abs(diag_lambda) ** 2))
        b_norm = jnp.sqrt(2.0 * D_OUT)
        c_norm = jnp.sqrt(float(D_HIDDEN))
        B_re = jax.random.normal(ks[3], (D_HIDDEN, D_OUT), dtype=jnp.float32) / b_norm
        B_im = jax.random.normal(ks[4], (D_HIDDEN, D_OUT), dtype=jnp.float32) / b_norm
        C_re = jax.random.normal(ks[5], (D_OUT, D_HIDDEN), dtype=jnp.float32) / c_norm
        C_im = jax.random.normal(ks[6], (D_OUT, D_HIDDEN), dtype=jnp.float32) / c_norm
        D = jax.random.normal(ks[7], (D_OUT,), dtype=jnp.float32)
        return {'x': x, 'theta_log': theta_log, 'nu_log': nu_log, 'gamma_log': gamma_log, 'B_re': B_re, 'B_im': B_im, 'C_re': C_re, 'C_im': C_im, 'D': D}
    _L2_attn_all = _L2_attn_setup()
    _L2_attn_in = {k: v for k, v in _L2_attn_all.items() if k in ('theta_log', 'nu_log', 'gamma_log', 'B_re', 'B_im', 'C_re', 'C_im', 'D')}
    del _L2_attn_all

    def _L2_ffn_setup():
        import jax, jax.numpy as jnp
        import numpy as np
        D = 256
        H = 1024
        E = 8
        TOPK = 2
        CAP_F = 1.25
        key = jax.random.key(seed)
        ks = jax.random.split(key, 6)
        sc = 0.02
        return {'x': jax.random.normal(ks[0], (4, 512, D), jnp.float32), 'Wg': jax.random.normal(ks[1], (D, E), jnp.float32) * sc, 'bg': jnp.zeros((E,), jnp.float32), 'W1': jax.random.normal(ks[2], (E, D, H), jnp.float32) * sc, 'W2': jax.random.normal(ks[3], (E, D, H), jnp.float32) * sc, 'W3': jax.random.normal(ks[4], (E, H, D), jnp.float32) * sc}
    _L2_ffn_all = _L2_ffn_setup()
    _L2_ffn_in = {k: v for k, v in _L2_ffn_all.items() if k in ('Wg', 'bg', 'W1', 'W2', 'W3')}
    del _L2_ffn_all

    def _L3_xattn_setup():
        import jax, jax.numpy as jnp
        import numpy as np
        HEADS = 8
        DIM_HEAD = 64
        SCALE = DIM_HEAD ** (-0.5)
        key = jax.random.key(seed)
        ks = jax.random.split(key, 7)
        B, Nq, Nc = (4, 512, 512)
        Dq, Dc = (256, 192)
        inner = HEADS * DIM_HEAD
        x = jax.random.normal(ks[0], (B, Nq, Dq), dtype=jnp.float32)
        context = jax.random.normal(ks[1], (B, Nc, Dc), dtype=jnp.float32)
        Wq = jax.random.normal(ks[2], (Dq, inner), dtype=jnp.float32) * Dq ** (-0.5)
        Wk = jax.random.normal(ks[3], (Dc, inner), dtype=jnp.float32) * Dc ** (-0.5)
        Wv = jax.random.normal(ks[4], (Dc, inner), dtype=jnp.float32) * Dc ** (-0.5)
        Wo = jax.random.normal(ks[5], (inner, Dq), dtype=jnp.float32) * inner ** (-0.5)
        bo = jax.random.normal(ks[6], (Dq,), dtype=jnp.float32) * 0.01
        return {'x': x, 'context': context, 'Wq': Wq, 'Wk': Wk, 'Wv': Wv, 'Wo': Wo, 'bo': bo}
    _L3_xattn_all = _L3_xattn_setup()
    _L3_xattn_in = {k: v for k, v in _L3_xattn_all.items() if k in ('Wq', 'Wk', 'Wv', 'Wo', 'bo')}
    del _L3_xattn_all

    def _L3_attn_setup():
        import jax, jax.numpy as jnp
        import numpy as np
        D_MODEL = 256
        D_STATE = 16
        D_CONV = 3
        D_INNER = 2 * D_MODEL
        B, S = (4, 512)

        def _mamba_forward(x, in_proj_w, conv_w, conv_b, x_proj_w, dt_proj_w, dt_proj_b, out_proj_w, A_log, D_param):
            combined = x @ in_proj_w
            u, x_gate = jnp.split(combined, 2, axis=-1)
            u_c = jax.lax.conv_general_dilated(u.transpose(0, 2, 1), conv_w, window_strides=(1,), padding='SAME', feature_group_count=D_INNER, dimension_numbers=('NCW', 'OIW', 'NCW'))
            u = jax.nn.silu((u_c + conv_b[None, :, None]).transpose(0, 2, 1))
            x_dbl = u @ x_proj_w
            delta, b, c = jnp.split(x_dbl, [D_INNER, D_INNER + D_STATE], axis=-1)
            delta = jax.nn.softplus(delta @ dt_proj_w + dt_proj_b)
            a = -jnp.exp(A_log)

            def step(h, inp):
                u_t, d_t, b_t, c_t = inp
                h = jnp.exp(d_t[:, :, None] * a) * h + d_t[:, :, None] * b_t[:, None, :] * u_t[:, :, None]
                y_t = jnp.einsum('bds,bs->bd', h, c_t)
                return (h, y_t)
            h0 = jnp.zeros((x.shape[0], D_INNER, D_STATE), x.dtype)
            xs = (u.transpose(1, 0, 2), delta.transpose(1, 0, 2), b.transpose(1, 0, 2), c.transpose(1, 0, 2))
            _, ys = jax.lax.scan(step, h0, xs)
            y = ys.transpose(1, 0, 2)
            y = y + u * D_param
            y = y * jax.nn.silu(x_gate)
            return y @ out_proj_w
        key = jax.random.key(seed)
        ks = jax.random.split(key, 9)
        s = 0.02
        x = jax.random.normal(ks[0], (B, S, D_MODEL), jnp.float32)
        in_proj_w = jax.random.normal(ks[1], (D_MODEL, 2 * D_INNER), jnp.float32) * s
        conv_w = jax.random.normal(ks[2], (D_INNER, 1, D_CONV), jnp.float32) * s
        conv_b = jax.random.normal(ks[3], (D_INNER,), jnp.float32) * s
        x_proj_w = jax.random.normal(ks[4], (D_INNER, D_INNER + 2 * D_STATE), jnp.float32) * s
        dt_proj_w = jax.random.normal(ks[5], (D_INNER, D_INNER), jnp.float32) * s
        dt_proj_b = jax.random.normal(ks[6], (D_INNER,), jnp.float32) * s
        out_proj_w = jax.random.normal(ks[7], (D_INNER, D_MODEL), jnp.float32) * s
        A_log = jnp.tile(jnp.log(jnp.arange(1, D_STATE + 1, dtype=jnp.float32))[None, :], (D_INNER, 1))
        D_param = jnp.ones((D_INNER,), jnp.float32)
        return {'x': x, 'in_proj_w': in_proj_w, 'conv_w': conv_w, 'conv_b': conv_b, 'x_proj_w': x_proj_w, 'dt_proj_w': dt_proj_w, 'dt_proj_b': dt_proj_b, 'out_proj_w': out_proj_w, 'A_log': A_log, 'D_param': D_param}
    _L3_attn_all = _L3_attn_setup()
    _L3_attn_in = {k: v for k, v in _L3_attn_all.items() if k in ('in_proj_w', 'conv_w', 'conv_b', 'x_proj_w', 'dt_proj_w', 'dt_proj_b', 'out_proj_w', 'A_log', 'D_param')}
    del _L3_attn_all

    def _L3_ffn_setup():
        import jax, jax.numpy as jnp
        import numpy as np
        import math
        D_IN = 256
        FEATURES = (1024, 1024, 256)
        BATCH, SEQ = (8, 512)

        def _conn_dense(kernel_bool, x):
            w = jnp.where(kernel_bool, jnp.float32(1.0), jnp.float32(-1.0))
            return x @ w
        key = jax.random.key(seed)
        kx, kk0, kk1, kk2 = jax.random.split(key, 4)
        x = jax.random.normal(kx, (BATCH, SEQ, D_IN), dtype=jnp.float32)
        k0 = jax.random.randint(kk0, (2 * D_IN, FEATURES[0]), 0, 2).astype(jnp.bool_)
        k1 = jax.random.randint(kk1, (FEATURES[0], FEATURES[1]), 0, 2).astype(jnp.bool_)
        k2 = jax.random.randint(kk2, (FEATURES[1], FEATURES[2]), 0, 2).astype(jnp.bool_)
        s0 = jnp.asarray(1.0 / math.sqrt(2 * D_IN), dtype=jnp.float32)
        s1 = jnp.asarray(1.0 / math.sqrt(FEATURES[0]), dtype=jnp.float32)
        s2 = jnp.asarray(1.0 / math.sqrt(FEATURES[1]), dtype=jnp.float32)
        return {'x': x, 'k0': k0, 'k1': k1, 'k2': k2, 's0': s0, 's1': s1, 's2': s2}
    _L3_ffn_all = _L3_ffn_setup()
    _L3_ffn_in = {k: v for k, v in _L3_ffn_all.items() if k in ('k0', 'k1', 'k2', 's0', 's1', 's2')}
    del _L3_ffn_all
    return {'x': x, 'ctx_768': ctx_768, 'L0_xattn_Wq': _L0_xattn_in['Wq'], 'L0_xattn_bq': _L0_xattn_in['bq'], 'L0_xattn_Wk': _L0_xattn_in['Wk'], 'L0_xattn_bk': _L0_xattn_in['bk'], 'L0_xattn_Wv': _L0_xattn_in['Wv'], 'L0_xattn_bv': _L0_xattn_in['bv'], 'L0_attn_w_qkv': _L0_attn_in['w_qkv'], 'L0_attn_ln_w': _L0_attn_in['ln_w'], 'L0_attn_w_proj': _L0_attn_in['w_proj'], 'L0_ffn_gate_w': _L0_ffn_in['gate_w'], 'L0_ffn_w1': _L0_ffn_in['w1'], 'L0_ffn_w2': _L0_ffn_in['w2'], 'L0_ffn_w3': _L0_ffn_in['w3'], 'L0_ffn_sw1': _L0_ffn_in['sw1'], 'L0_ffn_sw2': _L0_ffn_in['sw2'], 'L0_ffn_sw3': _L0_ffn_in['sw3'], 'L1_xattn_Wq': _L1_xattn_in['Wq'], 'L1_xattn_bq': _L1_xattn_in['bq'], 'L1_xattn_Wkv': _L1_xattn_in['Wkv'], 'L1_xattn_bkv': _L1_xattn_in['bkv'], 'L1_xattn_Wo': _L1_xattn_in['Wo'], 'L1_xattn_bo': _L1_xattn_in['bo'], 'L1_attn_attention_mask': _L1_attn_in['attention_mask'], 'L1_attn_ln_attn_g': _L1_attn_in['ln_attn_g'], 'L1_attn_ln_attn_b': _L1_attn_in['ln_attn_b'], 'L1_attn_Wq': _L1_attn_in['Wq'], 'L1_attn_bq': _L1_attn_in['bq'], 'L1_attn_Wk': _L1_attn_in['Wk'], 'L1_attn_bk': _L1_attn_in['bk'], 'L1_attn_Wv': _L1_attn_in['Wv'], 'L1_attn_bv': _L1_attn_in['bv'], 'L1_attn_ln_conv_g': _L1_attn_in['ln_conv_g'], 'L1_attn_ln_conv_b': _L1_attn_in['ln_conv_b'], 'L1_attn_conv_w': _L1_attn_in['conv_w'], 'L1_attn_conv_b': _L1_attn_in['conv_b'], 'L1_attn_ln_boom_g': _L1_attn_in['ln_boom_g'], 'L1_attn_ln_boom_b': _L1_attn_in['ln_boom_b'], 'L1_attn_Wb': _L1_attn_in['Wb'], 'L1_attn_bb': _L1_attn_in['bb'], 'L1_attn_Wu': _L1_attn_in['Wu'], 'L1_attn_bu': _L1_attn_in['bu'], 'L1_ffn_router_W': _L1_ffn_in['router_W'], 'L1_ffn_router_b': _L1_ffn_in['router_b'], 'L1_ffn_W1': _L1_ffn_in['W1'], 'L1_ffn_b1': _L1_ffn_in['b1'], 'L1_ffn_W2': _L1_ffn_in['W2'], 'L1_ffn_b2': _L1_ffn_in['b2'], 'L2_xattn_Wq': _L2_xattn_in['Wq'], 'L2_xattn_Wk': _L2_xattn_in['Wk'], 'L2_xattn_Wv': _L2_xattn_in['Wv'], 'L2_xattn_Wo': _L2_xattn_in['Wo'], 'L2_xattn_bo': _L2_xattn_in['bo'], 'L2_attn_theta_log': _L2_attn_in['theta_log'], 'L2_attn_nu_log': _L2_attn_in['nu_log'], 'L2_attn_gamma_log': _L2_attn_in['gamma_log'], 'L2_attn_B_re': _L2_attn_in['B_re'], 'L2_attn_B_im': _L2_attn_in['B_im'], 'L2_attn_C_re': _L2_attn_in['C_re'], 'L2_attn_C_im': _L2_attn_in['C_im'], 'L2_attn_D': _L2_attn_in['D'], 'L2_ffn_Wg': _L2_ffn_in['Wg'], 'L2_ffn_bg': _L2_ffn_in['bg'], 'L2_ffn_W1': _L2_ffn_in['W1'], 'L2_ffn_W2': _L2_ffn_in['W2'], 'L2_ffn_W3': _L2_ffn_in['W3'], 'L3_xattn_Wq': _L3_xattn_in['Wq'], 'L3_xattn_Wk': _L3_xattn_in['Wk'], 'L3_xattn_Wv': _L3_xattn_in['Wv'], 'L3_xattn_Wo': _L3_xattn_in['Wo'], 'L3_xattn_bo': _L3_xattn_in['bo'], 'L3_attn_in_proj_w': _L3_attn_in['in_proj_w'], 'L3_attn_conv_w': _L3_attn_in['conv_w'], 'L3_attn_conv_b': _L3_attn_in['conv_b'], 'L3_attn_x_proj_w': _L3_attn_in['x_proj_w'], 'L3_attn_dt_proj_w': _L3_attn_in['dt_proj_w'], 'L3_attn_dt_proj_b': _L3_attn_in['dt_proj_b'], 'L3_attn_out_proj_w': _L3_attn_in['out_proj_w'], 'L3_attn_A_log': _L3_attn_in['A_log'], 'L3_attn_D_param': _L3_attn_in['D_param'], 'L3_ffn_k0': _L3_ffn_in['k0'], 'L3_ffn_k1': _L3_ffn_in['k1'], 'L3_ffn_k2': _L3_ffn_in['k2'], 'L3_ffn_s0': _L3_ffn_in['s0'], 'L3_ffn_s1': _L3_ffn_in['s1'], 'L3_ffn_s2': _L3_ffn_in['s2']}

def reference(x, ctx_768, L0_xattn_Wq, L0_xattn_bq, L0_xattn_Wk, L0_xattn_bk, L0_xattn_Wv, L0_xattn_bv, L0_attn_w_qkv, L0_attn_ln_w, L0_attn_w_proj, L0_ffn_gate_w, L0_ffn_w1, L0_ffn_w2, L0_ffn_w3, L0_ffn_sw1, L0_ffn_sw2, L0_ffn_sw3, L1_xattn_Wq, L1_xattn_bq, L1_xattn_Wkv, L1_xattn_bkv, L1_xattn_Wo, L1_xattn_bo, L1_attn_attention_mask, L1_attn_ln_attn_g, L1_attn_ln_attn_b, L1_attn_Wq, L1_attn_bq, L1_attn_Wk, L1_attn_bk, L1_attn_Wv, L1_attn_bv, L1_attn_ln_conv_g, L1_attn_ln_conv_b, L1_attn_conv_w, L1_attn_conv_b, L1_attn_ln_boom_g, L1_attn_ln_boom_b, L1_attn_Wb, L1_attn_bb, L1_attn_Wu, L1_attn_bu, L1_ffn_router_W, L1_ffn_router_b, L1_ffn_W1, L1_ffn_b1, L1_ffn_W2, L1_ffn_b2, L2_xattn_Wq, L2_xattn_Wk, L2_xattn_Wv, L2_xattn_Wo, L2_xattn_bo, L2_attn_theta_log, L2_attn_nu_log, L2_attn_gamma_log, L2_attn_B_re, L2_attn_B_im, L2_attn_C_re, L2_attn_C_im, L2_attn_D, L2_ffn_Wg, L2_ffn_bg, L2_ffn_W1, L2_ffn_W2, L2_ffn_W3, L3_xattn_Wq, L3_xattn_Wk, L3_xattn_Wv, L3_xattn_Wo, L3_xattn_bo, L3_attn_in_proj_w, L3_attn_conv_w, L3_attn_conv_b, L3_attn_x_proj_w, L3_attn_dt_proj_w, L3_attn_dt_proj_b, L3_attn_out_proj_w, L3_attn_A_log, L3_attn_D_param, L3_ffn_k0, L3_ffn_k1, L3_ffn_k2, L3_ffn_s0, L3_ffn_s1, L3_ffn_s2):
    import jax
    import jax.numpy as jnp

    def _L0_xattn_ref(query, key, value, Wq, bq, Wk, bk, Wv, bv):
        import jax, jax.numpy as jnp
        import numpy as np
        Q_DIM, K_DIM, V_DIM, OUT_DIM = (256, 192, 192, 256)
        scale = OUT_DIM ** (-0.5)
        q = jnp.einsum('bsd,od->bso', query, Wq) + bq
        k = jnp.einsum('bsd,od->bso', key, Wk) + bk
        v = jnp.einsum('bsd,od->bso', value, Wv) + bv
        scores = jnp.einsum('bqo,bko->bqk', q, k) * scale
        probs = jax.nn.softmax(scores, axis=-1)
        return jnp.einsum('bqk,bko->bqo', probs, v)

    def _L0_attn_ref(x, w_qkv, ln_w, w_proj):
        import jax, jax.numpy as jnp
        import numpy as np
        B, T, C = (4, 1024, 256)
        H = 16
        LS = 64
        EPS = 1e-06

        def rmsnorm(x, w):
            xf = x.astype(jnp.float32)
            y = xf * jax.lax.rsqrt(jnp.mean(xf * xf, axis=-1, keepdims=True) + EPS)
            return y.astype(x.dtype) * w
        Bx, Tx, Cx = x.shape
        ng = Tx // LS
        hd = Cx // H
        xg = x.reshape(Bx, ng, LS, Cx)
        qkv = jnp.einsum('bglc,cd->bgld', xg, w_qkv)
        q, k, v = jnp.split(qkv, 3, axis=-1)
        q = rmsnorm(q, ln_w)
        k = rmsnorm(k, ln_w)
        q = q.reshape(Bx, ng, LS, H, hd).transpose(0, 1, 3, 2, 4)
        k = k.reshape(Bx, ng, LS, H, hd).transpose(0, 1, 3, 2, 4)
        v = v.reshape(Bx, ng, LS, H, hd).transpose(0, 1, 3, 2, 4)
        scale = 1.0 / np.sqrt(hd)
        att = jnp.einsum('bghqd,bghkd->bghqk', q, k) * scale
        causal = jnp.tril(jnp.ones((LS, LS), dtype=bool))
        att = jnp.where(causal, att, -jnp.finfo(att.dtype).max)
        att = jax.nn.softmax(att, axis=-1)
        y = jnp.einsum('bghqk,bghkd->bghqd', att, v)
        y = y.transpose(0, 1, 3, 2, 4).reshape(Bx, Tx, Cx)
        return jnp.einsum('btc,cd->btd', y, w_proj)

    def _L0_ffn_ref(x, gate_w, w1, w2, w3, sw1, sw2, sw3):
        import jax, jax.numpy as jnp
        import numpy as np
        DIM = 256
        HIDDEN = 1024
        E = 8
        K = 2

        def _ffn_hidden(h, multiple_of=64):
            h = int(2 * h / 3)
            return multiple_of * ((h + multiple_of - 1) // multiple_of)
        EXP_HID = _ffn_hidden(HIDDEN)
        SH_HID = _ffn_hidden(HIDDEN // 2)

        def _swiglu(t, a, b, c):
            return jax.nn.silu(t @ a) * (t @ c) @ b
        B, S, D = x.shape
        xt = x.reshape(-1, D)
        T = xt.shape[0]
        logits = xt @ gate_w.T
        scores = jax.nn.softmax(logits, axis=-1)
        topk_w, topk_i = jax.lax.top_k(scores, K)
        comb = jnp.zeros((T, E), x.dtype).at[jnp.arange(T)[:, None], topk_i].add(topk_w)
        y = jnp.zeros_like(xt)
        for e in range(E):
            y = y + comb[:, e:e + 1] * _swiglu(xt, w1[e], w2[e], w3[e])
        y = y.reshape(B, S, D)
        return y + _swiglu(x, sw1, sw2, sw3)

    def _L1_xattn_ref(x, y, Wq, bq, Wkv, bkv, Wo, bo):
        import jax, jax.numpy as jnp
        import numpy as np
        N_HEADS = 16
        b, l, d = x.shape
        m = y.shape[1]
        h = N_HEADS
        dh = d // h
        q = (jnp.einsum('bld,ed->ble', x, Wq) + bq).reshape(b, l, h, dh)
        kv = (jnp.einsum('bmc,ec->bme', y, Wkv) + bkv).reshape(b, m, h, 2 * dh)
        k, v = (kv[..., :dh], kv[..., dh:])
        scale = 1.0 / jnp.sqrt(jnp.asarray(dh, x.dtype))
        att = jax.nn.softmax(jnp.einsum('blhd,bmhd->blmh', q, k) * scale, axis=2)
        out = jnp.einsum('blmh,bmhd->blhd', att, v).reshape(b, l, d)
        return jnp.einsum('bld,ed->ble', out, Wo) + bo

    def _L1_attn_ref(hidden_states, attention_mask, ln_attn_g, ln_attn_b, Wq, bq, Wk, bk, Wv, bv, ln_conv_g, ln_conv_b, conv_w, conv_b, ln_boom_g, ln_boom_b, Wb, bb, Wu, bu):
        import jax, jax.numpy as jnp
        import numpy as np
        EPS = 1e-05

        def _ln(x, g, b):
            m = jnp.mean(x, axis=-1, keepdims=True)
            v = jnp.mean((x - m) ** 2, axis=-1, keepdims=True)
            return (x - m) * jax.lax.rsqrt(v + EPS) * g + b

        def _forward(x, ln_attn_g, ln_attn_b, Wq, bq, Wk, bk, Wv, bv, ln_conv_g, ln_conv_b, conv_w, conv_b, ln_boom_g, ln_boom_b, Wb, bb, Wu, bu):
            B, S, D = x.shape
            K = conv_w.shape[-1]
            G = D // conv_w.shape[1]
            h = _ln(x, ln_conv_g, ln_conv_b)
            hc = jnp.transpose(h, (0, 2, 1))
            hc = jnp.pad(hc, ((0, 0), (0, 0), (K - 1, 0)))
            conv = jax.lax.conv_general_dilated(hc, conv_w, window_strides=(1,), padding='VALID', dimension_numbers=('NCH', 'OIH', 'NCH'), feature_group_count=G)
            conv = conv + conv_b[None, :, None]
            x = x + jnp.transpose(conv, (0, 2, 1))
            h = _ln(x, ln_attn_g, ln_attn_b)
            q = jnp.einsum('bsd,ed->bse', h, Wq) + bq
            k = jnp.einsum('bsd,ed->bse', h, Wk) + bk
            v = jnp.einsum('bsd,ed->bse', h, Wv) + bv
            scale = jnp.arange(1, S + 1, dtype=x.dtype)[None, :, None]
            pooled_q = jnp.cumsum(q, axis=1) / scale
            pooled_k = jnp.cumsum(pooled_q * k, axis=1) / scale
            x = x + pooled_k * v
            h = _ln(x, ln_boom_g, ln_boom_b)
            h = jax.nn.gelu(jnp.einsum('bsd,ed->bse', h, Wb) + bb, approximate=False)
            h = jnp.einsum('bse,de->bsd', h, Wu) + bu
            return x + h
        return _forward(hidden_states, ln_attn_g, ln_attn_b, Wq, bq, Wk, bk, Wv, bv, ln_conv_g, ln_conv_b, conv_w, conv_b, ln_boom_g, ln_boom_b, Wb, bb, Wu, bu)

    def _L1_ffn_ref(x, router_W, router_b, W1, b1, W2, b2):
        import jax, jax.numpy as jnp
        import numpy as np
        D_MODEL = 256
        D_FF = 1024
        N_EXPERTS = 8
        INIT_SCALE = 0.1

        def _trunc_normal(key, shape, std):
            return std * jax.random.truncated_normal(key, -2.0, 2.0, shape, dtype=jnp.float32)
        logits = jnp.einsum('bsd,de->bse', x.astype(jnp.float32), router_W) + router_b
        probs = jax.nn.softmax(logits, axis=-1)
        top1 = jnp.argmax(probs, axis=-1)
        mask = jax.nn.one_hot(top1, N_EXPERTS, dtype=x.dtype)
        gates = mask * probs.astype(x.dtype)
        h = jax.nn.relu(jnp.einsum('bsd,edf->besf', x, W1) + b1[:, None, :])
        y = jnp.einsum('besf,efd->besd', h, W2) + b2[:, None, :]
        out = jnp.einsum('bse,besd->bsd', gates, y)
        return out

    def _L2_xattn_ref(x, context, Wq, Wk, Wv, Wo, bo):
        import jax, jax.numpy as jnp
        import numpy as np
        HEADS = 8
        DIM_HEAD = 64
        QUERY_DIM = 256
        CONTEXT_DIM = 192
        INNER = HEADS * DIM_HEAD
        B, Sq, _ = x.shape
        h, d = (HEADS, DIM_HEAD)
        scale = d ** (-0.5)
        q = (x @ Wq).reshape(B, Sq, h, d).transpose(0, 2, 1, 3)
        k = (context @ Wk).reshape(B, -1, h, d).transpose(0, 2, 1, 3)
        v = (context @ Wv).reshape(B, -1, h, d).transpose(0, 2, 1, 3)
        scores = jnp.einsum('bhid,bhjd->bhij', q, k) * scale
        attn = jax.nn.softmax(scores, axis=-1)
        out = jnp.einsum('bhij,bhjd->bhid', attn, v)
        out = out.transpose(0, 2, 1, 3).reshape(B, Sq, h * d)
        return out @ Wo + bo

    def _L2_attn_ref(x, theta_log, nu_log, gamma_log, B_re, B_im, C_re, C_im, D):
        import jax, jax.numpy as jnp
        import numpy as np
        B, L, D_OUT, D_HIDDEN = (16, 1024, 256, 128)
        MAX_PHASE = 6.28
        R_MIN, R_MAX = (0.9, 0.999)

        def _binop(q_i, q_j):
            A_i, b_i = q_i
            A_j, b_j = q_j
            return (A_j * A_i, A_j * b_i + b_j)

        def _reference_tuple_inner(x, theta_log, nu_log, gamma_log, B_re, B_im, C_re, C_im, D):
            diag_lambda = jnp.exp(-jnp.exp(nu_log) + 1j * jnp.exp(theta_log))
            B_norm = (B_re + 1j * B_im) * jnp.exp(gamma_log)[:, None]
            C = C_re + 1j * C_im
            Bu = jnp.einsum('hd,bld->blh', B_norm, x.astype(B_norm.dtype))
            Lam = jnp.broadcast_to(diag_lambda, Bu.shape)
            _, h = jax.lax.associative_scan(_binop, (Lam, Bu), axis=1)
            y = jnp.einsum('oh,blh->blo', C, h).real + D * x
            return (y, h[:, -1])
        return _reference_tuple_inner(x, theta_log, nu_log, gamma_log, B_re, B_im, C_re, C_im, D)[0]

    def _L2_ffn_ref(x, Wg, bg, W1, W2, W3):
        import jax, jax.numpy as jnp
        import numpy as np
        D = 256
        H = 1024
        E = 8
        TOPK = 2
        CAP_F = 1.25
        b, s, d = x.shape
        xt = x.reshape(-1, d)
        T = xt.shape[0]
        capacity = int(T / E * CAP_F)
        gate_logits = xt @ Wg + bg
        top_v, top_i = jax.lax.top_k(gate_logits, TOPK)
        expert_label = jax.nn.one_hot(top_i, E, dtype=xt.dtype).sum(axis=1)
        seq = jnp.cumsum(expert_label, axis=0) * expert_label
        valid = (seq > 0) & (seq <= capacity)
        slot = (seq - 1.0).astype(jnp.int32)
        flat_idx = jnp.where(valid, jnp.arange(E, dtype=jnp.int32)[None, :] * capacity + slot, E * capacity)
        src = jnp.broadcast_to(xt[:, None, :], (T, E, d)).reshape(-1, d)
        buf = jnp.zeros((E * capacity + 1, d), xt.dtype).at[flat_idx.reshape(-1)].set(src)
        disp = buf[:-1].reshape(E, capacity, d)
        h = jax.nn.silu(jnp.einsum('ecd,edh->ech', disp, W1)) * jnp.einsum('ecd,edh->ech', disp, W2)
        out = jnp.einsum('ech,ehd->ecd', h, W3)
        out_flat = jnp.concatenate([out.reshape(E * capacity, d), jnp.zeros((1, d), xt.dtype)], axis=0)
        all_expert_output = out_flat[flat_idx]
        sel = jnp.take_along_axis(all_expert_output, top_i[:, :, None], axis=1)
        routing_w = jax.nn.softmax(top_v, axis=-1)
        y = (routing_w[:, :, None] * sel).sum(axis=1)
        return y.reshape(b, s, d)

    def _L3_xattn_ref(x, context, Wq, Wk, Wv, Wo, bo):
        import jax, jax.numpy as jnp
        import numpy as np
        HEADS = 8
        DIM_HEAD = 64
        SCALE = DIM_HEAD ** (-0.5)
        B, Nq, _ = x.shape
        q = (x @ Wq).reshape(B, Nq, HEADS, DIM_HEAD)
        k = (context @ Wk).reshape(B, context.shape[1], HEADS, DIM_HEAD)
        v = (context @ Wv).reshape(B, context.shape[1], HEADS, DIM_HEAD)
        sim = jnp.einsum('bihd,bjhd->bhij', q, k) * SCALE
        attn = jax.nn.softmax(sim, axis=-1)
        out = jnp.einsum('bhij,bjhd->bihd', attn, v)
        out = out.reshape(B, Nq, HEADS * DIM_HEAD)
        return out @ Wo + bo

    def _L3_attn_ref(x, in_proj_w, conv_w, conv_b, x_proj_w, dt_proj_w, dt_proj_b, out_proj_w, A_log, D_param):
        import jax, jax.numpy as jnp
        import numpy as np
        D_MODEL = 256
        D_STATE = 16
        D_CONV = 3
        D_INNER = 2 * D_MODEL
        B, S = (4, 512)

        def _mamba_forward(x, in_proj_w, conv_w, conv_b, x_proj_w, dt_proj_w, dt_proj_b, out_proj_w, A_log, D_param):
            combined = x @ in_proj_w
            u, x_gate = jnp.split(combined, 2, axis=-1)
            u_c = jax.lax.conv_general_dilated(u.transpose(0, 2, 1), conv_w, window_strides=(1,), padding='SAME', feature_group_count=D_INNER, dimension_numbers=('NCW', 'OIW', 'NCW'))
            u = jax.nn.silu((u_c + conv_b[None, :, None]).transpose(0, 2, 1))
            x_dbl = u @ x_proj_w
            delta, b, c = jnp.split(x_dbl, [D_INNER, D_INNER + D_STATE], axis=-1)
            delta = jax.nn.softplus(delta @ dt_proj_w + dt_proj_b)
            a = -jnp.exp(A_log)

            def step(h, inp):
                u_t, d_t, b_t, c_t = inp
                h = jnp.exp(d_t[:, :, None] * a) * h + d_t[:, :, None] * b_t[:, None, :] * u_t[:, :, None]
                y_t = jnp.einsum('bds,bs->bd', h, c_t)
                return (h, y_t)
            h0 = jnp.zeros((x.shape[0], D_INNER, D_STATE), x.dtype)
            xs = (u.transpose(1, 0, 2), delta.transpose(1, 0, 2), b.transpose(1, 0, 2), c.transpose(1, 0, 2))
            _, ys = jax.lax.scan(step, h0, xs)
            y = ys.transpose(1, 0, 2)
            y = y + u * D_param
            y = y * jax.nn.silu(x_gate)
            return y @ out_proj_w
        return _mamba_forward(x, in_proj_w, conv_w, conv_b, x_proj_w, dt_proj_w, dt_proj_b, out_proj_w, A_log, D_param)

    def _L3_ffn_ref(x, k0, k1, k2, s0, s1, s2):
        import jax, jax.numpy as jnp
        import numpy as np
        import math
        D_IN = 256
        FEATURES = (1024, 1024, 256)
        BATCH, SEQ = (8, 512)

        def _conn_dense(kernel_bool, x):
            w = jnp.where(kernel_bool, jnp.float32(1.0), jnp.float32(-1.0))
            return x @ w
        h = jnp.concatenate([x, -x], axis=-1)
        h = s0 * _conn_dense(k0, h)
        h = jax.nn.relu(h) * 2
        h = s1 * _conn_dense(k1, h)
        h = jax.nn.relu(h) * 2
        h = s2 * _conn_dense(k2, h)
        return h
    x = x + _L0_xattn_ref(_layernorm(x, axis=-1), ctx_768, ctx_768, L0_xattn_Wq, L0_xattn_bq, L0_xattn_Wk, L0_xattn_bk, L0_xattn_Wv, L0_xattn_bv)
    x = x + _L0_attn_ref(_layernorm(x, axis=-1), L0_attn_w_qkv, L0_attn_ln_w, L0_attn_w_proj)
    x = x + _L0_ffn_ref(_layernorm(x, axis=-1), L0_ffn_gate_w, L0_ffn_w1, L0_ffn_w2, L0_ffn_w3, L0_ffn_sw1, L0_ffn_sw2, L0_ffn_sw3)
    x = x + _L1_xattn_ref(_layernorm(x, axis=-1), ctx_768, L1_xattn_Wq, L1_xattn_bq, L1_xattn_Wkv, L1_xattn_bkv, L1_xattn_Wo, L1_xattn_bo)
    x = x + _L1_attn_ref(_layernorm(x, axis=-1), L1_attn_attention_mask, L1_attn_ln_attn_g, L1_attn_ln_attn_b, L1_attn_Wq, L1_attn_bq, L1_attn_Wk, L1_attn_bk, L1_attn_Wv, L1_attn_bv, L1_attn_ln_conv_g, L1_attn_ln_conv_b, L1_attn_conv_w, L1_attn_conv_b, L1_attn_ln_boom_g, L1_attn_ln_boom_b, L1_attn_Wb, L1_attn_bb, L1_attn_Wu, L1_attn_bu)
    x = x + _L1_ffn_ref(_layernorm(x, axis=-1), L1_ffn_router_W, L1_ffn_router_b, L1_ffn_W1, L1_ffn_b1, L1_ffn_W2, L1_ffn_b2)
    x = x + _L2_xattn_ref(_layernorm(x, axis=-1), ctx_768, L2_xattn_Wq, L2_xattn_Wk, L2_xattn_Wv, L2_xattn_Wo, L2_xattn_bo)
    x = x + _L2_attn_ref(_layernorm(x, axis=-1), L2_attn_theta_log, L2_attn_nu_log, L2_attn_gamma_log, L2_attn_B_re, L2_attn_B_im, L2_attn_C_re, L2_attn_C_im, L2_attn_D)
    x = x + _L2_ffn_ref(_layernorm(x, axis=-1), L2_ffn_Wg, L2_ffn_bg, L2_ffn_W1, L2_ffn_W2, L2_ffn_W3)
    x = x + _L3_xattn_ref(_layernorm(x, axis=-1), ctx_768, L3_xattn_Wq, L3_xattn_Wk, L3_xattn_Wv, L3_xattn_Wo, L3_xattn_bo)
    x = x + _L3_attn_ref(_layernorm(x, axis=-1), L3_attn_in_proj_w, L3_attn_conv_w, L3_attn_conv_b, L3_attn_x_proj_w, L3_attn_dt_proj_w, L3_attn_dt_proj_b, L3_attn_out_proj_w, L3_attn_A_log, L3_attn_D_param)
    x = x + _L3_ffn_ref(_layernorm(x, axis=-1), L3_ffn_k0, L3_ffn_k1, L3_ffn_k2, L3_ffn_s0, L3_ffn_s1, L3_ffn_s2)
    return x

_drawn_inputs = setup_inputs


def setup_inputs(seed=0):
    import zlib

    import numpy as np

    out = dict(_drawn_inputs(seed))
    spreads = {'L0_attn_ln_w': (1.0, 0.2),
     'L1_attn_ln_attn_g': (1.0, 0.6),
     'L1_attn_ln_attn_b': (0.0, 0.8),
     'L1_attn_bq': (0.0, 0.8),
     'L1_attn_bk': (0.0, 0.8),
     'L1_attn_bv': (0.0, 0.8),
     'L1_attn_ln_conv_g': (1.0, 0.6),
     'L1_attn_ln_conv_b': (0.0, 0.637),
     'L1_attn_conv_b': (0.0, 0.1),
     'L1_attn_ln_boom_g': (1.0, 0.6),
     'L1_attn_ln_boom_b': (0.0, 0.8),
     'L1_attn_bb': (0.0, 0.588),
     'L1_attn_bu': (0.0, 0.347),
     'L1_ffn_router_b': (0.0, 0.8),
     'L1_ffn_b1': (0.0, 2.0),
     'L1_ffn_b2': (0.0, 0.8),
     'L2_ffn_bg': (0.0, 0.8),
     'L3_attn_D_param': (1.0, 0.6)}
    factors = {'L0_xattn_bq': 8.0,
     'L0_xattn_bk': 200.0,
     'L1_xattn_bq': 8.0,
     'L1_xattn_bkv': 8.0,
     'L1_xattn_bo': 8.0,
     'L1_attn_Wq': 7.917,
     'L1_attn_Wk': 7.802,
     'L1_attn_Wv': 7.43,
     'L1_ffn_router_W': 8.0,
     'L1_ffn_W1': 64.0,
     'L1_ffn_W2': 8.0,
     'L2_xattn_bo': 42.813,
     'L2_ffn_Wg': 8.0,
     'L2_ffn_W1': 8.0,
     'L2_ffn_W2': 8.0,
     'L2_ffn_W3': 8.0,
     'L3_xattn_bo': 64.0,
     'L3_attn_in_proj_w': 8.0,
     'L3_attn_conv_w': 8.0,
     'L3_attn_conv_b': 8.0,
     'L3_attn_x_proj_w': 8.0,
     'L3_attn_dt_proj_w': 8.0,
     'L3_attn_dt_proj_b': 8.0,
     'L3_attn_out_proj_w': 8.0,
     'L3_attn_A_log': 8.0,
     'L2_xattn_Wq': 3.404,
     'L3_xattn_Wq': 5.989,
     'L3_xattn_Wk': 6.061}
    for name, (base, spread) in spreads.items():
        noise = np.random.default_rng([zlib.crc32(name.encode()), seed]).standard_normal(out[name].shape)
        drawn = base * np.exp(spread * noise) if base else spread * noise
        out[name] = jnp.asarray(drawn.astype(out[name].dtype))
    for name, factor in factors.items():
        out[name] = (out[name] * factor).astype(out[name].dtype)
    return out
```

```python
import concourse.bass as bass
from concourse import mybir
from contextlib import ExitStack

F32 = mybir.dt.float32
BF16 = mybir.dt.bfloat16
U8 = mybir.dt.uint8
I32 = mybir.dt.int32
ALU = mybir.AluOpType
ACT = mybir.ActivationFunctionType
AX = mybir.AxisListType

P = 128
B, S, D = 16, 64, 256
T = B * S
NT = T // P
DC = D // P
SK, CC = 1024, 192
C1 = CC - P
KT = SK // P
HALF = 512


class Chip:

    SEMS = 24

    def __init__(self, nc):
        self.nc = nc
        self.sets = [[nc.alloc_semaphore(f"stage_{s}_{n}") for n in range(self.SEMS)] for s in range(2)]
        self.stages = self.names = 0
        self.folded = nc.alloc_semaphore("residual_folded")


class Stage:

    def __init__(self, chip):
        self.chip, self.nc = chip, chip.nc
        self.mine = list(chip.sets[chip.stages % 2])
        self.other = chip.sets[(chip.stages + 1) % 2]
        self.first = chip.stages == 0
        chip.stages += 1
        self.stack = ExitStack()

    def __enter__(self):
        self.stack.__enter__()
        return self

    def __exit__(self, *e):
        return self.stack.__exit__(*e)

    def sbuf(self, *shape, dtype=F32):
        self.chip.names = n = self.chip.names + 1
        return self.stack.enter_context(self.nc.sbuf_tensor(f"buf{n}", list(shape), dtype))

    def psum(self, *shape):
        self.chip.names = n = self.chip.names + 1
        return self.stack.enter_context(self.nc.psum_tensor(f"acc{n}", list(shape), F32))

    def sems(self, n):
        return [self.mine.pop() for _ in range(n)]

    def sem(self):
        return self.mine.pop()

    def block(self):
        return self.stack.enter_context(self.nc.Block(no_gpsimd_drain=True))

    def clear_other_set(self, sync):
        if not self.first:
            nums = [s.num for s in self.other]
            assert max(nums) - min(nums) == len(nums) - 1
            sync.sem_clear(range(min(nums), max(nums) + 1))


class Chain:

    def __init__(self, eng, sem, base=0):
        self.eng, self.sem, self.base, self.n = eng, sem, base, 0

    def link(self, ins):
        self.n += 1
        ins.then_inc(self.sem, 1)
        self.eng.wait_ge(self.sem, self.base + self.n)


def rows(w):
    return w


def layer_norm(chip, src, dstT, ident, eps=1e-5, keep=None, gain=None):
    nc = chip.nc
    with Stage(chip) as st:
        stats = st.sbuf(P, NT, 6)
        mv = st.sbuf(P, NT, 2)
        std = st.sbuf(P, NT)
        rstd = st.sbuf(P, NT)
        xn = keep if keep is not None else st.sbuf(P, NT, D)
        turned = [[st.psum(P, HALF) for h in range(2)] for c in range(DC)]
        steps, var_ready, std_ready, xn_ready, turned_ready, gain_in = st.sems(6)
        if gain is not None:
            gb = st.sbuf(P, 2, DC)
        block = st.block()

        def dst(c, h):
            return dstT(c, h) if callable(dstT) else dstT[:, c, h * HALF:(h + 1) * HALF]

        @block.sync
        def _(sync):
            st.clear_other_set(sync)
            if gain is not None:
                for n in range(2):
                    sync.dma_start(gb[:, n, :], gain[n]).then_inc(gain_in, 16)

        @block.vector
        def _(dve):
            c = Chain(dve, steps)
            for j in range(NT):
                ins = dve.bn_stats(stats[:, j, :], src[:, j, :])
                if j == NT - 1:
                    c.link(ins)
            for j in range(NT):
                ins = dve.bn_aggr(mv[:, j, :], stats[:, j, :])
                if j == NT - 1:
                    c.link(ins)
            dve.tensor_scalar(rstd[:, :], mv[:, :, 1], eps, None, ALU.add).then_inc(var_ready, 1)
            dve.wait_ge(std_ready, 1)
            c.link(dve.reciprocal(rstd[:, :], std[:, :]))
            for j in range(NT):
                dve.tensor_scalar(xn[:, j, :], src[:, j, :], mv[:, j, 0:1], rstd[:, j:j + 1],
                                  ALU.subtract, ALU.mult).then_inc(xn_ready, 1)
            if gain is not None:
                dve.wait_ge(gain_in, 32)
            for h in range(2):
                dve.wait_ge(turned_ready, 4 * h + 4)
                if gain is None:
                    dve.tensor_copy(dst(1, h), turned[1][h][:, :])
                else:
                    dve.tensor_scalar(dst(1, h), turned[1][h][:, :] if not callable(dstT) else
                                      turned[1][h][:, :].rearrange("p (b s) -> p b s", s=S),
                                      gb[:, 0, 1:2], gb[:, 1, 1:2], ALU.mult, ALU.add)

        @block.scalar
        def _(act):
            act.wait_ge(var_ready, 1)
            act.activation(std[:, :], rstd[:, :], ACT.Sqrt).then_inc(std_ready, 1)
            if gain is not None:
                act.wait_ge(gain_in, 32)
            for h in range(2):
                act.wait_ge(turned_ready, 4 * h + 4)
                if gain is None:
                    act.copy(dst(0, h), turned[0][h][:, :])
                else:
                    act.activation(dst(0, h), turned[0][h][:, :] if not callable(dstT) else
                                   turned[0][h][:, :].rearrange("p (b s) -> p b s", s=S),
                                   ACT.Identity, bias=gb[:, 1, 0:1], scale=gb[:, 0, 0:1])

        @block.tensor
        def _(pe):
            for j in range(NT):
                pe.wait_ge(xn_ready, j + 1)
                for c in range(DC):
                    ins = pe.transpose(turned[c][j // 4][:, (j % 4) * P:(j % 4 + 1) * P],
                                       xn[:, j, c * P:(c + 1) * P], ident[:, :])
                ins.then_inc(turned_ready, 1)


def matmul_jobs(chip, jobs, loads, setup=None, nbanks=6):
    nc = chip.nc
    with Stage(chip) as st:
        banks = [st.psum(P, HALF) for _ in range(nbanks)]
        loaded, prepared, filled, act_done, dve_done, steps = st.sems(6)
        done = {"act": act_done, "dve": dve_done}
        turn, counts = [], {"act": 0, "dve": 0}
        for _, _, on, _ in jobs:
            counts[on] += 1
            turn.append(counts[on])
        block = st.block()

        @block.sync
        def _(sync):
            st.clear_other_set(sync)
            for dst, src in loads[0::2]:
                sync.dma_start(dst, src).then_inc(loaded, 16)

        @block.tensor
        def _(pe):
            if loads:
                pe.wait_ge(loaded, 16 * len(loads))
            if setup is not None:
                pe.wait_ge(prepared, 1)
            for n, (pairs, (r, w), on, write) in enumerate(jobs):
                if n >= nbanks:
                    before = jobs[n - nbanks][2]
                    pe.wait_ge(done[before], turn[n - nbanks])
                for k, (lhsT, rhs) in enumerate(pairs):
                    ins = pe.matmul(banks[n % nbanks][0:r, 0:w], lhsT, rhs, start=(k == 0),
                                    stop=(k == len(pairs) - 1))
                ins.then_inc(filled, 1)

        @block.scalar
        def _(act):
            for dst, src in loads[1::2]:
                act.dma_start(dst, src).then_inc(loaded, 16)
            if loads:
                act.wait_ge(loaded, 16 * len(loads))
            for n, (pairs, (r, w), on, write) in enumerate(jobs):
                if on == "act":
                    act.wait_ge(filled, n + 1)
                    write(act, banks[n % nbanks][0:r, 0:w]).then_inc(act_done, 1)

        @block.vector
        def _(dve):
            if loads:
                dve.wait_ge(loaded, 16 * len(loads))
            if setup is not None:
                chain = Chain(dve, steps)
                setup(dve, chain)
                chain.link(dve.engine_nop())
                dve.sem_inc(prepared, 1)
            for n, (pairs, (r, w), on, write) in enumerate(jobs):
                if on == "dve":
                    dve.wait_ge(filled, n + 1)
                    write(dve, banks[n % nbanks][0:r, 0:w]).then_inc(dve_done, 1)


def copy_out(dst):
    def write(eng, acc):
        return eng.copy(dst, acc) if is_scalar_engine(eng) else eng.tensor_copy(dst, acc)
    return write


def is_scalar_engine(eng):
    return eng.engine == mybir.EngineType.Activation


def halves(h):
    return slice(h * HALF, (h + 1) * HALF)


def lru(chip, X, xn, xnT, ident, w):
    nc = chip.nc
    HID = 128
    with ExitStack() as es:
        def sb(*shape):
            chip.names = n = chip.names + 1
            return es.enter_context(nc.sbuf_tensor(f"lru{n}", list(shape), F32))
        Bre, Bim = sb(P, DC, HID), sb(P, DC, HID)
        Cre, Cim, Drow = sb(P, D), sb(P, D), sb(P, D)
        par = sb(P, 3)
        re = [sb(P, T), sb(P, T)]
        im = [sb(P, T), sb(P, T)]
        g = sb(P, 1)
        lam = sb(P, 6, 3)
        tmp = sb(P, 8)
        big = sb(P, T)
        with Stage(chip) as st:
            loaded, dsteps, ready, back = st.sems(4)
            block = st.block()

            @block.sync
            def _(sync):
                st.clear_other_set(sync)
                for n, name in enumerate(("theta_log", "nu_log", "gamma_log")):
                    sync.dma_start(par[:, n:n + 1], w[name]).then_inc(loaded, 16)

            @block.scalar
            def _(act):
                act.wait_ge(loaded, 48)
                act.activation(tmp[:, 0:1], par[:, 0:1], ACT.Exp)
                act.activation(tmp[:, 1:2], par[:, 1:2], ACT.Exp).then_inc(ready, 1)
                act.wait_ge(ready, 1)
                act.activation(tmp[:, 2:3], tmp[:, 1:2], ACT.Exp, scale=-1.0)
                act.activation(g[:, :], par[:, 2:3], ACT.Exp).then_inc(ready, 1)
                act.wait_ge(back, 1)
                act.activation(tmp[:, 6:7], tmp[:, 4:5], ACT.Sin)
                act.activation(tmp[:, 7:8], tmp[:, 5:6], ACT.Sin).then_inc(ready, 1)

            @block.vector
            def _(dve):
                c = Chain(dve, dsteps)
                dve.wait_ge(ready, 2)
                c.link(dve.tensor_scalar(tmp[:, 3:4], tmp[:, 0:1], 0.15915494309189535, 12582912.0,
                                         ALU.mult, ALU.add))
                c.link(dve.tensor_scalar(tmp[:, 3:4], tmp[:, 3:4], -12582912.0, None, ALU.add))
                for part in (6.28125, 0.0019350051879882812, 3.0199e-07):
                    c.link(dve.scalar_tensor_tensor(out=tmp[:, 0:1], in0=tmp[:, 3:4], scalar=-part,
                                                    in1=tmp[:, 0:1], op0=ALU.mult, op1=ALU.add))
                c.link(dve.tensor_scalar(tmp[:, 4:5], tmp[:, 0:1], 3.1415925, -3.1415925, ALU.min, ALU.max))
                c.link(dve.tensor_scalar(tmp[:, 5:6], tmp[:, 4:5], -1.0, None, ALU.mult))
                c.link(dve.tensor_tensor(tmp[:, 5:6], tmp[:, 5:6], tmp[:, 4:5], ALU.min))
                dve.tensor_scalar(tmp[:, 5:6], tmp[:, 5:6], 1.5707963267948966, None,
                                  ALU.add).then_inc(back, 1)
                dve.wait_ge(ready, 3)
                c.link(dve.tensor_tensor(lam[:, 0, 0:1], tmp[:, 7:8], tmp[:, 2:3], ALU.mult))
                c.link(dve.tensor_tensor(lam[:, 0, 1:2], tmp[:, 6:7], tmp[:, 2:3], ALU.mult))
                for k in range(6):
                    a, b = lam[:, k, 0:1], lam[:, k, 1:2]
                    c.link(dve.tensor_scalar(lam[:, k, 2:3], b, -1.0, None, ALU.mult))
                    if k < 5:
                        a2, b2 = lam[:, k + 1, 0:1], lam[:, k + 1, 1:2]
                        c.link(dve.tensor_tensor(tmp[:, 6:7], b, b, ALU.mult))
                        c.link(dve.scalar_tensor_tensor(out=a2, in0=a, scalar=a, in1=tmp[:, 6:7],
                                                        op0=ALU.mult, op1=ALU.subtract))
                        c.link(dve.tensor_tensor(b2, a, b, ALU.mult))
                        c.link(dve.tensor_scalar(b2, b2, 2.0, None, ALU.mult))
        jobs = []
        for dst, wt in ((re[0], Bre), (im[0], Bim)):
            for h in range(2):
                def write(eng, acc, dst=dst, h=h):
                    return eng.activation(dst[:, halves(h)], acc, ACT.Copy, scale=g[:, 0:1])
                jobs.append(([(wt[:, k, :], xnT[:, k, halves(h)]) for k in range(DC)], (P, HALF), "act", write))
        matmul_jobs(chip, jobs, [(Bre[:], w["B_re"]), (Bim[:], w["B_im"])])
        with Stage(chip) as st:
            dsteps, loaded = st.sems(2)
            block = st.block()

            @block.sync
            def _(sync):
                st.clear_other_set(sync)
                sync.dma_start(Drow[:, :], w["D"].partition_broadcast(P)).then_inc(loaded, 16)
                sync.wait_ge(loaded, 16)

            @block.vector
            def _(dve):
                c = Chain(dve, dsteps)
                for k in range(6):
                    s = 1 << k
                    v = [[t[i][:, :].rearrange("p (b s) -> p b s", s=S) for i in (k % 2, 1 - k % 2)] for t in (re, im)]
                    a, b, nb = (lam[:, k, n:n + 1] for n in range(3))
                    (r0, r1), (i0, i1) = v
                    for (src, dst, other, coef) in ((r0, r1, i0, nb), (i0, i1, r0, b)):
                        dve.tensor_copy(dst[:, :, 0:s], src[:, :, 0:s])
                        c.link(dve.scalar_tensor_tensor(out=dst[:, :, s:S], in0=src[:, :, 0:S - s], scalar=a,
                                                        in1=src[:, :, s:S], op0=ALU.mult, op1=ALU.add))
                        c.link(dve.scalar_tensor_tensor(out=dst[:, :, s:S], in0=other[:, :, 0:S - s], scalar=coef,
                                                        in1=dst[:, :, s:S], op0=ALU.mult, op1=ALU.add))
                c.link(dve.tensor_scalar(im[1][:, :], im[0][:, :], -1.0, None, ALU.mult))
                for j in range(NT):
                    if j == 0:
                        dve.wait_ge(loaded, 16)
                    c.link(dve.tensor_tensor(big[:, 0:D], xn[:, j, :], Drow[:, :], ALU.mult))
                    c.link(dve.tensor_tensor(X[:, j, :], X[:, j, :], big[:, 0:D], ALU.add))
        jobs = []
        for j in range(NT):
            def write(eng, acc, j=j):
                return eng.tensor_tensor(X[:, j, :], X[:, j, :], acc, ALU.add)
            t = slice(j * P, (j + 1) * P)
            jobs.append(([(re[0][:, t], Cre[:, :]), (im[1][:, t], Cim[:, :])], (P, D), "dve", write))
        matmul_jobs(chip, jobs, [(Cre[:, :], w["C_re"]), (Cim[:, :], w["C_im"])])


def fill(chip, sets, loads):
    with Stage(chip) as st:
        cleared, loaded = st.sems(2)
        block = st.block()

        @block.vector
        def _(dve):
            for dst, value in sets:
                dve.memset(dst, value).then_inc(cleared, 1)
            dve.wait_ge(cleared, len(sets))

        @block.sync
        def _(sync):
            st.clear_other_set(sync)
            sync.wait_ge(cleared, len(sets))
            for dst, src in loads:
                sync.dma_start(dst, src).then_inc(loaded, 16)
            if loads:
                sync.wait_ge(loaded, 16 * len(loads))


def turn_to_tokens(chip, srcT, ident, write):
    with Stage(chip) as st:
        banks = [st.psum(P, HALF) for _ in range(4)]
        turned, written = st.sems(2)
        block = st.block()

        @block.sync
        def _(sync):
            st.clear_other_set(sync)

        @block.tensor
        def _(pe):
            for j in range(NT):
                if j >= 4:
                    pe.wait_ge(written, j - 3)
                for c in range(DC):
                    ins = pe.transpose(banks[j % 4][:, c * P:(c + 1) * P],
                                       srcT[:, c, j * P:(j + 1) * P], ident[:, :])
                ins.then_inc(turned, 1)

        @block.vector
        def _(dve):
            for j in range(NT):
                dve.wait_ge(turned, j + 1)
                write(dve, j, banks[j % 4][:, 0:D]).then_inc(written, 1)


def buffers(chip, es):
    def sb(*shape, dtype=F32):
        chip.names = n = chip.names + 1
        return es.enter_context(chip.nc.sbuf_tensor(f"buf{n}", list(shape), dtype))
    return sb


def tile(j):
    return slice(j * P, (j + 1) * P)


def binary_mlp(chip, X, xn, xnT, ident, w):
    F = 1024
    FC = F // P
    with ExitStack() as es:
        sb = buffers(chip, es)
        W0, W1, W2 = sb(P, DC, F), sb(P, FC, F), sb(P, FC, D)
        h1, h2 = sb(P, FC, T), sb(P, FC, T)
        sc = sb(P, 3)
        with ExitStack() as inner:
            ib = buffers(chip, inner)
            words = ib(P, 4, F // 4, dtype=I32), ib(P, FC, F // 4, dtype=I32), ib(P, FC, D // 4, dtype=I32)
            k0, k1, k2 = (b[:, :, :].bitcast(U8) for b in words)
            with Stage(chip) as st:
                loaded, steps, k2_done = st.sems(3)
                block = st.block()

                @block.sync
                def _(sync):
                    st.clear_other_set(sync)
                    for n in range(3):
                        sync.dma_start(words[n][:, :, :], w[f"k{n}"]).then_inc(loaded, 16)
                    for n in range(3):
                        sync.dma_start(sc[:, n:n + 1], w[f"s{n}"].partition_broadcast(P)).then_inc(loaded, 16)

                @block.scalar
                def _(act):
                    act.wait_ge(loaded, 96)
                    act.activation(W2[:, :, :], k2[:, :, :], ACT.Copy, scale=2.0, bias=-1.0)
                    act.activation(W1[:, 0:4, :], k1[:, 0:4, :], ACT.Copy, scale=2.0, bias=-1.0)

                @block.vector
                def _(dve):
                    dve.wait_ge(loaded, 96)
                    c = Chain(dve, steps)
                    c.link(dve.tensor_tensor(W0[:, :, :], k0[:, 0:2, :], k0[:, 2:4, :], ALU.subtract))
                    dve.tensor_scalar(W0[:, :, :], W0[:, :, :], 2.0, None, ALU.mult)
                    dve.tensor_scalar(W1[:, 4:8, :], k1[:, 4:8, :], 2.0, -1.0, ALU.mult, ALU.add)
                    c.link(dve.tensor_scalar(sc[:, 0:2], sc[:, 0:2], 2.0, None, ALU.mult))

        def relu_to(dst, n):
            def write(eng, acc):
                if is_scalar_engine(eng):
                    return eng.activation(dst, acc, ACT.Relu, scale=sc[:, n:n + 1])
                return eng.tensor_scalar(dst, acc, sc[:, n:n + 1], 0.0, ALU.mult, ALU.max)
            return write

        jobs = []
        for n, (wt, src, kc, dst) in enumerate(((W0, xnT, DC, h1), (W1, h1, FC, h2))):
            for h in range(2):
                for m in range(FC):
                    jobs.append(([(wt[:, k, tile(m)], src[:, k, halves(h)]) for k in range(kc)], (P, HALF),
                                 ("act", "dve")[m % 2], relu_to(dst[:, m, halves(h)], n)))
            matmul_jobs(chip, jobs, [])
            jobs = []
        for j in range(NT):
            def write(eng, acc, j=j):
                return eng.scalar_tensor_tensor(out=X[:, j, :], in0=acc, scalar=sc[:, 2:3], in1=X[:, j, :],
                                                op0=ALU.mult, op1=ALU.add)
            jobs.append(([(h2[:, k, tile(j)], W2[:, k, :]) for k in range(FC)], (P, D), "dve", write))
        matmul_jobs(chip, jobs, [])


def conv_pool_mlp(chip, X, xn, xnT, ident, w):
    K, F = 4, 1024
    FC = F // P
    PAD = K - 1
    with ExitStack() as es:
        sb = buffers(chip, es)
        H = sb(P, NT, D)
        aT = sb(P, DC, T)
        ones = sb(1, P)
        with ExitStack() as inner:
            ib = buffers(chip, inner)
            hp = ib(P, DC, B, S + PAD)
            cw, cb = ib(P, DC, K, P), ib(P, DC)
            fill(chip, [(cw[:, :, :, :], 0.0), (hp[:, :, :, 0:PAD], 0.0), (ones[:, :], 1.0)],
                 [(cw[(g % 2) * 64:(g % 2) * 64 + 64, g // 2, :, (g % 2) * 64:(g % 2) * 64 + 64], w["conv_w"][g])
                  for g in range(4)] + [(cb[:, :], w["conv_b"])])
            layer_norm(chip, xn, lambda c, h: hp[:, c, h * 8:h * 8 + 8, PAD:], ident,
                       gain=(w["ln_conv_g"], w["ln_conv_b"]))
            convT = ib(P, DC, T)
            jobs = []
            for c in range(DC):
                for h in range(2):
                    def write(eng, acc, c=c, h=h):
                        return eng.activation(convT[:, c, halves(h)], acc, ACT.Identity, bias=cb[:, c:c + 1])
                    jobs.append(([(cw[:, c, k, :], hp[:, c, 8 * h:8 * h + 8, k:k + S]) for k in range(K)],
                                 (P, HALF), "act", write))
            matmul_jobs(chip, jobs, [])
            turn_to_tokens(chip, convT, ident,
                           lambda dve, j, acc: dve.tensor_tensor(H[:, j, :], xn[:, j, :], acc, ALU.add))
        layer_norm(chip, H, aT, ident, gain=(w["ln_attn_g"], w["ln_attn_b"]))
        with ExitStack() as inner:
            ib = buffers(chip, inner)
            q, k, v = (ib(P, DC, T) for _ in range(3))
            W = ib(P, 3, DC, D)
            bqkv = ib(P, 3, DC)
            inv, keep = ib(P, S), ib(P, T)
            jobs = []
            for n, dst in enumerate((q, k, v)):
                for m in range(DC):
                    for h in range(2):
                        def write(eng, acc, dst=dst, n=n, m=m, h=h):
                            b = bqkv[:, n, m:m + 1]
                            if is_scalar_engine(eng):
                                return eng.activation(dst[:, m, halves(h)], acc, ACT.Identity, bias=b)
                            return eng.tensor_scalar(dst[:, m, halves(h)], acc, b, None, ALU.add)
                        jobs.append(([(W[:, n, c, tile(m)], aT[:, c, halves(h)]) for c in range(DC)], (P, HALF),
                                     ("act", "dve")[h], write))
            loads = [(W[:, n, :, :], w["W" + x]) for n, x in enumerate("qkv")]
            loads += [(bqkv[:, n, :], w["b" + x]) for n, x in enumerate("qkv")]
            loads += [(inv[:, :], w["inv_len"].partition_broadcast(P))]
            matmul_jobs(chip, jobs, loads)
            with Stage(chip) as st:
                steps = st.sem()
                block = st.block()

                @block.sync
                def _(sync):
                    st.clear_other_set(sync)

                @block.vector
                def _(dve):
                    c = Chain(dve, steps)
                    c.link(dve.memset(keep[:, :], 1.0))
                    c.link(dve.memset(keep[:, :].rearrange("p (b s) -> p b s", s=S)[:, :, 0:1], 0.0))

                    def by_length(t, m):
                        v3 = t[:, m, :].rearrange("p (b s) -> p b s", s=S)
                        c.link(dve.tensor_tensor(v3, v3, inv[:, :].unsqueeze(1).broadcast_to([P, B, S]), ALU.mult))

                    for m in range(DC):
                        c.link(dve.tensor_tensor_scan(q[:, m, :], keep[:, :], q[:, m, :], 0.0, ALU.mult, ALU.add))
                        by_length(q, m)
                        c.link(dve.tensor_tensor(k[:, m, :], q[:, m, :], k[:, m, :], ALU.mult))
                        c.link(dve.tensor_tensor_scan(q[:, m, :], keep[:, :], k[:, m, :], 0.0, ALU.mult, ALU.add))
                        by_length(q, m)
                        c.link(dve.tensor_tensor(v[:, m, :], q[:, m, :], v[:, m, :], ALU.mult))
            turn_to_tokens(chip, v, ident,
                           lambda dve, j, acc: dve.tensor_tensor(H[:, j, :], H[:, j, :], acc, ALU.add))
        layer_norm(chip, H, aT, ident, gain=(w["ln_boom_g"], w["ln_boom_b"]))
        Wb, Wu, g = sb(P, DC, F), sb(P, FC, D), sb(P, FC, T)
        bb, bu = sb(P, FC), sb(1, D)
        jobs = []
        for h in range(2):
            for m in range(FC):
                def write(eng, acc, m=m, h=h):
                    return eng.activation(g[:, m, halves(h)], acc, ACT.Gelu, bias=bb[:, m:m + 1])
                jobs.append(([(Wb[:, c, tile(m)], aT[:, c, halves(h)]) for c in range(DC)], (P, HALF), "act", write))
        matmul_jobs(chip, jobs, [(Wb[:, :, :], w["Wb"]), (Wu[:, :, :], w["Wu"]), (bb[:, :], w["bb"]), (bu[:, :], w["bu"])])
        jobs = []
        for j in range(NT):
            def write(eng, acc, j=j):
                eng.tensor_tensor(X[:, j, :], X[:, j, :], H[:, j, :], ALU.add).then_inc(chip.folded, 1)
                eng.wait_ge(chip.folded, j + 1)
                return eng.tensor_tensor(X[:, j, :], X[:, j, :], acc, ALU.add)
            jobs.append(([(g[:, k, tile(j)], Wu[:, k, :]) for k in range(FC)] + [(ones[:, :], bu[:, :])],
                         (P, D), "dve", write))
        matmul_jobs(chip, jobs, [])


E = 8


def peeled(eng, n, first=1, last=0):
    yield from range(first)
    if n - last > first:
        with eng.Fori(first, n - last) as i:
            yield i
    yield from range(n - last, n)


def later(step, least):
    return step >= least if isinstance(step, int) else True


def route(chip, xnT, gate, gate_bias, K, share, w, choice, chosen, loads):
    nc = chip.nc
    with ExitStack() as es:
        sb = buffers(chip, es)
        logits, ex = sb(P, NT, E), sb(P, NT, E)
        above, equal = sb(P, NT, E, E), sb(P, NT, E, E)
        lower, small = sb(P, E * E), sb(P, NT)
        ones = sb(1, P)
        if gate_bias is not None:
            fill(chip, [(ones[:, :], 1.0)], [])
        jobs = []
        for j in range(NT):
            def write(eng, acc, j=j):
                return eng.tensor_copy(logits[:, j, :], acc)
            pairs = [(xnT[:, k, tile(j)], gate[:, k, :]) for k in range(DC)]
            if gate_bias is not None:
                pairs.append((ones[:, :], gate_bias[:, :]))
            jobs.append((pairs, (P, E), "dve", write))
        matmul_jobs(chip, jobs, loads + [(lower[:, :], w["lower"].partition_broadcast(P))])
        with Stage(chip) as st:
            steps, shifted, exp_done = st.sems(3)
            block = st.block()

            @block.sync
            def _(sync):
                st.clear_other_set(sync)

            @block.scalar
            def _(act):
                act.wait_ge(shifted, 1)
                act.activation(ex[:, :, :], ex[:, :, :], ACT.Exp).then_inc(exp_done, 1)

            @block.vector
            def _(dve):
                c = Chain(dve, steps)
                L = logits[:, :, :]
                full = [P, NT, E, E]
                c.link(dve.tensor_reduce(small[:, :], L, AX.X, ALU.max))
                dve.tensor_tensor(ex[:, :, :], L, small[:, :].unsqueeze(2).broadcast_to([P, NT, E]),
                                  ALU.subtract).then_inc(shifted, 1)
                other = L.unsqueeze(2).broadcast_to(full)
                own = L.unsqueeze(3).broadcast_to(full)
                flat = "p j a b -> p j (a b)"
                c.link(dve.tensor_tensor(above[:, :, :, :], other, own, ALU.is_gt))
                c.link(dve.tensor_tensor(equal[:, :, :, :], other, own, ALU.is_equal))
                c.link(dve.tensor_tensor(equal[:, :, :, :].rearrange(flat), equal[:, :, :, :].rearrange(flat),
                                         lower[:, :].unsqueeze(1).broadcast_to([P, NT, E * E]), ALU.mult))
                c.link(dve.tensor_tensor(above[:, :, :, :].rearrange(flat), above[:, :, :, :].rearrange(flat),
                                         equal[:, :, :, :].rearrange(flat), ALU.add))
                c.link(dve.tensor_reduce(chosen[:, :, :], above[:, :, :, :], AX.X, ALU.add))
                c.link(dve.tensor_scalar(chosen[:, :, :], chosen[:, :, :], K - 0.5, None, ALU.is_lt))
                dve.wait_ge(exp_done, 1)
                c.link(dve.tensor_tensor(choice[:, :, :], ex[:, :, :], chosen[:, :, :], ALU.mult))
                c.link(dve.tensor_reduce(small[:, :], (ex if share == "all" else choice)[:, :, :], AX.X, ALU.add))
                c.link(dve.reciprocal(small[:, :], small[:, :]))
                c.link(dve.tensor_tensor(choice[:, :, :], choice[:, :, :],
                                         small[:, :].unsqueeze(2).broadcast_to([P, NT, E]), ALU.mult))


def dense_experts(chip, X, xnT, choice, experts, width, gated, loads_of, bias=None):
    M = -(-width // P)
    last = width - (M - 1) * P
    UP = 2 if gated else 1
    with Stage(chip) as st:
        Wup = [[st.sbuf(P, DC, width) for _ in range(UP)] for _ in range(2)]
        Wdn = [st.sbuf(P, M, D) for _ in range(2)]
        hid = st.sbuf(P, M, T)
        scale = [st.sbuf(P, NT) for _ in range(2)]
        sil = [st.sbuf(P, HALF) for _ in range(2)]
        if bias is not None:
            b_up = [st.sbuf(P, M) for _ in range(2)]
            b_dn = [st.sbuf(1, D) for _ in range(2)]
            ones = st.sbuf(1, P)
        up = [[st.psum(P, HALF) for _ in range(UP)] for _ in range(2)]
        down = [st.psum(P, HALF) for _ in range(4)]
        weights_in = st.sems(2)
        up_filled, silu_done, hid_ready, down_filled, scale_ready, added, ones_ready = st.sems(7)
        block = st.block()
        NU = 2 * M
        rounds = experts // 2

        def size(m):
            return last if m == M - 1 else P

        n_loads = UP + (1 if last == P else 2) + (2 if bias is not None else 0)

        @block.sync
        def _(sync):
            st.clear_other_set(sync)
            for i in peeled(sync, rounds):
                for x in range(2):
                    e = i * 2 + x
                    if later(i, 1):
                        sync.wait_ge(added, (e - 1) * NT)
                    n = 0
                    for dst, src in loads_of(x, e, Wup, Wdn, b_up if bias is not None else None,
                                             b_dn if bias is not None else None):
                        sync.dma_start(dst, src).then_inc(weights_in[x], 16)
                        n += 1
                    assert n == n_loads

        @block.tensor
        def _(pe):
            if bias is not None:
                pe.wait_ge(ones_ready, 1)
            for i in peeled(pe, rounds):
                for x in range(2):
                    e = i * 2 + x
                    pe.wait_ge(weights_in[x], i * (16 * n_loads) + 16 * n_loads)
                    for h in range(2):
                        for m in range(M):
                            n = e * NU + h * M + m
                            if later(n, 2):
                                pe.wait_ge(hid_ready, n - 1)
                            for u in range(UP):
                                for k in range(DC):
                                    ins = pe.matmul(up[(h * M + m) % 2][u][0:size(m), :],
                                                    Wup[x][u][:, k, m * P:m * P + size(m)], xnT[:, k, halves(h)],
                                                    start=(k == 0), stop=(k == DC - 1))
                            ins.then_inc(up_filled, 1)
                    for j in range(NT):
                        pe.wait_ge(hid_ready, e * NU + (j // 4 + 1) * M)
                        if later(e * NT + j, 4):
                            pe.wait_ge(added, e * NT + j - 3)
                        for k in range(M):
                            ins = pe.matmul(down[j % 4][:, 0:D], hid[0:size(k), k, tile(j)], Wdn[x][0:size(k), k, :],
                                            start=(k == 0), stop=(k == M - 1 and bias is None))
                        if bias is not None:
                            ins = pe.matmul(down[j % 4][:, 0:D], ones[:, :], b_dn[x][:, :], start=False, stop=True)
                        ins.then_inc(down_filled, 1)

        @block.scalar
        def _(act):
            for i in peeled(act, rounds):
                for x in range(2):
                    e = i * 2 + x
                    if bias is not None:
                        act.wait_ge(weights_in[x], i * (16 * n_loads) + 16 * n_loads)
                    for h in range(2):
                        for m in range(M):
                            n = e * NU + h * M + m
                            acc = up[(h * M + m) % 2][0][0:size(m), :]
                            act.wait_ge(up_filled, n + 1)
                            if gated:
                                if later(n, 2):
                                    act.wait_ge(hid_ready, n - 1)
                                act.activation(sil[(h * M + m) % 2][0:size(m), :], acc, ACT.Silu).then_inc(silu_done, 1)
                            else:
                                if m == 0 and later(e, 1):
                                    act.wait_ge(down_filled, e * NT - NT + 4 * h + 4)
                                act.activation(hid[0:size(m), m, halves(h)], acc, ACT.Relu,
                                               bias=b_up[x][:, m:m + 1]).then_inc(hid_ready, 1)

        @block.vector
        def _(dve):
            if bias is not None:
                dve.memset(ones[:, :], 1.0).then_inc(ones_ready, 1)
            for i in peeled(dve, rounds):
                for x in range(2):
                    e = i * 2 + x
                    dve.tensor_copy(scale[x][:, :], choice[:, :, bass.ds(e, 1)].rearrange("p j o -> p (j o)")
                                    ).then_inc(scale_ready, 1)
                    if gated:
                        for h in range(2):
                            for m in range(M):
                                n = e * NU + h * M + m
                                if m == 0 and later(e, 1):
                                    dve.wait_ge(down_filled, e * NT - NT + 4 * h + 4)
                                dve.wait_ge(silu_done, n + 1)
                                s = (h * M + m) % 2
                                dve.tensor_tensor(hid[0:size(m), m, halves(h)], sil[s][0:size(m), :],
                                                  up[s][1][0:size(m), :], ALU.mult).then_inc(hid_ready, 1)
                    dve.wait_ge(scale_ready, e + 1)
                    if later(e, 1):
                        dve.wait_ge(added, e * NT)
                    for j in range(NT):
                        dve.wait_ge(down_filled, e * NT + j + 1)
                        dve.scalar_tensor_tensor(out=X[:, j, :], in0=down[j % 4][:, 0:D], scalar=scale[x][:, j:j + 1],
                                                 in1=X[:, j, :], op0=ALU.mult, op1=ALU.add).then_inc(added, 1)


def shared_and_routed(chip, X, xn, xnT, ident, w):
    HID, SH = 704, 384
    with ExitStack() as es:
        sb = buffers(chip, es)
        choice, chosen, gate = sb(P, NT, E), sb(P, NT, E), sb(P, DC, E)
        route(chip, xnT, gate, None, 2, "all", w, choice, chosen, [(gate[:, :, :], w["gate_w"])])
        FULL = HID // P

        def loads_of(x, e, Wup, Wdn, b_up, b_dn):
            one = bass.ds(e, 1)
            yield Wup[x][0][:, :, :], w["w1"][one].rearrange("o p k n -> p (o k) n")
            yield Wup[x][1][:, :, :], w["w3"][one].rearrange("o p k n -> p (o k) n")
            yield Wdn[x][:, 0:FULL, :], w["w2"][one].rearrange("o p k n -> p (o k) n")
            yield Wdn[x][0:HID - FULL * P, FULL, :], w["w2_tail"][one].rearrange("o p n -> (o p) n")
        dense_experts(chip, X, xnT, choice, E, HID, True, loads_of)
        MS = SH // P
        s1, s3, s2 = sb(P, DC, SH), sb(P, DC, SH), sb(P, MS, D)
        a, hid = sb(P, MS, T), sb(P, MS, T)
        jobs = []
        for h in range(2):
            for m in range(MS):
                def silu(eng, acc, m=m, h=h):
                    return eng.activation(a[:, m, halves(h)], acc, ACT.Silu)

                def copy(eng, acc, m=m, h=h):
                    return eng.tensor_copy(hid[:, m, halves(h)], acc)
                for wt, on, write in ((s1, "act", silu), (s3, "dve", copy)):
                    jobs.append(([(wt[:, k, tile(m)], xnT[:, k, halves(h)]) for k in range(DC)], (P, HALF), on, write))
        matmul_jobs(chip, jobs, [(s1[:, :, :], w["sw1"]), (s3[:, :, :], w["sw3"]), (s2[:, :, :], w["sw2"])])

        def gate_hidden(dve, chain):
            for m in range(MS):
                dve.tensor_tensor(hid[:, m, :], hid[:, m, :], a[:, m, :], ALU.mult)
        jobs = []
        for j in range(NT):
            def write(eng, acc, j=j):
                return eng.tensor_tensor(X[:, j, :], X[:, j, :], acc, ALU.add)
            jobs.append(([(hid[:, k, tile(j)], s2[:, k, :]) for k in range(MS)], (P, D), "dve", write))
        matmul_jobs(chip, jobs, [], setup=gate_hidden)


def top1_experts(chip, X, xn, xnT, ident, w):
    with ExitStack() as es:
        sb = buffers(chip, es)
        choice, chosen, gate, gb = sb(P, NT, E), sb(P, NT, E), sb(P, DC, E), sb(1, E)
        route(chip, xnT, gate, gb, 1, "all", w, choice, chosen,
              [(gate[:, :, :], w["router_W"]), (gb[:, :], w["router_b"])])

        def loads_of(x, e, Wup, Wdn, b_up, b_dn):
            one = bass.ds(e, 1)
            yield Wup[x][0][:, :, :], w["W1"][one].rearrange("o p k n -> p (o k) n")
            yield Wdn[x][:, :, :], w["W2"][one].rearrange("o p k n -> p (o k) n")
            yield b_up[x][:, :], w["b1"][one].rearrange("o p m -> p (o m)")
            yield b_dn[x][:, :], w["b2"][one]
        dense_experts(chip, X, xnT, choice, E, 1024, False, loads_of, bias=True)


def capacity_experts(chip, X, xn, xnT, ident, w):
    HID = 1024
    M = HID // P
    CAP = int(T / E * 1.25)
    HC = CAP // 2
    with ExitStack() as es:
        sb = buffers(chip, es)
        choice, chosen, gate, gb = sb(P, NT, E), sb(P, NT, E), sb(P, DC, E), sb(1, E)
        slot, before = sb(P, NT, E), sb(P, NT, E)
        tri, ones, iota = sb(P, P), sb(P, P), sb(P, CAP)
        route(chip, xnT, gate, gb, 2, "chosen", w, choice, chosen,
              [(gate[:, :, :], w["Wg"]), (gb[:, :], w["bg"])])

        def prefixes(dve, chain):
            dve.memset(ones[:, :], 1.0)
            chain.link(dve.memset(before[:, 0, :], 0.0))
            for j in range(1, NT):
                chain.link(dve.tensor_tensor(before[:, j, :], before[:, j - 1, :], chosen[:, j - 1, :], ALU.add))
        jobs = []
        for j in range(NT):
            def write(eng, acc, j=j):
                return eng.tensor_tensor(slot[:, j, :], acc, chosen[:, j, :], ALU.mult)
            jobs.append(([(tri[:, :], chosen[:, j, :]), (ones[:, :], before[:, j, :])], (P, E), "dve", write))
        matmul_jobs(chip, jobs, [(tri[:, :], w["tri"]), (iota[:, :], w["iota"].partition_broadcast(P))], setup=prefixes)

        with Stage(chip) as st:
            W1, W2 = ([st.sbuf(P, DC, HID) for _ in range(2)] for _ in range(2))
            W3 = [st.sbuf(P, M, D) for _ in range(2)]
            cur, scale = ([st.sbuf(P, NT) for _ in range(2)] for _ in range(2))
            hot = [st.sbuf(P, NT, CAP) for _ in range(2)]
            hotT = st.sbuf(HC, 2, T)
            taken = st.sbuf(P, DC, CAP)
            sil, hid = st.sbuf(P, M, CAP), st.sbuf(P, M, CAP)
            given = st.sbuf(HC, 2, D)
            acc_take, acc_out = st.psum(P, DC, HALF // 2), st.psum(HC, 2, D)
            acc_turn = [st.psum(P, HALF) for _ in range(2)]
            acc_up = [st.psum(P, 2, HALF // 2) for _ in range(2)]
            acc_y = [st.psum(P, HALF) for _ in range(2)]
            weights_in = st.sems(2)
            (cols_ready, cur_steps, hot_ready, take_filled, taken_ready, turned, turn_copied, up_filled, silu_done,
             hid_ready, out_filled, given_ready, y_filled, added) = st.sems(14)
            block = st.block()

            @block.sync
            def _(sync):
                st.clear_other_set(sync)
                for i in peeled(sync, E // 2):
                    for x in range(2):
                        e = i * 2 + x
                        if later(i, 1):
                            sync.wait_ge(out_filled, e - 1)
                        for dst, name in ((W1, "W1"), (W2, "W2"), (W3, "W3")):
                            sync.dma_start(dst[x][:, :, :], w[name][bass.ds(e, 1)].rearrange("o p k n -> p (o k) n")
                                           ).then_inc(weights_in[x], 16)

            @block.tensor
            def _(pe):
                for i in peeled(pe, E // 2):
                    for x in range(2):
                        e = i * 2 + x
                        pe.wait_ge(hot_ready, e + 1)
                        if later(e, 1):
                            pe.wait_ge(taken_ready, e)
                        for c in range(DC):
                            for j in range(NT):
                                ins = pe.matmul(acc_take[:, c, 0:CAP], xn[:, j, tile(c)], hot[x][:, j, :],
                                                start=(j == 0), stop=(j == NT - 1))
                        ins.then_inc(take_filled, 1)
                        for n in range(4):
                            if later(e * 4 + n, 2):
                                pe.wait_ge(turn_copied, e * 4 + n - 1)
                            for q in range(4):
                                s, j = n // 2, (n % 2) * 4 + q
                                ins = pe.transpose(acc_turn[n % 2][0:HC, q * P:(q + 1) * P],
                                                   hot[x][:, j, s * HC:(s + 1) * HC], ident[:, :])
                            ins.then_inc(turned, 1)
                        pe.wait_ge(weights_in[x], i * 48 + 48)
                        pe.wait_ge(taken_ready, e + 1)
                        for m in range(M):
                            if later(e * M + m, 2):
                                pe.wait_ge(hid_ready, e * M + m - 1)
                            for u, wt in enumerate((W1[x], W2[x])):
                                for k in range(DC):
                                    ins = pe.matmul(acc_up[m % 2][:, u, 0:CAP], wt[:, k, tile(m)], taken[:, k, :],
                                                    start=(k == 0), stop=(k == DC - 1))
                            ins.then_inc(up_filled, 1)
                        pe.wait_ge(hid_ready, e * M + M)
                        if later(e, 1):
                            pe.wait_ge(given_ready, e)
                        for s in range(2):
                            for k in range(M):
                                ins = pe.matmul(acc_out[:, s, :], hid[:, k, s * HC:(s + 1) * HC], W3[x][:, k, :],
                                                start=(k == 0), stop=(k == M - 1))
                        ins.then_inc(out_filled, 1)
                        pe.wait_ge(given_ready, e + 1)
                        pe.wait_ge(turn_copied, e * 4 + 4)
                        for j in range(NT):
                            if later(e * NT + j, 2):
                                pe.wait_ge(added, e * NT + j - 1)
                            for s in range(2):
                                ins = pe.matmul(acc_y[j % 2][:, 0:D], hotT[:, s, tile(j)], given[:, s, :],
                                                start=(s == 0), stop=(s == 1))
                            ins.then_inc(y_filled, 1)

            @block.scalar
            def _(act):
                for i in peeled(act, E // 2):
                    for x in range(2):
                        e = i * 2 + x
                        act.wait_ge(take_filled, e + 1)
                        if later(e, 1):
                            act.wait_ge(up_filled, e * M)
                        act.copy(taken[:, :, :], acc_take[:, :, 0:CAP]).then_inc(taken_ready, 1)
                        for n in range(4):
                            act.wait_ge(turned, e * 4 + n + 1)
                            if n == 0 and later(e, 1):
                                act.wait_ge(y_filled, e * NT)
                            act.copy(hotT[:, n // 2, halves(n % 2)], acc_turn[n % 2][0:HC, :]).then_inc(turn_copied, 1)
                        for m in range(M):
                            act.wait_ge(up_filled, e * M + m + 1)
                            if m == 0 and later(e, 1):
                                act.wait_ge(hid_ready, e * M)
                            act.activation(sil[:, m, :], acc_up[m % 2][:, 0, 0:CAP], ACT.Silu).then_inc(silu_done, 1)
                        act.wait_ge(out_filled, e + 1)
                        if later(e, 1):
                            act.wait_ge(y_filled, e * NT)
                        act.copy(given[:, :, :], acc_out[:, :, :]).then_inc(given_ready, 1)

            @block.vector
            def _(dve):
                def one_hot(e, x):
                    at = bass.ds(e, 1)
                    if later(e, 2):
                        dve.wait_ge(added, e * NT - NT)
                    dve.tensor_copy(cur[x][:, :], slot[:, :, at].rearrange("p j o -> p (j o)"))
                    dve.tensor_copy(scale[x][:, :], choice[:, :, at].rearrange("p j o -> p (j o)")
                                    ).then_inc(cols_ready, 1)
                    dve.wait_ge(cols_ready, e + 1)
                    if later(e, 2):
                        dve.wait_ge(turned, e * 4 - 4)
                    for j in range(NT):
                        ins = dve.tensor_scalar(hot[x][:, j, :], iota[:, :], cur[x][:, j:j + 1], None, ALU.is_equal)
                    ins.then_inc(hot_ready, 1)

                for i in peeled(dve, E // 2):
                    for x in range(2):
                        e = i * 2 + x
                        one_hot(e, x)
                        for m in range(M):
                            dve.wait_ge(silu_done, e * M + m + 1)
                            if m == 0 and later(e, 1):
                                dve.wait_ge(out_filled, e)
                            dve.tensor_tensor(hid[:, m, :], sil[:, m, :], acc_up[m % 2][:, 1, 0:CAP],
                                              ALU.mult).then_inc(hid_ready, 1)
                        if later(e, 1):
                            dve.wait_ge(added, e * NT)
                        for j in range(NT):
                            dve.wait_ge(y_filled, e * NT + j + 1)
                            dve.scalar_tensor_tensor(out=X[:, j, :], in0=acc_y[j % 2][:, 0:D],
                                                     scalar=scale[x][:, j:j + 1], in1=X[:, j, :],
                                                     op0=ALU.mult, op1=ALU.add).then_inc(added, 1)


def attend_context(chip, X, q0, q1, out0, out1, out_bias, ones, w, heads, ident):
    nc = chip.nc
    HT = min(heads, 2)
    R = HT * S
    N = heads // HT
    BL = 2 if N > 1 else 4
    U = BL * N
    PAIR = 2 * N
    ROUNDS, G = B // BL, B * N
    K1 = q1.shape[0]
    NB = 2 if N > 1 else 4
    with Stage(chip) as st:
        ctx = [st.sbuf(P, KT, CC) for _ in range(NB)]
        ct0, ct1 = [st.sbuf(P, SK) for _ in range(NB)], [st.sbuf(K1, SK) for _ in range(NB)]
        a0, a1 = [st.sbuf(P, heads, S) for _ in range(NB)], [st.sbuf(K1, heads, S) for _ in range(NB)]
        probs = [st.sbuf(R, SK) for _ in range(2)]
        probsT = [st.sbuf(P, KT, R) for _ in range(2)]
        mixed = [st.sbuf(R, CC) for _ in range(2)]
        m0, m1 = st.sbuf(P, heads, P), st.sbuf(C1, heads, P)
        negmax, total, inverse = st.sbuf(R, 4), st.sbuf(R, 4), st.sbuf(R, 4)
        acc_s = [st.psum(R, SK) for _ in range(2)]
        acc_t = st.psum(P, KT, R)
        acc_o = st.psum(R, HALF)
        acc_my = st.psum(P, HALF)
        acc_m0, acc_m1, acc_y = acc_my[:, 0:R], acc_my[0:C1, R:2 * R], acc_my[:, D:2 * D]
        ctx_in = st.sems(NB)
        (ones_ready, staged, scores_ready, max_ready, probs_ready, probs_turned, turned_copied, mixed_filled,
         inverse_ready, mixed_ready, mixed_turned, mixed_copied, y_filled, added) = st.sems(14)
        block = st.block()

        def steps(eng, body):
            for i in peeled(eng, ROUNDS, 2):
                for u in range(U):
                    body(i, u, i * U + u)
            for u in range(5):
                body(ROUNDS, u, G + u)

        def constant_wait(pe):
            if R < P:
                pe.wait_ge(ones_ready, NB)

        def live(g, lag):
            return lag <= g < G + lag if isinstance(g, int) else True

        @block.sync
        def _(sync):
            st.clear_other_set(sync)
            if K1 > C1:
                sync.wait_ge(ones_ready, NB)
            for i in peeled(sync, ROUNDS, 2):
                for b in range(BL):
                    x, n = b % NB, i * BL + b
                    if later(n, NB):
                        sync.wait_ge(mixed_filled, n * N - (NB - 1) * N)
                    one = bass.ds(n, 1)
                    sync.dma_start(ctx[x][:, :, :], w["ctx"][one].rearrange("o p k c -> p (o k) c")).then_inc(ctx_in[x], 16)
                    sync.dma_start(ct0[x][:, :], w["ctxT"][one, 0:P].rearrange("o p k -> p (o k)")).then_inc(ctx_in[x], 16)
                    sync.dma_start(ct1[x][0:C1, :], w["ctxT"][one, P:CC].rearrange("o p k -> p (o k)")
                                   ).then_inc(ctx_in[x], 16)

        @block.gpsimd
        def _(pool):
            for i in peeled(pool, ROUNDS, 2):
                for b in range(BL):
                    x, n = b % NB, i * BL + b
                    if later(n, NB):
                        pool.wait_ge(scores_ready, n * N - (NB - 1) * N)
                    pool.tensor_copy(a0[x][:, :, :], q0[:, :, bass.ds(n * S, S)]).then_inc(staged, 1)
                    pool.tensor_copy(a1[x][:, :, :], q1[:, :, bass.ds(n * S, S)]).then_inc(staged, 1)

        @block.tensor
        def _(pe):
            if K1 > C1:
                pe.wait_ge(ones_ready, NB)

            def body(i, u, g):
                ends = live(g, 4) and (u - 4) % PAIR == PAIR - 1
                p = i * (U // PAIR) + (u - 3 - PAIR) // PAIR
                if ends:
                    pe.wait_ge(mixed_copied, g - 3)
                    for h in range(heads):
                        pe.matmul(acc_y, m0[:, h, :], out0[:, h, :], start=(h == 0), stop=False)
                        pe.matmul(acc_y, m1[:, h, :], out1[:, h, :], start=False, stop=False)
                    pe.matmul(acc_y, ones[:, :], out_bias[:, :], start=False, stop=True).then_inc(y_filled, 1)
                if live(g, 0):
                    b, r = u // N, u % N
                    x = b % NB
                    if r == 0:
                        pe.wait_ge(staged, (i * BL + b) * 2 + 2)
                        pe.wait_ge(ctx_in[x], i * (48 * BL // NB) + (b // NB) * 48 + 48)
                    if later(g, 2):
                        pe.wait_ge(probs_ready, g - 1)
                    for h in range(2):
                        pe.matmul(acc_s[u % 2][:, halves(h)], a0[x][:, r * HT:(r + 1) * HT, :], ct0[x][:, halves(h)],
                                  start=True, stop=False)
                        ins = pe.matmul(acc_s[u % 2][:, halves(h)], a1[x][:, r * HT:(r + 1) * HT, :],
                                        ct1[x][:, halves(h)], start=False, stop=True)
                    ins.then_inc(scores_ready, 1)
                if live(g, 1):
                    constant_wait(pe)
                    pe.wait_ge(probs_ready, g)
                    if later(g, 2):
                        pe.wait_ge(turned_copied, g - 1)
                    for k in range(KT):
                        ins = pe.transpose(acc_t[:, k, :], probs[(u - 1) % 2][:, tile(k)], ident[0:R, 0:R])
                    ins.then_inc(probs_turned, 1)
                if ends:
                    pe.wait_ge(added, p + 1)
                if live(g, 3) and later(g, 4):
                    pe.wait_ge(mixed_copied, g - 3)
                if live(g, 2):
                    b = (u - 2) % U // N
                    pe.wait_ge(turned_copied, g - 1)
                    if later(g, 3):
                        pe.wait_ge(mixed_ready, g - 2)
                    for k in range(KT):
                        ins = pe.matmul(acc_o[:, 0:CC], probsT[u % 2][:, k, :], ctx[b % NB][:, k, :],
                                        start=(k == 0), stop=(k == KT - 1))
                    ins.then_inc(mixed_filled, 1)
                if live(g, 3):
                    constant_wait(pe)
                    pe.wait_ge(mixed_ready, g - 2)
                    pe.transpose(acc_m0, mixed[(u - 3) % 2][:, 0:P], ident[0:R, 0:R])
                    pe.transpose(acc_m1, mixed[(u - 3) % 2][:, P:CC], ident[0:R, 0:R]).then_inc(mixed_turned, 1)
            steps(pe, body)

        @block.scalar
        def _(act):
            def body(i, u, g):
                if live(g, 0):
                    act.wait_ge(max_ready, g + 1)
                    if later(g, 2):
                        act.wait_ge(probs_turned, g - 1)
                    if later(g, 4):
                        act.wait_ge(inverse_ready, g - 3)
                    act.activation(probs[u % 2][:, :], acc_s[u % 2][:, :], ACT.Exp, bias=negmax[:, u % 4:u % 4 + 1],
                                   accum_out=total[:, u % 4:u % 4 + 1]).then_inc(probs_ready, 1)
                if live(g, 3):
                    v = (u - 3) % U
                    h0, at = v % N * HT, (v // N) % 2 * S
                    act.wait_ge(mixed_turned, g - 2)
                    p = i * (U // PAIR) + (u - 3) // PAIR
                    if v % PAIR == 0 and later(p, 1):
                        act.wait_ge(y_filled, p)
                    act.copy(m0[:, h0:h0 + HT, at:at + S], acc_m0.rearrange("p (h s) -> p h s", s=S))
                    act.copy(m1[:, h0:h0 + HT, at:at + S], acc_m1.rearrange("p (h s) -> p h s", s=S)
                             ).then_inc(mixed_copied, 1)
            steps(act, body)

        @block.vector
        def _(dve):
            if K1 > C1:
                for x in range(NB):
                    dve.memset(ct1[x][C1:K1, :], 1.0).then_inc(ones_ready, 1)

            def body(i, u, g):
                if live(g, 0):
                    dve.wait_ge(scores_ready, g + 1)
                    dve.tensor_reduce(negmax[:, u % 4:u % 4 + 1], acc_s[u % 2][:, :], AX.X, ALU.max, negate=True
                                      ).then_inc(max_ready, 1)
                if live(g, 1):
                    dve.wait_ge(probs_turned, g)
                    if later(g, 3):
                        dve.wait_ge(mixed_filled, g - 2)
                    dve.tensor_copy(probsT[(u - 1) % 2][:, :, :], acc_t[:, :, :]).then_inc(turned_copied, 1)
                if live(g, 4) and (u - 4) % PAIR == PAIR - 1:
                    p = i * (U // PAIR) + (u - 3 - PAIR) // PAIR
                    at = bass.ds(p, 1)
                    dve.wait_ge(y_filled, p + 1)
                    dve.tensor_tensor(X[:, at, :].rearrange("p o d -> p (o d)"), X[:, at, :].rearrange("p o d -> p (o d)"),
                                      acc_y, ALU.add).then_inc(added, 1)
                if live(g, 2):
                    v = (u - 2) % 4
                    dve.wait_ge(probs_ready, g - 1)
                    dve.reciprocal(inverse[:, v:v + 1], total[:, v:v + 1]).then_inc(inverse_ready, 1)
                    dve.wait_ge(inverse_ready, g - 1)
                    dve.wait_ge(mixed_filled, g - 1)
                    if later(g, 4):
                        dve.wait_ge(mixed_turned, g - 3)
                    dve.tensor_scalar(mixed[u % 2][:, :], acc_o[:, 0:CC], inverse[:, v:v + 1], None, ALU.mult
                                      ).then_inc(mixed_ready, 1)
            steps(dve, body)


def one_head_xattn(chip, X, xn, xnT, ident, w):
    with ExitStack() as es:
        sb = buffers(chip, es)
        qT, q0, q1 = sb(P, DC, T), sb(P, 1, T), sb(C1 + 1, 1, T)
        Wq, Wk, bq = sb(P, DC, D), sb(P, DC, CC + 1), sb(P, DC)
        out0, out1, bv, ones = sb(P, 1, D), sb(C1, 1, D), sb(1, D), sb(1, P)
        fill(chip, [(ones[:, :], 1.0)], [])
        jobs = []
        for m in range(DC):
            for h in range(2):
                def write(eng, acc, m=m, h=h):
                    return eng.tensor_scalar(qT[:, m, halves(h)], acc, bq[:, m:m + 1], D ** -0.5, ALU.add, ALU.mult)
                jobs.append(([(Wq[:, k, tile(m)], xnT[:, k, halves(h)]) for k in range(DC)], (P, HALF), "dve", write))
        matmul_jobs(chip, jobs, [(Wq[:, :, :], w["Wq"]), (bq[:, :], w["bq"]), (Wk[:, :, :], w["Wk"]),
                                 (out0[:, 0, :], w["Wv"][0:P]), (out1[:, 0, :], w["Wv"][P:CC]),
                                 (bv[:, :], w["bv"])])
        jobs = []
        for h in range(2):
            for dst, c0, c1 in ((q0, 0, P), (q1, P, CC + 1)):
                jobs.append(([(Wk[:, k, c0:c1], qT[:, k, halves(h)]) for k in range(DC)], (c1 - c0, HALF),
                             ("act", "dve")[h], copy_out(dst[:, 0, halves(h)])))
        matmul_jobs(chip, jobs, [])
        attend_context(chip, X, q0, q1, out0, out1, bv, ones, w, 1, ident)


def eight_head_xattn(chip, X, xn, xnT, ident, w):
    HEADS, DH = 8, 64
    INNER = HEADS * DH
    MC = INNER // P
    with ExitStack() as es:
        sb = buffers(chip, es)
        q0, q1 = sb(P, HEADS, T), sb(C1, HEADS, T)
        out0, out1, bo, ones = sb(P, HEADS, D), sb(C1, HEADS, D), sb(1, D), sb(1, P)
        fill(chip, [(ones[:, :], 1.0)], [])
        with ExitStack() as inner:
            ib = buffers(chip, inner)
            qT, Wq = ib(P, MC, T), ib(P, DC, INNER)
            WkT, WvT, Wo = ib(P, MC, CC), ib(P, MC, CC), ib(P, MC, D)
            jobs = []
            for m in range(MC):
                for h in range(2):
                    def write(eng, acc, m=m, h=h):
                        dst = qT[:, m, halves(h)]
                        if is_scalar_engine(eng):
                            return eng.activation(dst, acc, ACT.Copy, scale=DH ** -0.5)
                        return eng.tensor_scalar(dst, acc, DH ** -0.5, None, ALU.mult)
                    jobs.append(([(Wq[:, k, tile(m)], xnT[:, k, halves(h)]) for k in range(DC)], (P, HALF),
                                 ("act", "dve")[h], write))
            matmul_jobs(chip, jobs, [(Wq[:, :, :], w["Wq"]), (WkT[:, :, :], w["WkT"]), (WvT[:, :, :], w["WvT"]),
                                     (Wo[:, :, :], w["Wo"]), (bo[:, :], w["bo"])])
            jobs = []
            for n in range(HEADS):
                at = slice((n % 2) * DH, (n % 2) * DH + DH)
                for t, (qd, od, c0, c1) in enumerate(((q0, out0, 0, P), (q1, out1, P, CC))):
                    for h in range(2):
                        jobs.append(([(WkT[at, n // 2, c0:c1], qT[at, n // 2, halves(h)])], (c1 - c0, HALF),
                                     ("act", "dve")[h], copy_out(qd[:, n, halves(h)])))
                    jobs.append(([(WvT[at, n // 2, c0:c1], Wo[at, n // 2, :])], (c1 - c0, D),
                                 ("act", "dve")[t], copy_out(od[:, n, :])))
            matmul_jobs(chip, jobs, [])
        attend_context(chip, X, q0, q1, out0, out1, bo, ones, w, HEADS, ident)


def sixteen_head_xattn(chip, X, xn, xnT, ident, w):
    nc = chip.nc
    HEADS, DH = 16, 16
    N = HEADS // 2
    G = B * N
    BL = 2
    U = BL * N
    ROUNDS = B // BL
    with ExitStack() as es:
        sb = buffers(chip, es)
        qT, Wq, bq = sb(P, DC, T), sb(P, DC, D), sb(P, DC)
        Wk0, Wk1, bk = sb(P, D), sb(C1, D), sb(P, DC)
        Wv0, Wv1 = sb(P, D), sb(C1 + 1, D)
        Wo, bo, ones = sb(P, DC, D), sb(1, D), sb(1, P)
        pairs_mask = sb(P, N // DC, 2)
        own = sb(P, 2)
        fold = sb(P, S)
        fill(chip, [(ones[:, :], 1.0)], [])
        jobs = []
        for m in range(DC):
            for h in range(2):
                def write(eng, acc, m=m, h=h):
                    return eng.tensor_scalar(qT[:, m, halves(h)], acc, bq[:, m:m + 1], DH ** -0.5, ALU.add, ALU.mult)
                jobs.append(([(Wq[:, k, tile(m)], xnT[:, k, halves(h)]) for k in range(DC)], (P, HALF), "dve", write))
        matmul_jobs(chip, jobs, [(Wq[:, :, :], w["Wq"]), (bq[:, :], w["bq"]), (Wk0[:, :], w["Wk"][0:P]),
                                 (Wk1[:, :], w["Wk"][P:CC]), (bk[:, :], w["bk"]), (Wv0[:, :], w["Wv"][0:P]),
                                 (Wv1[:, :], w["Wv"][P:CC + 1]), (Wo[:, :, :], w["Wo"]), (bo[:, :], w["bo"]),
                                 (pairs_mask[:, :, :], w["pairs_mask"]), (own[:, :], w["own"]), (fold[:, :], w["fold"])])
        with Stage(chip) as st:
            ct0, ct1 = [st.sbuf(P, SK) for _ in range(2)], [st.sbuf(C1 + 1, SK) for _ in range(2)]
            kT = [st.sbuf(P, DC, SK) for _ in range(2)]
            v = [st.sbuf(P, KT, D) for _ in range(2)]
            a = [st.sbuf(P, N, 2, S) for _ in range(2)]
            probs = [st.sbuf(P, SK) for _ in range(2)]
            probsT = [st.sbuf(P, KT, P) for _ in range(2)]
            mixed = [st.sbuf(P, N, 2 * DH) for _ in range(2)]
            mT = st.sbuf(P, DC, P)
            negmax, total, inverse = st.sbuf(P, 4), st.sbuf(P, 4), st.sbuf(P, 4)
            acc_s = [st.psum(P, SK) for _ in range(2)]
            acc_t = [st.psum(P, HALF) for _ in range(2)]
            acc_kv = st.psum(P, HALF)
            acc_o = st.psum(P, HALF)
            acc_m, acc_y = acc_o[:, 64:64 + DC * S], acc_o[:, D:2 * D]
            ctx_in = st.sems(2)
            (ones_ready, staged, scores_ready, max_ready, probs_ready, probs_turned, turned_copied, mixed_filled,
             inverse_ready, mixed_ready, folded, folded_copied, y_filled, added, kv_filled, kv_ready) = st.sems(16)
            block = st.block()

            def steps(eng, body):
                for i in peeled(eng, ROUNDS, 2, 1):
                    for u in range(U):
                        body(i, u, i * U + u)
                for u in range(4):
                    body(ROUNDS, u, G + u)

            def live(g, lag):
                return lag <= g < G + lag if isinstance(g, int) else True

            def ends_batch(g, u, lag):
                return live(g, lag) and (u - lag) % N == N - 1

            @block.sync
            def _(sync):
                st.clear_other_set(sync)
                sync.wait_ge(ones_ready, 2)
                for i in peeled(sync, ROUNDS):
                    for x in range(BL):
                        n = i * BL + x
                        if later(n, 2):
                            sync.wait_ge(kv_filled, n * 8 - 8)
                        one = bass.ds(n, 1)
                        sync.dma_start(ct0[x][:, :], w["ctxT"][one, 0:P].rearrange("o p k -> p (o k)")
                                       ).then_inc(ctx_in[x], 16)
                        sync.dma_start(ct1[x][0:C1, :], w["ctxT"][one, P:CC].rearrange("o p k -> p (o k)")
                                       ).then_inc(ctx_in[x], 16)

            @block.gpsimd
            def _(pool):
                for i in peeled(pool, ROUNDS):
                    for x in range(BL):
                        n = i * BL + x
                        if later(n, 2):
                            pool.wait_ge(scores_ready, n * N - N)
                        for c in range(DC):
                            for s in range(2):
                                q = N // DC
                                pool.tensor_tensor(
                                    a[x][:, c * q:(c + 1) * q, s, :],
                                    qT[:, c:c + 1, bass.ds(n * S, S)].broadcast_to([P, q, S]),
                                    pairs_mask[:, :, s:s + 1].broadcast_to([P, q, S]), ALU.mult).then_inc(staged, 1)

            def project(pe, x, t, done):
                if t < 4:
                    m, h = t // 2, t % 2
                    pe.matmul(acc_kv[:, :], Wk0[:, tile(m)], ct0[x][:, halves(h)], start=True, stop=False)
                    ins = pe.matmul(acc_kv[:, :], Wk1[:, tile(m)], ct1[x][0:C1, halves(h)], start=False, stop=True)
                else:
                    for s in range(2):
                        k = (t - 4) * 2 + s
                        pe.matmul(acc_kv[:, s * D:(s + 1) * D], ct0[x][:, tile(k)], Wv0[:, :], start=True, stop=False)
                        ins = pe.matmul(acc_kv[:, s * D:(s + 1) * D], ct1[x][:, tile(k)], Wv1[:, :],
                                        start=False, stop=True)
                ins.then_inc(kv_filled, 1)

            def project_out(act, x, t):
                if t < 4:
                    m, h = t // 2, t % 2
                    return act.activation(kT[x][:, m, halves(h)], acc_kv[:, :], ACT.Identity, bias=bk[:, m:m + 1])
                k = (t - 4) * 2
                return act.copy(v[x][:, k:k + 2, :], acc_kv[:, :].rearrange("p (k d) -> p k d", k=2))

            @block.tensor
            def _(pe):
                pe.wait_ge(ones_ready, 2)
                pe.wait_ge(ctx_in[0], 32)
                for t in range(8):
                    if t:
                        pe.wait_ge(kv_ready, t)
                    project(pe, 0, t, t)

                def body(i, u, g):
                    x, r = u // N, u % N
                    if ends_batch(g, u, 3):
                        xb = (u - 3) % U // N
                        b = i * BL + (u - 3 - (N - 1)) // N
                        pe.wait_ge(mixed_ready, g - 2)
                        if later(b, 1):
                            pe.wait_ge(folded_copied, b)
                        for c in range(DC):
                            ins = pe.matmul(acc_m[:, c * S:(c + 1) * S],
                                            mixed[xb][:, 4 * c:4 * c + 4, :], fold[:, :], start=True, stop=True)
                        ins.then_inc(folded, 1)
                        pe.wait_ge(folded_copied, b + 1)
                        if xb == 1:
                            for c in range(DC):
                                pe.matmul(acc_y, mT[:, c, :], Wo[:, c, :], start=(c == 0), stop=False)
                            pe.matmul(acc_y, ones[:, :], bo[:, :], start=False, stop=True).then_inc(y_filled, 1)
                            pe.wait_ge(added, i + (u - 3 - (U - 1)) // U + 1)
                    if live(g, 0):
                        if r == 0:
                            pe.wait_ge(staged, (i * BL + x) * 4 + 4)
                            pe.wait_ge(kv_ready, (i * BL + x) * 8 + 8)
                        if later(g, 2):
                            pe.wait_ge(probs_ready, g - 1)
                        for h in range(2):
                            ins = pe.matmul(acc_s[u % 2][:, halves(h)], a[x][:, r, :, :], kT[x][:, r // 4, halves(h)],
                                            start=True, stop=True)
                        ins.then_inc(scores_ready, 1)
                    if live(g, 1):
                        pe.wait_ge(probs_ready, g)
                        for s in range(2):
                            if later(g, 2):
                                pe.wait_ge(turned_copied, 2 * g - 3 + s)
                            for k in range(4):
                                ins = pe.transpose(acc_t[s][:, tile(k)], probs[(u - 1) % 2][:, tile(4 * s + k)],
                                                   ident[:, :])
                            ins.then_inc(probs_turned, 1)
                    if live(g, 0) and (not isinstance(g, int) or g < G - N):
                        if r == 0:
                            pe.wait_ge(ctx_in[1 - x], (i + (1 if x == 1 else 0)) * 32 + 32)
                        pe.wait_ge(kv_ready, g + 8)
                        project(pe, 1 - x, r, g)
                    if live(g, 2):
                        r2, x2 = (u - 2) % N, (u - 2) % U // N
                        pe.wait_ge(turned_copied, 2 * g - 2)
                        if later(g, 3):
                            pe.wait_ge(mixed_ready, g - 2)
                        for k in range(KT):
                            ins = pe.matmul(acc_o[:, 0:2 * DH], probsT[u % 2][:, k, :],
                                            v[x2][:, k, r2 * 2 * DH:(r2 + 1) * 2 * DH],
                                            start=(k == 0), stop=(k == KT - 1))
                        ins.then_inc(mixed_filled, 1)
                steps(pe, body)

            @block.scalar
            def _(act):
                for t in range(8):
                    act.wait_ge(kv_filled, t + 1)
                    project_out(act, 0, t).then_inc(kv_ready, 1)

                def body(i, u, g):
                    x, r = u // N, u % N
                    if live(g, 0):
                        act.wait_ge(max_ready, g + 1)
                        if later(g, 2):
                            act.wait_ge(probs_turned, 2 * g - 2)
                        if later(g, 4):
                            act.wait_ge(inverse_ready, g - 3)
                        act.activation(probs[u % 2][:, :], acc_s[u % 2][:, :], ACT.Exp,
                                       bias=negmax[:, u % 4:u % 4 + 1], accum_out=total[:, u % 4:u % 4 + 1]
                                       ).then_inc(probs_ready, 1)
                    if live(g, 0) and (not isinstance(g, int) or g < G - N):
                        act.wait_ge(kv_filled, g + 9)
                        if later(g, N):
                            act.wait_ge(scores_ready if r < 4 else mixed_filled, i * U + x * N)
                        project_out(act, 1 - x, r).then_inc(kv_ready, 1)
                steps(act, body)

            @block.vector
            def _(dve):
                for x in range(2):
                    dve.memset(ct1[x][C1:C1 + 1, :], 1.0).then_inc(ones_ready, 1)

                def body(i, u, g):
                    if ends_batch(g, u, 3):
                        xb = (u - 3) % U // N
                        b = i * BL + (u - 3 - (N - 1)) // N
                        dve.wait_ge(folded, b + 1)
                        p = i + (u - 3 - (U - 1)) // U
                        dve.tensor_copy(mT[:, :, xb * S:(xb + 1) * S], acc_m.rearrange("p (c s) -> p c s", c=DC)
                                        ).then_inc(folded_copied, 1)
                        if xb == 1:
                            at = bass.ds(p, 1)
                            dve.wait_ge(y_filled, p + 1)
                            dve.tensor_tensor(X[:, at, :].rearrange("p o d -> p (o d)"),
                                              X[:, at, :].rearrange("p o d -> p (o d)"), acc_y, ALU.add
                                              ).then_inc(added, 1)
                    if live(g, 0):
                        dve.wait_ge(scores_ready, g + 1)
                        dve.tensor_reduce(negmax[:, u % 4:u % 4 + 1], acc_s[u % 2][:, :], AX.X, ALU.max, negate=True
                                          ).then_inc(max_ready, 1)
                    if live(g, 1):
                        for s in range(2):
                            dve.wait_ge(probs_turned, 2 * g - 1 + s)
                            if later(g, 3) and s == 0:
                                dve.wait_ge(mixed_filled, g - 2)
                            dve.tensor_copy(probsT[(u - 1) % 2][:, 4 * s:4 * s + 4, :],
                                            acc_t[s][:, :].rearrange("p (k r) -> p k r", r=P)
                                            ).then_inc(turned_copied, 1)
                    if live(g, 2):
                        c4, r2, x2 = (u - 2) % 4, (u - 2) % N, (u - 2) % U // N
                        dve.wait_ge(probs_ready, g - 1)
                        dve.reciprocal(inverse[:, c4:c4 + 1], total[:, c4:c4 + 1]).then_inc(inverse_ready, 1)
                        dve.wait_ge(inverse_ready, g - 1)
                        dve.wait_ge(mixed_filled, g - 1)
                        for s in range(2):
                            ins = dve.tensor_scalar(mixed[x2][:, r2, s * DH:(s + 1) * DH],
                                                    acc_o[:, s * DH:(s + 1) * DH], inverse[:, c4:c4 + 1],
                                                    own[:, s:s + 1], ALU.mult, ALU.mult)
                        ins.then_inc(mixed_ready, 1)
                steps(dve, body)


def log1p_coefficients():
    import numpy as np
    n = 64
    q = (1 - np.cos((np.arange(n) + 0.5) * np.pi / n)) / 18
    r = np.sqrt(q)
    fit = np.polynomial.Polynomial.fit(q, 2 * np.arctanh(r) / r, 4, domain=[0, 1 / 9]).convert()
    return [float(c) for c in fit.coef]


def selective_scan(chip, X, xn, xnT, ident, w):
    nc = chip.nc
    CH, NS = 512, 16
    C = CH // P
    with ExitStack() as es:
        sb = buffers(chip, es)
        u, gate, delta, du = (sb(P, C, T) for _ in range(4))
        A, Dp, cw, cb, dtb = sb(P, NS, C), sb(P, C), sb(P, C, 3), sb(P, C), sb(P, C)
        rows_dram = nc.dram_tensor("state_rows", [2 * NS, T], F32, kind="Internal").ap()

        with ExitStack() as inner:
            ib = buffers(chip, inner)
            up, Win = ib(P, C, B, S + 2), ib(P, DC, 2 * CH)
            fill(chip, [(up[:, :, :, 0:1], 0.0), (up[:, :, :, S + 1:S + 2], 0.0)], [])
            jobs = []
            for m in range(2 * C):
                for h in range(2):
                    def write(eng, acc, m=m, h=h):
                        if m < C:
                            return eng.tensor_copy(up[:, m, 8 * h:8 * h + 8, 1:S + 1],
                                                   acc.rearrange("p (b s) -> p b s", s=S))
                        return eng.activation(gate[:, m - C, halves(h)], acc, ACT.Silu)
                    jobs.append(([(Win[:, k, tile(m)], xnT[:, k, halves(h)]) for k in range(DC)], (P, HALF),
                                 "dve" if m < C else "act", write))
            matmul_jobs(chip, jobs, [(Win[:, :, :], w["in_proj_w"]), (cw[:, :, :], w["conv_w"]), (cb[:, :], w["conv_b"]),
                                     (Dp[:, :], w["D_param"]), (dtb[:, :], w["dt_proj_b"]), (A[:, :, :], w["A_log"])])
            with Stage(chip) as st:
                steps, conv_done, a_ready = st.sems(3)
                block = st.block()

                @block.sync
                def _(sync):
                    st.clear_other_set(sync)

                @block.vector
                def _(dve):
                    c = Chain(dve, steps)
                    for m in range(C):
                        t = delta[:, m, :].rearrange("p (b s) -> p b s", s=S)
                        c.link(dve.tensor_scalar(t, up[:, m, :, 0:S], cw[:, m, 0:1], cb[:, m:m + 1], ALU.mult, ALU.add))
                        for k in (1, 2):
                            ins = dve.scalar_tensor_tensor(out=t, in0=up[:, m, :, k:k + S], scalar=cw[:, m, k:k + 1],
                                                           in1=t, op0=ALU.mult, op1=ALU.add)
                            if k == 1:
                                c.link(ins)
                        ins.then_inc(conv_done, 1)
                    dve.wait_ge(a_ready, 1)
                    dve.tensor_scalar(A[:, :, :], A[:, :, :], -1.0, None, ALU.mult)

                @block.scalar
                def _(act):
                    act.activation(A[:, :, :], A[:, :, :], ACT.Exp).then_inc(a_ready, 1)
                    for m in range(C):
                        act.wait_ge(conv_done, m + 1)
                        act.activation(u[:, m, :], delta[:, m, :], ACT.Silu)

        with ExitStack() as inner:
            ib = buffers(chip, inner)
            low, Wx, Wdt, bc = ib(P, C, T), ib(P, C, CH + 2 * NS), ib(P, C, CH), ib(2 * NS, T)
            jobs = []
            for h in range(2):
                for m in range(C + 1):
                    r = P if m < C else 2 * NS
                    dst = low[:, m, halves(h)] if m < C else bc[:, halves(h)]
                    jobs.append(([(Wx[:, k, m * P:m * P + r], u[:, k, halves(h)]) for k in range(C)], (r, HALF),
                                 ("act", "dve")[m % 2], copy_out(dst)))
            matmul_jobs(chip, jobs, [(Wx[:, :, :], w["x_proj_w"]), (Wdt[:, :, :], w["dt_proj_w"])])
            jobs = []
            for m in range(C):
                for h in range(2):
                    def write(eng, acc, m=m, h=h):
                        b = dtb[:, m:m + 1]
                        if is_scalar_engine(eng):
                            return eng.activation(delta[:, m, halves(h)], acc, ACT.Identity, bias=b)
                        return eng.tensor_scalar(delta[:, m, halves(h)], acc, b, None, ALU.add)
                    jobs.append(([(Wdt[:, k, tile(m)], low[:, k, halves(h)]) for k in range(C)], (P, HALF),
                                 ("act", "dve")[h], write))
            matmul_jobs(chip, jobs, [(rows_dram, bc[:, :])])
        with ExitStack() as inner:
            ib = buffers(chip, inner)
            e, r, q, p = (ib(P, C, T) for _ in range(4))
            c0, c1, c2, c3, c4 = log1p_coefficients()
            with Stage(chip) as st:
                steps, e_ready = st.sems(2)
                block = st.block()

                @block.sync
                def _(sync):
                    st.clear_other_set(sync)

                @block.scalar
                def _(act):
                    for m in range(C):
                        act.activation(e[:, m, :], delta[:, m, :], ACT.Abs).then_inc(e_ready, 1)
                        act.wait_ge(e_ready, 2 * m + 1)
                        act.activation(e[:, m, :], e[:, m, :], ACT.Exp, scale=-1.0).then_inc(e_ready, 1)

                @block.vector
                def _(dve):
                    c = Chain(dve, steps)

                    def stt(out, in0, scalar, in1, op0, op1):
                        return dve.scalar_tensor_tensor(out=out, in0=in0, scalar=scalar, in1=in1, op0=op0, op1=op1)
                    for m in range(C):
                        dve.wait_ge(e_ready, 2 * m + 2)
                        em, rm, qm, pm, z = (t[:, m, :] for t in (e, r, q, p, delta))
                        c.link(dve.tensor_scalar(rm, em, 2.0, None, ALU.add))
                        c.link(dve.reciprocal(rm, rm))
                        c.link(dve.tensor_tensor(rm, rm, em, ALU.mult))
                        c.link(dve.tensor_tensor(qm, rm, rm, ALU.mult))
                        c.link(dve.tensor_scalar(pm, qm, c4, None, ALU.mult))
                        for k in (c3, c2, c1):
                            c.link(stt(pm, pm, k, qm, ALU.add, ALU.mult))
                        c.link(stt(pm, pm, c0, rm, ALU.add, ALU.mult))
                        c.link(stt(z, z, 0.0, pm, ALU.max, ALU.add))
                        dve.tensor_tensor(du[:, m, :], z, u[:, m, :], ALU.mult)

        ROUNDS = NS // 2
        with Stage(chip) as st:
            brow, crow = ([st.sbuf(P, T) for _ in range(2)] for _ in range(2))
            acur = [st.sbuf(P, C) for _ in range(2)]
            decay, drive, state, out = ([st.sbuf(P, T) for _ in range(2)] for _ in range(4))
            acc = [[st.psum(P, HALF) for _ in range(2)] for _ in range(C)]
            rows_in = st.sems(2)
            a_ready, exp_done, decay_ready, drive_ready, scanned, out_ready, summed, y_steps = st.sems(8)
            block = st.block()

            def rounds(eng):
                for i in peeled(eng, ROUNDS, 1, 1):
                    for x in range(2):
                        for c in range(C):
                            yield i, x, i * 2 + x, c, (i * 2 + x) * C + c

            @block.sync
            def _(sync):
                st.clear_other_set(sync)
                for i in peeled(sync, ROUNDS, 1, 1):
                    for x in range(2):
                        s = i * 2 + x
                        if later(s, 2):
                            sync.wait_ge(out_ready, s * C - C)
                        for dst, base in ((brow, 0), (crow, NS)):
                            sync.dma_start(dst[x][:, :], rows_dram[bass.ds(s + base, 1), :].broadcast_to([P, T])
                                           ).then_inc(rows_in[x], 16)

            @block.gpsimd
            def _(pool):
                for i, x, s, c, n in rounds(pool):
                    if c == 0:
                        if later(s, 2):
                            pool.wait_ge(exp_done, s * C - C)
                        pool.tensor_copy(acur[x][:, :], A[:, bass.ds(s, 1), :].rearrange("p o c -> p (o c)")
                                         ).then_inc(a_ready, 1)
                        pool.wait_ge(rows_in[x], i * 32 + 32)
                    pool.wait_ge(scanned, n + 1)
                    if later(n, 2):
                        pool.wait_ge(summed, n - 1)
                    pool.tensor_tensor(out[c % 2][:, :], state[c % 2][:, :], crow[x][:, :], ALU.mult
                                       ).then_inc(out_ready, 1)

            @block.scalar
            def _(act):
                for i, x, s, c, n in rounds(act):
                    if c == 0:
                        act.wait_ge(a_ready, s + 1)
                    if later(n, 2):
                        act.wait_ge(scanned, n - 1)
                    act.activation(decay[c % 2][:, :], delta[:, c, :], ACT.Exp, scale=acur[x][:, c:c + 1]
                                   ).then_inc(exp_done, 1)

            @block.vector
            def _(dve):
                for i, x, s, c, n in rounds(dve):
                    if c == 0:
                        dve.wait_ge(rows_in[x], i * 32 + 32)
                    if later(n, 2):
                        dve.wait_ge(scanned, n - 1)
                    dve.tensor_tensor(drive[c % 2][:, :], du[:, c, :], brow[x][:, :], ALU.mult).then_inc(drive_ready, 1)
                    dve.wait_ge(exp_done, n + 1)
                    dve.memset(decay[c % 2][:, :].rearrange("p (b s) -> p b s", s=S)[:, :, 0:1], 0.0
                               ).then_inc(decay_ready, 1)
                    dve.wait_ge(drive_ready, n + 1)
                    dve.wait_ge(decay_ready, n + 1)
                    if later(n, 2):
                        dve.wait_ge(out_ready, n - 1)
                    dve.tensor_tensor_scan(state[c % 2][:, :], decay[c % 2][:, :], drive[c % 2][:, :], 0.0,
                                           ALU.mult, ALU.add).then_inc(scanned, 1)
                dve.wait_ge(summed, NS * C)
                ch = Chain(dve, y_steps)
                for c in range(C):
                    for h in range(2):
                        t = u[:, c, halves(h)]
                        ch.link(dve.scalar_tensor_tensor(out=t, in0=t, scalar=Dp[:, c:c + 1], in1=acc[c][h][:, :],
                                                         op0=ALU.mult, op1=ALU.add))
                    dve.tensor_tensor(u[:, c, :], u[:, c, :], gate[:, c, :], ALU.mult)

            @block.tensor
            def _(pe):
                for i, x, s, c, n in rounds(pe):
                    pe.wait_ge(out_ready, n + 1)
                    first = isinstance(s, int) and s == 0
                    last = isinstance(s, int) and s == NS - 1
                    for h in range(2):
                        ins = pe.matmul(acc[c][h][:, :], ident[:, :], out[c % 2][:, halves(h)], start=first, stop=last)
                    ins.then_inc(summed, 1)

        with ExitStack() as inner:
            Wo = buffers(chip, inner)(P, C, D)
            jobs = []
            for j in range(NT):
                def write(eng, acc, j=j):
                    return eng.tensor_tensor(X[:, j, :], X[:, j, :], acc, ALU.add)
                jobs.append(([(u[:, k, tile(j)], Wo[:, k, :]) for k in range(C)], (P, D), "dve", write))
            matmul_jobs(chip, jobs, [(Wo[:, :, :], w["out_proj_w"])])


def turn_to_features(chip, pairs, ident):
    with Stage(chip) as st:
        banks = [st.psum(P, HALF) for _ in range(6)]
        turned, act_done, dve_done = st.sems(3)
        block = st.block()
        units = [(src, dst, c, h) for src, dst in pairs for c in range(DC) for h in range(2)]

        @block.sync
        def _(sync):
            st.clear_other_set(sync)

        @block.tensor
        def _(pe):
            for n, (src, dst, c, h) in enumerate(units):
                if n >= 6:
                    pe.wait_ge((act_done, dve_done)[n % 2], (n - 6) // 2 + 1)
                for q in range(4):
                    ins = pe.transpose(banks[n % 6][:, tile(q)], src[:, 4 * h + q, tile(c)], ident[:, :])
                ins.then_inc(turned, 1)

        @block.scalar
        def _(act):
            for n, (src, dst, c, h) in enumerate(units):
                if n % 2 == 0:
                    act.wait_ge(turned, n + 1)
                    act.copy(dst[:, c, halves(h)], banks[n % 6][:, :]).then_inc(act_done, 1)

        @block.vector
        def _(dve):
            for n, (src, dst, c, h) in enumerate(units):
                if n % 2 == 1:
                    dve.wait_ge(turned, n + 1)
                    dve.tensor_copy(dst[:, c, halves(h)], banks[n % 6][:, :]).then_inc(dve_done, 1)


def local_attention(chip, X, xn, xnT, ident, w):
    nc = chip.nc
    DH = 16
    N = D // DH // 2
    BL = 2
    ROUNDS = B // BL
    with ExitStack() as es:
        sb = buffers(chip, es)
        v = sb(S, B, D)
        qT, kT, Wp = sb(P, DC, T), sb(P, DC, T), sb(P, DC, D)
        pairs_mask, own, fold, causal = sb(P, N // DC, 2), sb(P, 2), sb(P, S), sb(P, S)
        with ExitStack() as inner:
            ib = buffers(chip, inner)
            W, lnw = ib(P, DC, 3 * D), ib(P, D)
            qk = [ib(P, NT, D) for _ in range(2)]
            sq = ib(P, NT, D)
            ms, std = ib(P, 2, NT), ib(P, 2, NT)
            jobs = []
            for n in range(2):
                for j in range(NT):
                    jobs.append(([(xnT[:, k, tile(j)], W[:, k, n * D:(n + 1) * D]) for k in range(DC)], (P, D),
                                 ("act", "dve")[n], copy_out(qk[n][:, j, :])))
            for b in range(B):
                jobs.append(([(xnT[:, k, b * S:(b + 1) * S], W[:, k, 2 * D:]) for k in range(DC)], (S, D),
                             ("act", "dve")[b % 2], copy_out(v[:, b, :])))
            matmul_jobs(chip, jobs, [(W[:, :, :], w["w_qkv"]), (Wp[:, :, :], w["w_proj"]),
                                     (lnw[:, :], w["ln_w"].partition_broadcast(P)),
                                     (pairs_mask[:, :, :], w["pairs_mask"]), (own[:, :], w["own"]),
                                     (fold[:, :], w["fold"]), (causal[:, :], w["causal"])])
            with Stage(chip) as st:
                steps, mean_ready, std_ready = st.sems(3)
                block = st.block()

                @block.sync
                def _(sync):
                    st.clear_other_set(sync)

                @block.vector
                def _(dve):
                    c = Chain(dve, steps)
                    for n in range(2):
                        c.link(dve.tensor_tensor(sq[:, :, :], qk[n][:, :, :], qk[n][:, :, :], ALU.mult))
                        c.link(dve.tensor_reduce(ms[:, n, :], sq[:, :, :], AX.X, ALU.add))
                    dve.tensor_scalar(ms[:, :, :], ms[:, :, :], 1.0 / D, 1e-6, ALU.mult, ALU.add).then_inc(mean_ready, 1)
                    dve.wait_ge(std_ready, 1)
                    c.link(dve.reciprocal(std[:, :, :], std[:, :, :]))
                    for n in range(2):
                        c.link(dve.tensor_tensor(qk[n][:, :, :], qk[n][:, :, :],
                                                 std[:, n, :].unsqueeze(2).broadcast_to([P, NT, D]), ALU.mult))
                        dve.tensor_tensor(qk[n][:, :, :], qk[n][:, :, :],
                                          lnw[:, :].unsqueeze(1).broadcast_to([P, NT, D]), ALU.mult)

                @block.scalar
                def _(act):
                    act.wait_ge(mean_ready, 1)
                    act.activation(std[:, :, :], ms[:, :, :], ACT.Sqrt).then_inc(std_ready, 1)
            turn_to_features(chip, ((qk[0], qT), (qk[1], kT)), ident)

        with Stage(chip) as st:
            a = [st.sbuf(P, N, 2, S) for _ in range(2)]
            sc = [st.sbuf(P, N, S) for _ in range(2)]
            probsT = [st.sbuf(S, N, P) for _ in range(2)]
            mx, total = ([st.sbuf(P, N) for _ in range(2)] for _ in range(2))
            side = st.sbuf(P, N, 2)
            mixed = [st.sbuf(P, N, 2, DH) for _ in range(2)]
            mT = st.sbuf(P, DC, P)
            acc_s = [st.psum(P, N, S) for _ in range(2)]
            acc_t = st.psum(S, N, P)
            acc_o, acc_f, acc_y = st.psum(P, HALF), st.psum(P, HALF), st.psum(P, HALF)
            (always, staged, scored, shifted, exp_done, turned, turned_copied, mixed_filled, mixed_ready, folded,
             folded_copied, y_filled, added, score_steps, norm_steps, side_steps) = st.sems(16)
            block = st.block()

            def steps(eng, body):
                for i in peeled(eng, ROUNDS, 3):
                    for x in range(BL):
                        body(i, x, i * BL + x)
                for x in range(2):
                    body(ROUNDS, x, B + x)

            def live(g, lag):
                return lag <= g < B + lag if isinstance(g, int) else True

            @block.sync
            def _(sync):
                st.clear_other_set(sync)

            @block.gpsimd
            def _(pool):
                for i in peeled(pool, ROUNDS, 3):
                    for x in range(BL):
                        n = i * BL + x
                        if later(n, 2):
                            pool.wait_ge(scored, n - 1)
                        for c in range(DC):
                            for s in range(2):
                                q = N // DC
                                pool.tensor_tensor(
                                    a[x][:, c * q:(c + 1) * q, s, :],
                                    qT[:, c:c + 1, bass.ds(n * S, S)].broadcast_to([P, q, S]),
                                    pairs_mask[:, :, s:s + 1].broadcast_to([P, q, S]), ALU.mult).then_inc(staged, 1)

            @block.tensor
            def _(pe):
                pe.wait_ge(always, 1)

                def body(i, x, g):
                    if live(g, 0):
                        pe.wait_ge(staged, g * 4 + 4)
                        if later(g, 2):
                            pe.wait_ge(shifted, g - 1)
                        for r in range(N):
                            ins = pe.matmul(acc_s[x % 2][:, r, :], a[x % 2][:, r, :, :],
                                            kT[:, r // 4, bass.ds(g * S, S)], start=True, stop=True)
                        ins.then_inc(scored, 1)
                    if live(g, 1):
                        pe.wait_ge(always, 1)
                        pe.wait_ge(exp_done, g)
                        if later(g, 2):
                            pe.wait_ge(turned_copied, g - 1)
                        for r in range(N):
                            ins = pe.transpose(acc_t[:, r, :], sc[(x + 1) % 2][:, r, :], ident[:, :])
                        ins.then_inc(turned, 1)
                    if live(g, 2):
                        pe.wait_ge(turned_copied, g - 1)
                        if later(g, 3):
                            pe.wait_ge(mixed_ready, g - 2)
                        at = bass.ds(g - 2, 1)
                        pe.wait_ge(always, 1)
                        for r in range(N):
                            ins = pe.matmul(acc_o[:, r * 2 * DH:(r + 1) * 2 * DH], probsT[x % 2][:, r, :],
                                            v[:, at, r * 2 * DH:(r + 1) * 2 * DH], start=True, stop=True)
                        ins.then_inc(mixed_filled, 1)
                        pe.wait_ge(mixed_ready, g - 1)
                        if later(g, 3):
                            pe.wait_ge(folded_copied, g - 2)
                        for c in range(DC):
                            ins = pe.matmul(acc_f[:, c * S:(c + 1) * S], mixed[x % 2][:, 4 * c:4 * c + 4, :, :],
                                            fold[:, :], start=True, stop=True)
                        ins.then_inc(folded, 1)
                        if x % 2 == 1:
                            pe.wait_ge(folded_copied, g - 1)
                            if later(g, 4):
                                pe.wait_ge(added, i - 1)
                            for c in range(DC):
                                ins = pe.matmul(acc_y[:, 0:D], mT[:, c, :], Wp[:, c, :], start=(c == 0),
                                                stop=(c == DC - 1))
                            ins.then_inc(y_filled, 1)
                steps(pe, body)

            @block.scalar
            def _(act):
                def body(i, x, g):
                    if live(g, 0):
                        act.wait_ge(shifted, g + 1)
                        act.activation(sc[x % 2][:, :, :], sc[x % 2][:, :, :], ACT.Exp).then_inc(exp_done, 1)
                    if live(g, 1):
                        act.wait_ge(turned, g)
                        if later(g, 3):
                            act.wait_ge(mixed_filled, g - 2)
                        act.copy(probsT[(x + 1) % 2][:, :, :], acc_t[:, :, :]).then_inc(turned_copied, 1)
                steps(act, body)

            @block.vector
            def _(dve):
                dve.memset(total[0][:, :], 0.0).then_inc(always, 1)

                def body(i, x, g):
                    if live(g, 0):
                        t, m = sc[x % 2], mx[x % 2]
                        c = Chain(dve, score_steps, g * 2)
                        dve.wait_ge(scored, g + 1)
                        if later(g, 2):
                            dve.wait_ge(turned, g - 1)
                        c.link(dve.scalar_tensor_tensor(out=t[:, :, :], in0=acc_s[x % 2][:, :, :], scalar=DH ** -0.5,
                                                        in1=causal[:, :].unsqueeze(1).broadcast_to([P, N, S]),
                                                        op0=ALU.mult, op1=ALU.add))
                        c.link(dve.tensor_reduce(m[:, :], t[:, :, :], AX.X, ALU.max))
                        dve.tensor_tensor(t[:, :, :], t[:, :, :], m[:, :].unsqueeze(2).broadcast_to([P, N, S]),
                                          ALU.subtract).then_inc(shifted, 1)
                    if live(g, 1):
                        y = (x + 1) % 2
                        c = Chain(dve, norm_steps, g * 2 - 2)
                        dve.wait_ge(exp_done, g)
                        c.link(dve.tensor_reduce(total[y][:, :], sc[y][:, :, :], AX.X, ALU.add))
                        c.link(dve.reciprocal(total[y][:, :], total[y][:, :]))
                    if live(g, 2):
                        y = x % 2
                        c = Chain(dve, side_steps, g - 2)
                        c.link(dve.tensor_tensor(side[:, :, :], total[y][:, :].unsqueeze(2).broadcast_to([P, N, 2]),
                                                 own[:, :].unsqueeze(1).broadcast_to([P, N, 2]), ALU.mult))
                        dve.wait_ge(mixed_filled, g - 1)
                        if later(g, 4):
                            dve.wait_ge(folded, g - 3)
                        dve.tensor_tensor(mixed[y][:, :, :, :].rearrange("p r s d -> p (r s) d"),
                                          acc_o[:, 0:D].rearrange("p (r d) -> p r d", d=DH),
                                          side[:, :, :].rearrange("p r s -> p (r s)").unsqueeze(2).broadcast_to(
                                              [P, 2 * N, DH]), ALU.mult).then_inc(mixed_ready, 1)
                        dve.wait_ge(folded, g - 1)
                        if y == 0 and later(g, 4):
                            dve.wait_ge(y_filled, i - 1)
                        dve.tensor_copy(mT[:, :, y * S:(y + 1) * S], acc_f[:, 0:DC * S].rearrange("p (c s) -> p c s", c=DC)
                                        ).then_inc(folded_copied, 1)
                        if y == 1:
                            at = bass.ds(i - 1, 1)
                            dve.wait_ge(y_filled, i)
                            dve.tensor_tensor(X[:, at, :].rearrange("p o d -> p (o d)"),
                                              X[:, at, :].rearrange("p o d -> p (o d)"), acc_y[:, 0:D], ALU.add
                                              ).then_inc(added, 1)
                steps(dve, body)


def program(nc, w, out, stages):
    chip = Chip(nc)
    with ExitStack() as es:
        X = es.enter_context(nc.sbuf_tensor("x_tokens", [P, NT, D], F32))
        xn = es.enter_context(nc.sbuf_tensor("xn_tokens", [P, NT, D], F32))
        xnT = es.enter_context(nc.sbuf_tensor("xn_features", [P, DC, T], F32))
        ident = es.enter_context(nc.sbuf_tensor("identity", [P, P], F32))
        with Stage(chip) as st:
            loaded = st.sem()
            block = st.block()

            @block.sync
            def _(sync):
                st.clear_other_set(sync)
                sync.dma_start(X[:, :, :], w["x"]).then_inc(loaded, 16)
                sync.dma_start(ident[:, :], w["identity"]).then_inc(loaded, 16)
                sync.wait_ge(loaded, 32)

        def sub(prefix):
            own = {k[len(prefix):]: v for k, v in w.items() if k.startswith(prefix)}
            return {**own, "ctx": w["ctx"], "ctxT": w["ctxT"]}

        for s in stages:
            layer_norm(chip, X, xnT, ident, keep=xn)
            LAYERS[s](chip, X, xn, xnT, ident, sub(s + "_"))

        with Stage(chip) as st:
            stored = nc.alloc_semaphore("x_stored")
            block = st.block()

            @block.sync
            def _(sync):
                st.clear_other_set(sync)
                sync.dma_start(out, X[:, :, :]).then_inc(stored, 16)
                sync.wait_ge(stored, 16)


LAYERS = {"L0_attn": local_attention, "L3_attn": selective_scan, "L1_xattn": sixteen_head_xattn, "L0_xattn": one_head_xattn, "L2_xattn": eight_head_xattn, "L3_xattn": eight_head_xattn, "L0_ffn": shared_and_routed, "L1_ffn": top1_experts, "L2_ffn": capacity_experts, "L2_attn": lru, "L3_ffn": binary_mlp, "L1_attn": conv_pool_mlp}
STAGES = ["L0_xattn", "L0_attn", "L0_ffn", "L1_xattn", "L1_attn", "L1_ffn", "L2_xattn", "L2_attn", "L2_ffn", "L3_xattn", "L3_attn", "L3_ffn"]


def layouts(inputs):
    import numpy as np
    a = {k: np.asarray(v) for k, v in inputs.items()}

    def kpn(m):
        return m.reshape(-1, P, m.shape[-1]).transpose(1, 0, 2)

    o = {"x": kpn(a["x"].reshape(T, D)), "identity": np.eye(P, dtype=np.float32)}
    for n in ("theta_log", "nu_log", "gamma_log"):
        o["L2_attn_" + n] = a["L2_attn_" + n].reshape(P, 1)
    for n in ("B_re", "B_im"):
        o["L2_attn_" + n] = kpn(a["L2_attn_" + n].T)
    for n in ("C_re", "C_im"):
        o["L2_attn_" + n] = a["L2_attn_" + n].T
    o["L2_attn_D"] = a["L2_attn_D"]
    for n in ("k0", "k1", "k2"):
        o["L3_ffn_" + n] = np.ascontiguousarray(kpn(a["L3_ffn_" + n])).view(np.int32)
    for n in ("s0", "s1", "s2"):
        o["L3_ffn_" + n] = a["L3_ffn_" + n].reshape(1)

    def cols(v):
        return v.reshape(-1, P).T

    p = "L1_attn_"
    o[p + "conv_w"] = a[p + "conv_w"].reshape(4, 64, 64, 4).transpose(0, 2, 3, 1)
    o[p + "conv_b"] = cols(a[p + "conv_b"])
    for n in ("conv", "attn", "boom"):
        for x in "gb":
            o[f"{p}ln_{n}_{x}"] = cols(a[f"{p}ln_{n}_{x}"])
    for x in "qkv":
        o[p + "W" + x] = kpn(a[p + "W" + x].T)
        o[p + "b" + x] = cols(a[p + "b" + x])
    o[p + "inv_len"] = (1.0 / np.arange(1, S + 1)).astype(np.float32)
    o[p + "Wb"], o[p + "Wu"] = kpn(a[p + "Wb"].T), kpn(a[p + "Wu"].T)
    o[p + "bb"], o[p + "bu"] = cols(a[p + "bb"]), a[p + "bu"].reshape(1, D)
    c = a["ctx_768"]
    o["ctx"], o["ctxT"] = c.reshape(B, KT, P, CC).transpose(0, 2, 1, 3), c.transpose(0, 2, 1)
    p = "L0_xattn_"
    o[p + "Wq"], o[p + "bq"] = kpn(a[p + "Wq"].T), cols(a[p + "bq"])
    o[p + "Wk"] = kpn(np.concatenate([a[p + "Wk"], a[p + "bk"].reshape(D, 1)], axis=1))
    o[p + "Wv"], o[p + "bv"] = a[p + "Wv"].T, a[p + "bv"].reshape(1, D)
    for p in ("L2_xattn_", "L3_xattn_"):
        o[p + "Wq"], o[p + "Wo"], o[p + "bo"] = kpn(a[p + "Wq"]), kpn(a[p + "Wo"]), a[p + "bo"].reshape(1, D)
        o[p + "WkT"], o[p + "WvT"] = kpn(a[p + "Wk"].T), kpn(a[p + "Wv"].T)
    p = "L1_xattn_"
    H1, DH = 16, 16
    o[p + "Wq"], o[p + "bq"] = kpn(a[p + "Wq"].T), cols(a[p + "bq"])
    wkv, bkv = a[p + "Wkv"].reshape(H1, 2, DH, CC), a[p + "bkv"].reshape(H1, 2, DH)
    o[p + "Wk"], o[p + "bk"] = wkv[:, 0].reshape(D, CC).T, cols(bkv[:, 0].reshape(D))
    o[p + "Wv"] = np.concatenate([wkv[:, 1].reshape(D, CC).T, bkv[:, 1].reshape(1, D)])
    o[p + "Wo"], o[p + "bo"] = kpn(a[p + "Wo"].T), a[p + "bo"].reshape(1, D)
    o[p + "pairs_mask"] = (np.arange(P)[:, None] // DH == np.arange(P // DH)[None]).astype(np.float32).reshape(P, 4, 2)
    o[p + "own"] = (np.arange(P)[:, None] // S == np.arange(2)[None]).astype(np.float32)
    o[p + "fold"] = np.concatenate([np.eye(S, dtype=np.float32)] * 2)
    q = "L0_attn_"
    for n in ("pairs_mask", "own", "fold"):
        o[q + n] = o[p + n]
    o[q + "causal"] = np.where(np.arange(S)[None] <= np.arange(P)[:, None] % S, 0.0, -1e30).astype(np.float32)
    o[q + "w_qkv"], o[q + "w_proj"], o[q + "ln_w"] = kpn(a[q + "w_qkv"]), kpn(a[q + "w_proj"]), a[q + "ln_w"]
    p = "L3_attn_"
    for n in ("in_proj_w", "x_proj_w", "dt_proj_w", "out_proj_w"):
        o[p + n] = kpn(a[p + n])
    for n in ("conv_b", "dt_proj_b", "D_param"):
        o[p + n] = cols(a[p + n])
    o[p + "conv_w"] = a[p + "conv_w"].reshape(4, P, 3).transpose(1, 0, 2)
    o[p + "A_log"] = a[p + "A_log"].reshape(4, P, 16).transpose(1, 2, 0)
    lower = np.tril(np.ones((E, E), np.float32), -1).reshape(E * E)

    def per_expert(m):
        return m.reshape(E, -1, P, m.shape[-1]).transpose(0, 2, 1, 3)

    p = "L0_ffn_"
    o[p + "lower"] = o["L1_ffn_lower"] = o["L2_ffn_lower"] = lower
    o[p + "gate_w"] = kpn(a[p + "gate_w"].T)
    o[p + "w1"], o[p + "w3"] = per_expert(a[p + "w1"]), per_expert(a[p + "w3"])
    whole = a[p + "w2"].shape[1] // P * P
    o[p + "w2"], o[p + "w2_tail"] = per_expert(a[p + "w2"][:, :whole]), a[p + "w2"][:, whole:]
    for n in ("sw1", "sw2", "sw3"):
        o[p + n] = kpn(a[p + n])
    p = "L1_ffn_"
    o[p + "router_W"], o[p + "router_b"] = kpn(a[p + "router_W"]), a[p + "router_b"].reshape(1, E)
    o[p + "W1"], o[p + "W2"] = per_expert(a[p + "W1"]), per_expert(a[p + "W2"])
    o[p + "b1"] = a[p + "b1"].reshape(E, -1, P).transpose(0, 2, 1)
    o[p + "b2"] = a[p + "b2"]
    p = "L2_ffn_"
    o[p + "Wg"], o[p + "bg"] = kpn(a[p + "Wg"]), a[p + "bg"].reshape(1, E)
    for n in ("W1", "W2", "W3"):
        o[p + n] = per_expert(a[p + n])
    o[p + "tri"] = np.triu(np.ones((P, P), np.float32))
    o[p + "iota"] = np.arange(1, int(T / E * 1.25) + 1, dtype=np.float32)
    return o


def kernel(**inputs):
    import numpy as np
    import concourse.bacc as bacc
    from concourse.bass_utils import run_bass_kernel_spmd as run

    nc = bacc.Bacc("TRN2", target_bir_lowering=False, num_devices=1)
    arrays, w = {}, {}
    for name, a in layouts(inputs).items():
        a = np.ascontiguousarray(a)
        arrays[f"in_{name}"] = a
        w[name] = nc.dram_tensor(f"in_{name}", a.shape, mybir.dt.from_np(a.dtype), kind="ExternalInput").ap()
    out = nc.dram_tensor("out_0", (P, NT, D), F32, kind="ExternalOutput").ap()
    program(nc, w, out, STAGES)
    r = run(nc, [arrays], core_ids=[0])
    got = np.asarray(r.results[0]["out_0"])
    return got.transpose(1, 0, 2).reshape(B, S, D)
```

```python
import concourse.bass as bass
from concourse import mybir
from contextlib import ExitStack

F32 = mybir.dt.float32
BF16 = mybir.dt.bfloat16
U8 = mybir.dt.uint8
I32 = mybir.dt.int32
ALU = mybir.AluOpType
ACT = mybir.ActivationFunctionType
AX = mybir.AxisListType

P = 128
B, S, D = 16, 64, 256
T = B * S
NT = T // P
DC = D // P
SK, CC = 1024, 192
C1 = CC - P
KT = SK // P
HALF = 512


class Chip:

    SEMS = 24

    def __init__(self, nc):
        self.nc = nc
        self.sets = [[nc.alloc_semaphore(f"stage_{s}_{n}") for n in range(self.SEMS)] for s in range(2)]
        self.stages = self.names = 0
        self.folded = nc.alloc_semaphore("residual_folded")


class Stage:

    def __init__(self, chip):
        self.chip, self.nc = chip, chip.nc
        self.mine = list(chip.sets[chip.stages % 2])
        self.other = chip.sets[(chip.stages + 1) % 2]
        self.first = chip.stages == 0
        chip.stages += 1
        self.stack = ExitStack()

    def __enter__(self):
        self.stack.__enter__()
        return self

    def __exit__(self, *e):
        return self.stack.__exit__(*e)

    def sbuf(self, *shape, dtype=F32):
        self.chip.names = n = self.chip.names + 1
        return self.stack.enter_context(self.nc.sbuf_tensor(f"buf{n}", list(shape), dtype))

    def psum(self, *shape):
        self.chip.names = n = self.chip.names + 1
        return self.stack.enter_context(self.nc.psum_tensor(f"acc{n}", list(shape), F32))

    def sems(self, n):
        return [self.mine.pop() for _ in range(n)]

    def sem(self):
        return self.mine.pop()

    def block(self):
        return self.stack.enter_context(self.nc.Block(no_gpsimd_drain=True))

    def clear_other_set(self, sync):
        if not self.first:
            nums = [s.num for s in self.other]
            assert max(nums) - min(nums) == len(nums) - 1
            sync.sem_clear(range(min(nums), max(nums) + 1))


class Chain:

    def __init__(self, eng, sem, base=0):
        self.eng, self.sem, self.base, self.n = eng, sem, base, 0

    def link(self, ins):
        self.n += 1
        ins.then_inc(self.sem, 1)
        self.eng.wait_ge(self.sem, self.base + self.n)


def rows(w):
    return w


def layer_norm(chip, src, dstT, ident, eps=1e-5, keep=None, gain=None):
    nc = chip.nc
    with Stage(chip) as st:
        stats = st.sbuf(P, NT, 6)
        mv = st.sbuf(P, NT, 2)
        std = st.sbuf(P, NT)
        rstd = st.sbuf(P, NT)
        xn = keep if keep is not None else st.sbuf(P, NT, D)
        turned = [[st.psum(P, HALF) for h in range(2)] for c in range(DC)]
        steps, var_ready, std_ready, xn_ready, turned_ready, gain_in = st.sems(6)
        if gain is not None:
            gb = st.sbuf(P, 2, DC)
        block = st.block()

        def dst(c, h):
            return dstT(c, h) if callable(dstT) else dstT[:, c, h * HALF:(h + 1) * HALF]

        @block.sync
        def _(sync):
            st.clear_other_set(sync)
            if gain is not None:
                for n in range(2):
                    sync.dma_start(gb[:, n, :], gain[n]).then_inc(gain_in, 16)

        @block.vector
        def _(dve):
            c = Chain(dve, steps)
            for j in range(NT):
                ins = dve.bn_stats(stats[:, j, :], src[:, j, :])
                if j == NT - 1:
                    c.link(ins)
            for j in range(NT):
                ins = dve.bn_aggr(mv[:, j, :], stats[:, j, :])
                if j == NT - 1:
                    c.link(ins)
            dve.tensor_scalar(rstd[:, :], mv[:, :, 1], eps, None, ALU.add).then_inc(var_ready, 1)
            dve.wait_ge(std_ready, 1)
            c.link(dve.reciprocal(rstd[:, :], std[:, :]))
            for j in range(NT):
                dve.tensor_scalar(xn[:, j, :], src[:, j, :], mv[:, j, 0:1], rstd[:, j:j + 1],
                                  ALU.subtract, ALU.mult).then_inc(xn_ready, 1)
            if gain is not None:
                dve.wait_ge(gain_in, 32)
            for h in range(2):
                dve.wait_ge(turned_ready, 4 * h + 4)
                if gain is None:
                    dve.tensor_copy(dst(1, h), turned[1][h][:, :])
                else:
                    dve.tensor_scalar(dst(1, h), turned[1][h][:, :] if not callable(dstT) else
                                      turned[1][h][:, :].rearrange("p (b s) -> p b s", s=S),
                                      gb[:, 0, 1:2], gb[:, 1, 1:2], ALU.mult, ALU.add)

        @block.scalar
        def _(act):
            act.wait_ge(var_ready, 1)
            act.activation(std[:, :], rstd[:, :], ACT.Sqrt).then_inc(std_ready, 1)
            if gain is not None:
                act.wait_ge(gain_in, 32)
            for h in range(2):
                act.wait_ge(turned_ready, 4 * h + 4)
                if gain is None:
                    act.copy(dst(0, h), turned[0][h][:, :])
                else:
                    act.activation(dst(0, h), turned[0][h][:, :] if not callable(dstT) else
                                   turned[0][h][:, :].rearrange("p (b s) -> p b s", s=S),
                                   ACT.Identity, bias=gb[:, 1, 0:1], scale=gb[:, 0, 0:1])

        @block.tensor
        def _(pe):
            for j in range(NT):
                pe.wait_ge(xn_ready, j + 1)
                for c in range(DC):
                    ins = pe.transpose(turned[c][j // 4][:, (j % 4) * P:(j % 4 + 1) * P],
                                       xn[:, j, c * P:(c + 1) * P], ident[:, :])
                ins.then_inc(turned_ready, 1)


def matmul_jobs(chip, jobs, loads, setup=None, nbanks=6):
    nc = chip.nc
    with Stage(chip) as st:
        banks = [st.psum(P, HALF) for _ in range(nbanks)]
        loaded, prepared, filled, act_done, dve_done, steps = st.sems(6)
        done = {"act": act_done, "dve": dve_done}
        turn, counts = [], {"act": 0, "dve": 0}
        for _, _, on, _ in jobs:
            counts[on] += 1
            turn.append(counts[on])
        block = st.block()

        @block.sync
        def _(sync):
            st.clear_other_set(sync)
            for dst, src in loads[0::2]:
                sync.dma_start(dst, src).then_inc(loaded, 16)

        @block.tensor
        def _(pe):
            if loads:
                pe.wait_ge(loaded, 16 * len(loads))
            if setup is not None:
                pe.wait_ge(prepared, 1)
            for n, (pairs, (r, w), on, write) in enumerate(jobs):
                if n >= nbanks:
                    before = jobs[n - nbanks][2]
                    pe.wait_ge(done[before], turn[n - nbanks])
                for k, (lhsT, rhs) in enumerate(pairs):
                    ins = pe.matmul(banks[n % nbanks][0:r, 0:w], lhsT, rhs, start=(k == 0),
                                    stop=(k == len(pairs) - 1))
                ins.then_inc(filled, 1)

        @block.scalar
        def _(act):
            for dst, src in loads[1::2]:
                act.dma_start(dst, src).then_inc(loaded, 16)
            if loads:
                act.wait_ge(loaded, 16 * len(loads))
            for n, (pairs, (r, w), on, write) in enumerate(jobs):
                if on == "act":
                    act.wait_ge(filled, n + 1)
                    write(act, banks[n % nbanks][0:r, 0:w]).then_inc(act_done, 1)

        @block.vector
        def _(dve):
            if loads:
                dve.wait_ge(loaded, 16 * len(loads))
            if setup is not None:
                chain = Chain(dve, steps)
                setup(dve, chain)
                chain.link(dve.engine_nop())
                dve.sem_inc(prepared, 1)
            for n, (pairs, (r, w), on, write) in enumerate(jobs):
                if on == "dve":
                    dve.wait_ge(filled, n + 1)
                    write(dve, banks[n % nbanks][0:r, 0:w]).then_inc(dve_done, 1)


def copy_out(dst):
    def write(eng, acc):
        return eng.copy(dst, acc) if is_scalar_engine(eng) else eng.tensor_copy(dst, acc)
    return write


def is_scalar_engine(eng):
    return eng.engine == mybir.EngineType.Activation


def halves(h):
    return slice(h * HALF, (h + 1) * HALF)


def lru(chip, X, xn, xnT, ident, w):
    nc = chip.nc
    HID = 128
    with ExitStack() as es:
        def sb(*shape):
            chip.names = n = chip.names + 1
            return es.enter_context(nc.sbuf_tensor(f"lru{n}", list(shape), F32))
        Bre, Bim = sb(P, DC, HID), sb(P, DC, HID)
        Cre, Cim, Drow = sb(P, D), sb(P, D), sb(P, D)
        par = sb(P, 3)
        re = [sb(P, T), sb(P, T)]
        im = [sb(P, T), sb(P, T)]
        g = sb(P, 1)
        lam = sb(P, 6, 3)
        tmp = sb(P, 8)
        big = sb(P, T)
        with Stage(chip) as st:
            loaded, dsteps, ready, back = st.sems(4)
            block = st.block()

            @block.sync
            def _(sync):
                st.clear_other_set(sync)
                for n, name in enumerate(("theta_log", "nu_log", "gamma_log")):
                    sync.dma_start(par[:, n:n + 1], w[name]).then_inc(loaded, 16)

            @block.scalar
            def _(act):
                act.wait_ge(loaded, 48)
                act.activation(tmp[:, 0:1], par[:, 0:1], ACT.Exp)
                act.activation(tmp[:, 1:2], par[:, 1:2], ACT.Exp).then_inc(ready, 1)
                act.wait_ge(ready, 1)
                act.activation(tmp[:, 2:3], tmp[:, 1:2], ACT.Exp, scale=-1.0)
                act.activation(g[:, :], par[:, 2:3], ACT.Exp).then_inc(ready, 1)
                act.wait_ge(back, 1)
                act.activation(tmp[:, 6:7], tmp[:, 4:5], ACT.Sin)
                act.activation(tmp[:, 7:8], tmp[:, 5:6], ACT.Sin).then_inc(ready, 1)

            @block.vector
            def _(dve):
                c = Chain(dve, dsteps)
                dve.wait_ge(ready, 2)
                c.link(dve.tensor_scalar(tmp[:, 3:4], tmp[:, 0:1], 0.15915494309189535, 12582912.0,
                                         ALU.mult, ALU.add))
                c.link(dve.tensor_scalar(tmp[:, 3:4], tmp[:, 3:4], -12582912.0, None, ALU.add))
                for part in (6.28125, 0.0019350051879882812, 3.0199e-07):
                    c.link(dve.scalar_tensor_tensor(out=tmp[:, 0:1], in0=tmp[:, 3:4], scalar=-part,
                                                    in1=tmp[:, 0:1], op0=ALU.mult, op1=ALU.add))
                c.link(dve.tensor_scalar(tmp[:, 4:5], tmp[:, 0:1], 3.1415925, -3.1415925, ALU.min, ALU.max))
                c.link(dve.tensor_scalar(tmp[:, 5:6], tmp[:, 4:5], -1.0, None, ALU.mult))
                c.link(dve.tensor_tensor(tmp[:, 5:6], tmp[:, 5:6], tmp[:, 4:5], ALU.min))
                dve.tensor_scalar(tmp[:, 5:6], tmp[:, 5:6], 1.5707963267948966, None,
                                  ALU.add).then_inc(back, 1)
                dve.wait_ge(ready, 3)
                c.link(dve.tensor_tensor(lam[:, 0, 0:1], tmp[:, 7:8], tmp[:, 2:3], ALU.mult))
                c.link(dve.tensor_tensor(lam[:, 0, 1:2], tmp[:, 6:7], tmp[:, 2:3], ALU.mult))
                for k in range(6):
                    a, b = lam[:, k, 0:1], lam[:, k, 1:2]
                    c.link(dve.tensor_scalar(lam[:, k, 2:3], b, -1.0, None, ALU.mult))
                    if k < 5:
                        a2, b2 = lam[:, k + 1, 0:1], lam[:, k + 1, 1:2]
                        c.link(dve.tensor_tensor(tmp[:, 6:7], b, b, ALU.mult))
                        c.link(dve.scalar_tensor_tensor(out=a2, in0=a, scalar=a, in1=tmp[:, 6:7],
                                                        op0=ALU.mult, op1=ALU.subtract))
                        c.link(dve.tensor_tensor(b2, a, b, ALU.mult))
                        c.link(dve.tensor_scalar(b2, b2, 2.0, None, ALU.mult))
        jobs = []
        for dst, wt in ((re[0], Bre), (im[0], Bim)):
            for h in range(2):
                def write(eng, acc, dst=dst, h=h):
                    return eng.activation(dst[:, halves(h)], acc, ACT.Copy, scale=g[:, 0:1])
                jobs.append(([(wt[:, k, :], xnT[:, k, halves(h)]) for k in range(DC)], (P, HALF), "act", write))
        matmul_jobs(chip, jobs, [(Bre[:], w["B_re"]), (Bim[:], w["B_im"])])
        with Stage(chip) as st:
            dsteps, loaded = st.sems(2)
            block = st.block()

            @block.sync
            def _(sync):
                st.clear_other_set(sync)
                sync.dma_start(Drow[:, :], w["D"].partition_broadcast(P)).then_inc(loaded, 16)
                sync.wait_ge(loaded, 16)

            @block.vector
            def _(dve):
                c = Chain(dve, dsteps)
                for k in range(6):
                    s = 1 << k
                    v = [[t[i][:, :].rearrange("p (b s) -> p b s", s=S) for i in (k % 2, 1 - k % 2)] for t in (re, im)]
                    a, b, nb = (lam[:, k, n:n + 1] for n in range(3))
                    (r0, r1), (i0, i1) = v
                    for (src, dst, other, coef) in ((r0, r1, i0, nb), (i0, i1, r0, b)):
                        dve.tensor_copy(dst[:, :, 0:s], src[:, :, 0:s])
                        c.link(dve.scalar_tensor_tensor(out=dst[:, :, s:S], in0=src[:, :, 0:S - s], scalar=a,
                                                        in1=src[:, :, s:S], op0=ALU.mult, op1=ALU.add))
                        c.link(dve.scalar_tensor_tensor(out=dst[:, :, s:S], in0=other[:, :, 0:S - s], scalar=coef,
                                                        in1=dst[:, :, s:S], op0=ALU.mult, op1=ALU.add))
                c.link(dve.tensor_scalar(im[1][:, :], im[0][:, :], -1.0, None, ALU.mult))
                for j in range(NT):
                    if j == 0:
                        dve.wait_ge(loaded, 16)
                    c.link(dve.tensor_tensor(big[:, 0:D], xn[:, j, :], Drow[:, :], ALU.mult))
                    c.link(dve.tensor_tensor(X[:, j, :], X[:, j, :], big[:, 0:D], ALU.add))
        jobs = []
        for j in range(NT):
            def write(eng, acc, j=j):
                return eng.tensor_tensor(X[:, j, :], X[:, j, :], acc, ALU.add)
            t = slice(j * P, (j + 1) * P)
            jobs.append(([(re[0][:, t], Cre[:, :]), (im[1][:, t], Cim[:, :])], (P, D), "dve", write))
        matmul_jobs(chip, jobs, [(Cre[:, :], w["C_re"]), (Cim[:, :], w["C_im"])])


def fill(chip, sets, loads):
    with Stage(chip) as st:
        cleared, loaded = st.sems(2)
        block = st.block()

        @block.vector
        def _(dve):
            for dst, value in sets:
                dve.memset(dst, value).then_inc(cleared, 1)
            dve.wait_ge(cleared, len(sets))

        @block.sync
        def _(sync):
            st.clear_other_set(sync)
            sync.wait_ge(cleared, len(sets))
            for dst, src in loads:
                sync.dma_start(dst, src).then_inc(loaded, 16)
            if loads:
                sync.wait_ge(loaded, 16 * len(loads))


def turn_to_tokens(chip, srcT, ident, write):
    with Stage(chip) as st:
        banks = [st.psum(P, HALF) for _ in range(4)]
        turned, written = st.sems(2)
        block = st.block()

        @block.sync
        def _(sync):
            st.clear_other_set(sync)

        @block.tensor
        def _(pe):
            for j in range(NT):
                if j >= 4:
                    pe.wait_ge(written, j - 3)
                for c in range(DC):
                    ins = pe.transpose(banks[j % 4][:, c * P:(c + 1) * P],
                                       srcT[:, c, j * P:(j + 1) * P], ident[:, :])
                ins.then_inc(turned, 1)

        @block.vector
        def _(dve):
            for j in range(NT):
                dve.wait_ge(turned, j + 1)
                write(dve, j, banks[j % 4][:, 0:D]).then_inc(written, 1)


def buffers(chip, es):
    def sb(*shape, dtype=F32):
        chip.names = n = chip.names + 1
        return es.enter_context(chip.nc.sbuf_tensor(f"buf{n}", list(shape), dtype))
    return sb


def tile(j):
    return slice(j * P, (j + 1) * P)


def binary_mlp(chip, X, xn, xnT, ident, w):
    F = 1024
    FC = F // P
    with ExitStack() as es:
        sb = buffers(chip, es)
        W0, W1, W2 = sb(P, DC, F), sb(P, FC, F), sb(P, FC, D)
        h1, h2 = sb(P, FC, T), sb(P, FC, T)
        sc = sb(P, 3)
        with ExitStack() as inner:
            ib = buffers(chip, inner)
            words = ib(P, 4, F // 4, dtype=I32), ib(P, FC, F // 4, dtype=I32), ib(P, FC, D // 4, dtype=I32)
            k0, k1, k2 = (b[:, :, :].bitcast(U8) for b in words)
            with Stage(chip) as st:
                loaded, steps, k2_done = st.sems(3)
                block = st.block()

                @block.sync
                def _(sync):
                    st.clear_other_set(sync)
                    for n in range(3):
                        sync.dma_start(words[n][:, :, :], w[f"k{n}"]).then_inc(loaded, 16)
                    for n in range(3):
                        sync.dma_start(sc[:, n:n + 1], w[f"s{n}"].partition_broadcast(P)).then_inc(loaded, 16)

                @block.scalar
                def _(act):
                    act.wait_ge(loaded, 96)
                    act.activation(W2[:, :, :], k2[:, :, :], ACT.Copy, scale=2.0, bias=-1.0)
                    act.activation(W1[:, 0:4, :], k1[:, 0:4, :], ACT.Copy, scale=2.0, bias=-1.0)

                @block.vector
                def _(dve):
                    dve.wait_ge(loaded, 96)
                    c = Chain(dve, steps)
                    c.link(dve.tensor_tensor(W0[:, :, :], k0[:, 0:2, :], k0[:, 2:4, :], ALU.subtract))
                    dve.tensor_scalar(W0[:, :, :], W0[:, :, :], 2.0, None, ALU.mult)
                    dve.tensor_scalar(W1[:, 4:8, :], k1[:, 4:8, :], 2.0, -1.0, ALU.mult, ALU.add)
                    c.link(dve.tensor_scalar(sc[:, 0:2], sc[:, 0:2], 2.0, None, ALU.mult))

        def relu_to(dst, n):
            def write(eng, acc):
                if is_scalar_engine(eng):
                    return eng.activation(dst, acc, ACT.Relu, scale=sc[:, n:n + 1])
                return eng.tensor_scalar(dst, acc, sc[:, n:n + 1], 0.0, ALU.mult, ALU.max)
            return write

        jobs = []
        for n, (wt, src, kc, dst) in enumerate(((W0, xnT, DC, h1), (W1, h1, FC, h2))):
            for h in range(2):
                for m in range(FC):
                    jobs.append(([(wt[:, k, tile(m)], src[:, k, halves(h)]) for k in range(kc)], (P, HALF),
                                 ("act", "dve")[m % 2], relu_to(dst[:, m, halves(h)], n)))
            matmul_jobs(chip, jobs, [])
            jobs = []
        for j in range(NT):
            def write(eng, acc, j=j):
                return eng.scalar_tensor_tensor(out=X[:, j, :], in0=acc, scalar=sc[:, 2:3], in1=X[:, j, :],
                                                op0=ALU.mult, op1=ALU.add)
            jobs.append(([(h2[:, k, tile(j)], W2[:, k, :]) for k in range(FC)], (P, D), "dve", write))
        matmul_jobs(chip, jobs, [])


def conv_pool_mlp(chip, X, xn, xnT, ident, w):
    K, F = 4, 1024
    FC = F // P
    PAD = K - 1
    with ExitStack() as es:
        sb = buffers(chip, es)
        H = sb(P, NT, D)
        aT = sb(P, DC, T)
        ones = sb(1, P)
        with ExitStack() as inner:
            ib = buffers(chip, inner)
            hp = ib(P, DC, B, S + PAD)
            cw, cb = ib(P, DC, K, P), ib(P, DC)
            fill(chip, [(cw[:, :, :, :], 0.0), (hp[:, :, :, 0:PAD], 0.0), (ones[:, :], 1.0)],
                 [(cw[(g % 2) * 64:(g % 2) * 64 + 64, g // 2, :, (g % 2) * 64:(g % 2) * 64 + 64], w["conv_w"][g])
                  for g in range(4)] + [(cb[:, :], w["conv_b"])])
            layer_norm(chip, xn, lambda c, h: hp[:, c, h * 8:h * 8 + 8, PAD:], ident,
                       gain=(w["ln_conv_g"], w["ln_conv_b"]))
            convT = ib(P, DC, T)
            jobs = []
            for c in range(DC):
                for h in range(2):
                    def write(eng, acc, c=c, h=h):
                        return eng.activation(convT[:, c, halves(h)], acc, ACT.Identity, bias=cb[:, c:c + 1])
                    jobs.append(([(cw[:, c, k, :], hp[:, c, 8 * h:8 * h + 8, k:k + S]) for k in range(K)],
                                 (P, HALF), "act", write))
            matmul_jobs(chip, jobs, [])
            turn_to_tokens(chip, convT, ident,
                           lambda dve, j, acc: dve.tensor_tensor(H[:, j, :], xn[:, j, :], acc, ALU.add))
        layer_norm(chip, H, aT, ident, gain=(w["ln_attn_g"], w["ln_attn_b"]))
        with ExitStack() as inner:
            ib = buffers(chip, inner)
            q, k, v = (ib(P, DC, T) for _ in range(3))
            W = ib(P, 3, DC, D)
            bqkv = ib(P, 3, DC)
            inv, keep = ib(P, S), ib(P, T)
            jobs = []
            for n, dst in enumerate((q, k, v)):
                for m in range(DC):
                    for h in range(2):
                        def write(eng, acc, dst=dst, n=n, m=m, h=h):
                            b = bqkv[:, n, m:m + 1]
                            if is_scalar_engine(eng):
                                return eng.activation(dst[:, m, halves(h)], acc, ACT.Identity, bias=b)
                            return eng.tensor_scalar(dst[:, m, halves(h)], acc, b, None, ALU.add)
                        jobs.append(([(W[:, n, c, tile(m)], aT[:, c, halves(h)]) for c in range(DC)], (P, HALF),
                                     ("act", "dve")[h], write))
            loads = [(W[:, n, :, :], w["W" + x]) for n, x in enumerate("qkv")]
            loads += [(bqkv[:, n, :], w["b" + x]) for n, x in enumerate("qkv")]
            loads += [(inv[:, :], w["inv_len"].partition_broadcast(P))]
            matmul_jobs(chip, jobs, loads)
            with Stage(chip) as st:
                steps = st.sem()
                block = st.block()

                @block.sync
                def _(sync):
                    st.clear_other_set(sync)

                @block.vector
                def _(dve):
                    c = Chain(dve, steps)
                    c.link(dve.memset(keep[:, :], 1.0))
                    c.link(dve.memset(keep[:, :].rearrange("p (b s) -> p b s", s=S)[:, :, 0:1], 0.0))

                    def by_length(t, m):
                        v3 = t[:, m, :].rearrange("p (b s) -> p b s", s=S)
                        c.link(dve.tensor_tensor(v3, v3, inv[:, :].unsqueeze(1).broadcast_to([P, B, S]), ALU.mult))

                    for m in range(DC):
                        c.link(dve.tensor_tensor_scan(q[:, m, :], keep[:, :], q[:, m, :], 0.0, ALU.mult, ALU.add))
                        by_length(q, m)
                        c.link(dve.tensor_tensor(k[:, m, :], q[:, m, :], k[:, m, :], ALU.mult))
                        c.link(dve.tensor_tensor_scan(q[:, m, :], keep[:, :], k[:, m, :], 0.0, ALU.mult, ALU.add))
                        by_length(q, m)
                        c.link(dve.tensor_tensor(v[:, m, :], q[:, m, :], v[:, m, :], ALU.mult))
            turn_to_tokens(chip, v, ident,
                           lambda dve, j, acc: dve.tensor_tensor(H[:, j, :], H[:, j, :], acc, ALU.add))
        layer_norm(chip, H, aT, ident, gain=(w["ln_boom_g"], w["ln_boom_b"]))
        Wb, Wu, g = sb(P, DC, F), sb(P, FC, D), sb(P, FC, T)
        bb, bu = sb(P, FC), sb(1, D)
        jobs = []
        for h in range(2):
            for m in range(FC):
                def write(eng, acc, m=m, h=h):
                    return eng.activation(g[:, m, halves(h)], acc, ACT.Gelu, bias=bb[:, m:m + 1])
                jobs.append(([(Wb[:, c, tile(m)], aT[:, c, halves(h)]) for c in range(DC)], (P, HALF), "act", write))
        matmul_jobs(chip, jobs, [(Wb[:, :, :], w["Wb"]), (Wu[:, :, :], w["Wu"]), (bb[:, :], w["bb"]), (bu[:, :], w["bu"])])
        jobs = []
        for j in range(NT):
            def write(eng, acc, j=j):
                eng.tensor_tensor(X[:, j, :], X[:, j, :], H[:, j, :], ALU.add).then_inc(chip.folded, 1)
                eng.wait_ge(chip.folded, j + 1)
                return eng.tensor_tensor(X[:, j, :], X[:, j, :], acc, ALU.add)
            jobs.append(([(g[:, k, tile(j)], Wu[:, k, :]) for k in range(FC)] + [(ones[:, :], bu[:, :])],
                         (P, D), "dve", write))
        matmul_jobs(chip, jobs, [])


E = 8


def peeled(eng, n, first=1, last=0):
    yield from range(first)
    if n - last > first:
        with eng.Fori(first, n - last) as i:
            yield i
    yield from range(n - last, n)


def later(step, least):
    return step >= least if isinstance(step, int) else True


def route(chip, xnT, gate, gate_bias, K, share, w, choice, chosen, loads):
    nc = chip.nc
    with ExitStack() as es:
        sb = buffers(chip, es)
        logits, ex = sb(P, NT, E), sb(P, NT, E)
        above, equal = sb(P, NT, E, E), sb(P, NT, E, E)
        lower, small = sb(P, E * E), sb(P, NT)
        ones = sb(1, P)
        if gate_bias is not None:
            fill(chip, [(ones[:, :], 1.0)], [])
        jobs = []
        for j in range(NT):
            def write(eng, acc, j=j):
                return eng.tensor_copy(logits[:, j, :], acc)
            pairs = [(xnT[:, k, tile(j)], gate[:, k, :]) for k in range(DC)]
            if gate_bias is not None:
                pairs.append((ones[:, :], gate_bias[:, :]))
            jobs.append((pairs, (P, E), "dve", write))
        matmul_jobs(chip, jobs, loads + [(lower[:, :], w["lower"].partition_broadcast(P))])
        with Stage(chip) as st:
            steps, shifted, exp_done = st.sems(3)
            block = st.block()

            @block.sync
            def _(sync):
                st.clear_other_set(sync)

            @block.scalar
            def _(act):
                act.wait_ge(shifted, 1)
                act.activation(ex[:, :, :], ex[:, :, :], ACT.Exp).then_inc(exp_done, 1)

            @block.vector
            def _(dve):
                c = Chain(dve, steps)
                L = logits[:, :, :]
                full = [P, NT, E, E]
                c.link(dve.tensor_reduce(small[:, :], L, AX.X, ALU.max))
                dve.tensor_tensor(ex[:, :, :], L, small[:, :].unsqueeze(2).broadcast_to([P, NT, E]),
                                  ALU.subtract).then_inc(shifted, 1)
                other = L.unsqueeze(2).broadcast_to(full)
                own = L.unsqueeze(3).broadcast_to(full)
                flat = "p j a b -> p j (a b)"
                c.link(dve.tensor_tensor(above[:, :, :, :], other, own, ALU.is_gt))
                c.link(dve.tensor_tensor(equal[:, :, :, :], other, own, ALU.is_equal))
                c.link(dve.tensor_tensor(equal[:, :, :, :].rearrange(flat), equal[:, :, :, :].rearrange(flat),
                                         lower[:, :].unsqueeze(1).broadcast_to([P, NT, E * E]), ALU.mult))
                c.link(dve.tensor_tensor(above[:, :, :, :].rearrange(flat), above[:, :, :, :].rearrange(flat),
                                         equal[:, :, :, :].rearrange(flat), ALU.add))
                c.link(dve.tensor_reduce(chosen[:, :, :], above[:, :, :, :], AX.X, ALU.add))
                c.link(dve.tensor_scalar(chosen[:, :, :], chosen[:, :, :], K - 0.5, None, ALU.is_lt))
                dve.wait_ge(exp_done, 1)
                c.link(dve.tensor_tensor(choice[:, :, :], ex[:, :, :], chosen[:, :, :], ALU.mult))
                c.link(dve.tensor_reduce(small[:, :], (ex if share == "all" else choice)[:, :, :], AX.X, ALU.add))
                c.link(dve.reciprocal(small[:, :], small[:, :]))
                c.link(dve.tensor_tensor(choice[:, :, :], choice[:, :, :],
                                         small[:, :].unsqueeze(2).broadcast_to([P, NT, E]), ALU.mult))


TILES = 26


def routed_experts(chip, X, xn, ident, choice, chosen, w, width, gated, loads_of, bias=False):
    nc = chip.nc
    M = -(-width // P)
    last = width - (M - 1) * P
    UP = 2 if gated else 1
    with ExitStack() as es:
        sb = buffers(chip, es)
        pos, picked = sb(P, NT, E), sb(P, NT, E)
        before = sb(P, NT + 1, E)
        count, tiles, base, grid = sb(P, E), sb(P, E), sb(P, E), sb(P, TILES * E)
        tri, ones, lower, iota = sb(P, P), sb(P, P), sb(P, E * E), sb(P, P)
        tile_rows, expert_no, tile_no, tile_expert = sb(P, TILES), sb(P, E), sb(P, TILES), sb(P, TILES)
        expert_int, rounds_int = sb(1, TILES, dtype=I32), sb(1, 1, dtype=I32)

        def prefixes(dve, chain):
            dve.memset(ones[:, :], 1.0)
            chain.link(dve.memset(before[:, 0, :], 0.0))
            for j in range(1, NT + 1):
                chain.link(dve.tensor_tensor(before[:, j, :], before[:, j - 1, :], chosen[:, j - 1, :], ALU.add))
        jobs = [([(ones[:, :], before[:, NT, :])], (P, E), "dve", copy_out(count[:, :]))]
        for j in range(NT):
            jobs.append(([(tri[:, :], chosen[:, j, :]), (ones[:, :], before[:, j, :])], (P, E), "dve",
                         copy_out(pos[:, j, :])))
        matmul_jobs(chip, jobs, [(tri[:, :], w["tri"])] + [
            (dst[:, :], w[n].partition_broadcast(P)) for dst, n in (
                (lower, "lower"), (iota, "iota_slot"), (tile_rows, "tile_rows"), (expert_no, "expert_no"),
                (tile_no, "tile_no"))], setup=prefixes)

        with Stage(chip) as st:
            steps = st.sem()
            block = st.block()

            @block.sync
            def _(sync):
                st.clear_other_set(sync)

            @block.vector
            def _(dve):
                c = Chain(dve, steps)
                square = [P, E, E]
                g = grid[:, 0:E * E].rearrange("p (a b) -> p a b", b=E)
                c.link(dve.tensor_tensor(g, count[:, :].unsqueeze(2).broadcast_to(square),
                                         tile_rows[:, 0:E].unsqueeze(1).broadcast_to(square), ALU.is_gt))
                c.link(dve.tensor_reduce(tiles[:, :], g, AX.X, ALU.add))
                c.link(dve.tensor_tensor(g, lower[:, :].rearrange("p (a b) -> p a b", b=E),
                                         tiles[:, :].unsqueeze(1).broadcast_to(square), ALU.mult))
                c.link(dve.tensor_reduce(base[:, :], g, AX.X, ALU.add))
                c.link(dve.tensor_tensor(tiles[:, :], tiles[:, :], base[:, :], ALU.add))
                c.link(dve.tensor_scalar(count[0:1, 0:1], tiles[0:1, E - 1:E], 0.5, 0.5, ALU.add, ALU.mult))
                c.link(dve.tensor_copy(rounds_int[:, :], count[0:1, 0:1]))
                g = grid[:, :].rearrange("p (a b) -> p a b", b=E)
                wide = [P, TILES, E]
                c.link(dve.tensor_tensor(g, tile_no[:, :].unsqueeze(2).broadcast_to(wide),
                                         tiles[:, :].unsqueeze(1).broadcast_to(wide), ALU.is_ge))
                c.link(dve.tensor_reduce(tile_expert[:, :], g, AX.X, ALU.add))
                c.link(dve.tensor_scalar(tile_expert[:, :], tile_expert[:, :], E - 1.0, None, ALU.min))
                c.link(dve.tensor_copy(expert_int[:, :], tile_expert[0:1, :]))
                c.link(dve.tensor_scalar(base[:, :], base[:, :], float(P), None, ALU.mult))
                c.link(dve.tensor_tensor(pos[:, :, :], pos[:, :, :], base[:, :].unsqueeze(1).broadcast_to([P, NT, E]),
                                         ALU.add))
                c.link(dve.tensor_tensor(pos[:, :, :], pos[:, :, :], chosen[:, :, :], ALU.mult))

        with Stage(chip) as st:
            Wup = [[st.sbuf(P, DC, width) for _ in range(UP)] for _ in range(2)]
            Wdn = [st.sbuf(P, M, D) for _ in range(2)]
            b_up, b_dn = [st.sbuf(P, M) for _ in range(2)], [st.sbuf(1, D) for _ in range(2)]
            hot = [st.sbuf(P, NT, P) for _ in range(2)]
            hotT = [st.sbuf(P, T) for _ in range(2)]
            own, cur = st.sbuf(P, E), st.sbuf(P, NT)
            scale = [st.sbuf(P, NT) for _ in range(2)]
            taken, given = st.sbuf(P, DC, P), [st.sbuf(P, D) for _ in range(2)]
            sil, hid = st.sbuf(P, M, P), st.sbuf(P, M, P)
            acc_take, acc_down = st.psum(P, DC, P), st.psum(P, D)
            acc_turn = [st.psum(P, HALF) for _ in range(2)]
            acc_up = [st.psum(P, UP, P) for _ in range(2)]
            acc_y = [st.psum(P, HALF) for _ in range(2)]
            weights_in = st.sems(2)
            (own_steps, hot_ready, take_filled, taken_ready, turned, turn_copied, up_filled, silu_done, hid_ready,
             down_filled, given_ready, y_filled, added) = st.sems(13)
            block = st.block()
            n_loads = UP + (1 if last == P else 2) + (2 if bias else 0)

            def size(m):
                return last if m == M - 1 else P

            def rounds_of(eng):
                return eng.value_load(rounds_int[0:1, 0:1], min_val=2, max_val=TILES // 2 - 1)

            def rounds(eng, count):
                yield 0
                with eng.Fori(1, count) as i:
                    yield i

            @block.sync
            def _(sync):
                st.clear_other_set(sync)
                for i in rounds(sync, rounds_of(sync)):
                    for x in range(2):
                        n = i * 2 + x
                        if later(n, 2):
                            sync.wait_ge(down_filled, n - 1)
                        e = sync.value_load(expert_int[0:1, bass.ds(n, 1)], min_val=0, max_val=E - 1)
                        k = 0
                        for dst, src in loads_of(x, e, Wup, Wdn, b_up, b_dn):
                            sync.dma_start(dst, src).then_inc(weights_in[x], 16)
                            k += 1
                        assert k == n_loads

            @block.tensor
            def _(pe):
                def give(n, x):
                    pe.wait_ge(given_ready, n + 1)
                    for j in range(NT):
                        if later(n * NT + j, 2):
                            pe.wait_ge(added, n * NT + j - 1)
                        pe.matmul(acc_y[j % 2][:, 0:D], hotT[x][:, tile(j)], given[x][:, :], start=True, stop=True
                                  ).then_inc(y_filled, 1)

                count = rounds_of(pe)
                for i in rounds(pe, count):
                    for x in range(2):
                        n = i * 2 + x
                        pe.wait_ge(hot_ready, n + 1)
                        if later(n, 1):
                            pe.wait_ge(taken_ready, n)
                        for c in range(DC):
                            for j in range(NT):
                                ins = pe.matmul(acc_take[:, c, :], xn[:, j, tile(c)], hot[x][:, j, :],
                                                start=(j == 0), stop=(j == NT - 1))
                        ins.then_inc(take_filled, 1)
                        for s in range(2):
                            if later(n, 1):
                                pe.wait_ge(turn_copied, n * 2 - 1 + s)
                            for q in range(4):
                                ins = pe.transpose(acc_turn[s][:, tile(q)], hot[x][:, s * 4 + q, :], ident[:, :])
                            ins.then_inc(turned, 1)
                        pe.wait_ge(weights_in[x], i * (16 * n_loads) + 16 * n_loads)
                        pe.wait_ge(taken_ready, n + 1)
                        for m in range(M):
                            if later(n * M + m, 2):
                                pe.wait_ge(hid_ready, n * M + m - 1)
                            for u in range(UP):
                                for k in range(DC):
                                    ins = pe.matmul(acc_up[m % 2][0:size(m), u, :], Wup[x][u][:, k, m * P:m * P + size(m)],
                                                    taken[:, k, :], start=(k == 0), stop=(k == DC - 1))
                            ins.then_inc(up_filled, 1)
                        if x == 1:
                            give(n - 1, 0)
                        pe.wait_ge(hid_ready, n * M + M)
                        if later(n, 1):
                            pe.wait_ge(given_ready, n)
                        for k in range(M):
                            ins = pe.matmul(acc_down[:, :], hid[0:size(k), k, :], Wdn[x][0:size(k), k, :],
                                            start=(k == 0), stop=(k == M - 1 and not bias))
                        if bias:
                            ins = pe.matmul(acc_down[:, :], ones[0:1, :], b_dn[x][:, :], start=False, stop=True)
                        ins.then_inc(down_filled, 1)
                        if x == 1:
                            give(n, 1)

            @block.scalar
            def _(act):
                for i in rounds(act, rounds_of(act)):
                    for x in range(2):
                        n = i * 2 + x
                        act.wait_ge(take_filled, n + 1)
                        if later(n, 1):
                            act.wait_ge(up_filled, n * M)
                        act.copy(taken[:, :, :], acc_take[:, :, :]).then_inc(taken_ready, 1)
                        for s in range(2):
                            act.wait_ge(turned, n * 2 + s + 1)
                            if s == 0 and later(n, 2):
                                act.wait_ge(y_filled, n * NT - NT)
                            act.copy(hotT[x][:, halves(s)], acc_turn[s][:, :]).then_inc(turn_copied, 1)
                        if bias:
                            act.wait_ge(weights_in[x], i * (16 * n_loads) + 16 * n_loads)
                        for m in range(M):
                            act.wait_ge(up_filled, n * M + m + 1)
                            if gated:
                                if m == 0 and later(n, 1):
                                    act.wait_ge(hid_ready, n * M)
                                act.activation(sil[0:size(m), m, :], acc_up[m % 2][0:size(m), 0, :], ACT.Silu
                                               ).then_inc(silu_done, 1)
                            else:
                                if m == 0 and later(n, 1):
                                    act.wait_ge(down_filled, n)
                                act.activation(hid[0:size(m), m, :], acc_up[m % 2][0:size(m), 0, :], ACT.Relu,
                                               bias=b_up[x][0:size(m), m:m + 1]).then_inc(hid_ready, 1)
                        act.wait_ge(down_filled, n + 1)
                        if later(n, 2):
                            act.wait_ge(y_filled, n * NT - NT)
                        act.copy(given[x][:, :], acc_down[:, :]).then_inc(given_ready, 1)

            @block.vector
            def _(dve):
                def prepare(n, x):
                    c = Chain(dve, own_steps, n * 6)
                    if later(n, 2):
                        dve.wait_ge(added, n * NT - NT)
                    at = bass.ds(n, 1)
                    c.link(dve.tensor_scalar(own[:, :], expert_no[:, :], tile_expert[:, at], None, ALU.is_equal))
                    mine = own[:, :].unsqueeze(1).broadcast_to([P, NT, E])
                    for src, dst in ((choice, scale[x]), (pos, cur)):
                        c.link(dve.tensor_tensor(picked[:, :, :], src[:, :, :], mine, ALU.mult))
                        c.link(dve.tensor_reduce(dst[:, :], picked[:, :, :], AX.X, ALU.add))
                    c.link(dve.tensor_scalar(cur[:, :], cur[:, :], tile_rows[:, at], None, ALU.subtract))
                    if later(n, 2):
                        dve.wait_ge(turned, n * 2 - 2)
                    dve.tensor_tensor(hot[x][:, :, :], iota[:, :].unsqueeze(1).broadcast_to([P, NT, P]),
                                      cur[:, :].unsqueeze(2).broadcast_to([P, NT, P]), ALU.is_equal
                                      ).then_inc(hot_ready, 1)
                    dve.wait_ge(hot_ready, n + 1)

                def add(n, x):
                    if later(n, 1):
                        dve.wait_ge(added, n * NT)
                    for j in range(NT):
                        dve.wait_ge(y_filled, n * NT + j + 1)
                        dve.scalar_tensor_tensor(out=X[:, j, :], in0=acc_y[j % 2][:, 0:D], scalar=scale[x][:, j:j + 1],
                                                 in1=X[:, j, :], op0=ALU.mult, op1=ALU.add).then_inc(added, 1)

                count = rounds_of(dve)
                prepare(0, 0)
                for i in rounds(dve, count):
                    for x in range(2):
                        n = i * 2 + x
                        if gated:
                            for m in range(M):
                                dve.wait_ge(silu_done, n * M + m + 1)
                                if m == 0 and later(n, 1):
                                    dve.wait_ge(down_filled, n)
                                dve.tensor_tensor(hid[0:size(m), m, :], sil[0:size(m), m, :],
                                                  acc_up[m % 2][0:size(m), 1, :], ALU.mult).then_inc(hid_ready, 1)
                        if x == 1:
                            add(n - 1, 0)
                        prepare(n + 1, 1 - x)
                        if x == 1:
                            add(n, 1)


def shared_and_routed(chip, X, xn, xnT, ident, w):
    HID, SH = 704, 384
    with ExitStack() as es:
        sb = buffers(chip, es)
        choice, chosen, gate = sb(P, NT, E), sb(P, NT, E), sb(P, DC, E)
        route(chip, xnT, gate, None, 2, "all", w, choice, chosen, [(gate[:, :, :], w["gate_w"])])
        FULL = HID // P

        def loads_of(x, e, Wup, Wdn, b_up, b_dn):
            one = bass.ds(e, 1)
            yield Wup[x][0][:, :, :], w["w1"][one].rearrange("o p k n -> p (o k) n")
            yield Wup[x][1][:, :, :], w["w3"][one].rearrange("o p k n -> p (o k) n")
            yield Wdn[x][:, 0:FULL, :], w["w2"][one].rearrange("o p k n -> p (o k) n")
            yield Wdn[x][0:HID - FULL * P, FULL, :], w["w2_tail"][one].rearrange("o p n -> (o p) n")
        routed_experts(chip, X, xn, ident, choice, chosen, w, HID, True, loads_of)
        MS = SH // P
        s1, s3, s2 = sb(P, DC, SH), sb(P, DC, SH), sb(P, MS, D)
        a, hid = sb(P, MS, T), sb(P, MS, T)
        jobs = []
        for h in range(2):
            for m in range(MS):
                def silu(eng, acc, m=m, h=h):
                    return eng.activation(a[:, m, halves(h)], acc, ACT.Silu)

                def copy(eng, acc, m=m, h=h):
                    return eng.tensor_copy(hid[:, m, halves(h)], acc)
                for wt, on, write in ((s1, "act", silu), (s3, "dve", copy)):
                    jobs.append(([(wt[:, k, tile(m)], xnT[:, k, halves(h)]) for k in range(DC)], (P, HALF), on, write))
        matmul_jobs(chip, jobs, [(s1[:, :, :], w["sw1"]), (s3[:, :, :], w["sw3"]), (s2[:, :, :], w["sw2"])])

        def gate_hidden(dve, chain):
            for m in range(MS):
                dve.tensor_tensor(hid[:, m, :], hid[:, m, :], a[:, m, :], ALU.mult)
        jobs = []
        for j in range(NT):
            def write(eng, acc, j=j):
                return eng.tensor_tensor(X[:, j, :], X[:, j, :], acc, ALU.add)
            jobs.append(([(hid[:, k, tile(j)], s2[:, k, :]) for k in range(MS)], (P, D), "dve", write))
        matmul_jobs(chip, jobs, [], setup=gate_hidden)


def top1_experts(chip, X, xn, xnT, ident, w):
    with ExitStack() as es:
        sb = buffers(chip, es)
        choice, chosen, gate, gb = sb(P, NT, E), sb(P, NT, E), sb(P, DC, E), sb(1, E)
        route(chip, xnT, gate, gb, 1, "all", w, choice, chosen,
              [(gate[:, :, :], w["router_W"]), (gb[:, :], w["router_b"])])

        def loads_of(x, e, Wup, Wdn, b_up, b_dn):
            one = bass.ds(e, 1)
            yield Wup[x][0][:, :, :], w["W1"][one].rearrange("o p k n -> p (o k) n")
            yield Wdn[x][:, :, :], w["W2"][one].rearrange("o p k n -> p (o k) n")
            yield b_up[x][:, :], w["b1"][one].rearrange("o p m -> p (o m)")
            yield b_dn[x][:, :], w["b2"][one]
        routed_experts(chip, X, xn, ident, choice, chosen, w, 1024, False, loads_of, bias=True)


def capacity_experts(chip, X, xn, xnT, ident, w):
    HID = 1024
    M = HID // P
    CAP = int(T / E * 1.25)
    HC = CAP // 2
    with ExitStack() as es:
        sb = buffers(chip, es)
        choice, chosen, gate, gb = sb(P, NT, E), sb(P, NT, E), sb(P, DC, E), sb(1, E)
        slot, before = sb(P, NT, E), sb(P, NT, E)
        tri, ones, iota = sb(P, P), sb(P, P), sb(P, CAP)
        route(chip, xnT, gate, gb, 2, "chosen", w, choice, chosen,
              [(gate[:, :, :], w["Wg"]), (gb[:, :], w["bg"])])

        def prefixes(dve, chain):
            dve.memset(ones[:, :], 1.0)
            chain.link(dve.memset(before[:, 0, :], 0.0))
            for j in range(1, NT):
                chain.link(dve.tensor_tensor(before[:, j, :], before[:, j - 1, :], chosen[:, j - 1, :], ALU.add))
        jobs = []
        for j in range(NT):
            def write(eng, acc, j=j):
                return eng.tensor_tensor(slot[:, j, :], acc, chosen[:, j, :], ALU.mult)
            jobs.append(([(tri[:, :], chosen[:, j, :]), (ones[:, :], before[:, j, :])], (P, E), "dve", write))
        matmul_jobs(chip, jobs, [(tri[:, :], w["tri"]), (iota[:, :], w["iota"].partition_broadcast(P))], setup=prefixes)

        with Stage(chip) as st:
            W1, W2 = ([st.sbuf(P, DC, HID) for _ in range(2)] for _ in range(2))
            W3 = [st.sbuf(P, M, D) for _ in range(2)]
            cur, scale = ([st.sbuf(P, NT) for _ in range(2)] for _ in range(2))
            hot = [st.sbuf(P, NT, CAP) for _ in range(2)]
            hotT = st.sbuf(HC, 2, T)
            taken = st.sbuf(P, DC, CAP)
            sil, hid = st.sbuf(P, M, CAP), st.sbuf(P, M, CAP)
            given = st.sbuf(HC, 2, D)
            acc_take, acc_out = st.psum(P, DC, HALF // 2), st.psum(HC, 2, D)
            acc_turn = [st.psum(P, HALF) for _ in range(2)]
            acc_up = [st.psum(P, 2, HALF // 2) for _ in range(2)]
            acc_y = [st.psum(P, HALF) for _ in range(2)]
            weights_in = st.sems(2)
            (cols_ready, cur_steps, hot_ready, take_filled, taken_ready, turned, turn_copied, up_filled, silu_done,
             hid_ready, out_filled, given_ready, y_filled, added) = st.sems(14)
            block = st.block()

            @block.sync
            def _(sync):
                st.clear_other_set(sync)
                for i in peeled(sync, E // 2):
                    for x in range(2):
                        e = i * 2 + x
                        if later(i, 1):
                            sync.wait_ge(out_filled, e - 1)
                        for dst, name in ((W1, "W1"), (W2, "W2"), (W3, "W3")):
                            sync.dma_start(dst[x][:, :, :], w[name][bass.ds(e, 1)].rearrange("o p k n -> p (o k) n")
                                           ).then_inc(weights_in[x], 16)

            @block.tensor
            def _(pe):
                for i in peeled(pe, E // 2):
                    for x in range(2):
                        e = i * 2 + x
                        pe.wait_ge(hot_ready, e + 1)
                        if later(e, 1):
                            pe.wait_ge(taken_ready, e)
                        for c in range(DC):
                            for j in range(NT):
                                ins = pe.matmul(acc_take[:, c, 0:CAP], xn[:, j, tile(c)], hot[x][:, j, :],
                                                start=(j == 0), stop=(j == NT - 1))
                        ins.then_inc(take_filled, 1)
                        for n in range(4):
                            if later(e * 4 + n, 2):
                                pe.wait_ge(turn_copied, e * 4 + n - 1)
                            for q in range(4):
                                s, j = n // 2, (n % 2) * 4 + q
                                ins = pe.transpose(acc_turn[n % 2][0:HC, q * P:(q + 1) * P],
                                                   hot[x][:, j, s * HC:(s + 1) * HC], ident[:, :])
                            ins.then_inc(turned, 1)
                        pe.wait_ge(weights_in[x], i * 48 + 48)
                        pe.wait_ge(taken_ready, e + 1)
                        for m in range(M):
                            if later(e * M + m, 2):
                                pe.wait_ge(hid_ready, e * M + m - 1)
                            for u, wt in enumerate((W1[x], W2[x])):
                                for k in range(DC):
                                    ins = pe.matmul(acc_up[m % 2][:, u, 0:CAP], wt[:, k, tile(m)], taken[:, k, :],
                                                    start=(k == 0), stop=(k == DC - 1))
                            ins.then_inc(up_filled, 1)
                        pe.wait_ge(hid_ready, e * M + M)
                        if later(e, 1):
                            pe.wait_ge(given_ready, e)
                        for s in range(2):
                            for k in range(M):
                                ins = pe.matmul(acc_out[:, s, :], hid[:, k, s * HC:(s + 1) * HC], W3[x][:, k, :],
                                                start=(k == 0), stop=(k == M - 1))
                        ins.then_inc(out_filled, 1)
                        pe.wait_ge(given_ready, e + 1)
                        pe.wait_ge(turn_copied, e * 4 + 4)
                        for j in range(NT):
                            if later(e * NT + j, 2):
                                pe.wait_ge(added, e * NT + j - 1)
                            for s in range(2):
                                ins = pe.matmul(acc_y[j % 2][:, 0:D], hotT[:, s, tile(j)], given[:, s, :],
                                                start=(s == 0), stop=(s == 1))
                            ins.then_inc(y_filled, 1)

            @block.scalar
            def _(act):
                for i in peeled(act, E // 2):
                    for x in range(2):
                        e = i * 2 + x
                        act.wait_ge(take_filled, e + 1)
                        if later(e, 1):
                            act.wait_ge(up_filled, e * M)
                        act.copy(taken[:, :, :], acc_take[:, :, 0:CAP]).then_inc(taken_ready, 1)
                        for n in range(4):
                            act.wait_ge(turned, e * 4 + n + 1)
                            if n == 0 and later(e, 1):
                                act.wait_ge(y_filled, e * NT)
                            act.copy(hotT[:, n // 2, halves(n % 2)], acc_turn[n % 2][0:HC, :]).then_inc(turn_copied, 1)
                        for m in range(M):
                            act.wait_ge(up_filled, e * M + m + 1)
                            if m == 0 and later(e, 1):
                                act.wait_ge(hid_ready, e * M)
                            act.activation(sil[:, m, :], acc_up[m % 2][:, 0, 0:CAP], ACT.Silu).then_inc(silu_done, 1)
                        act.wait_ge(out_filled, e + 1)
                        if later(e, 1):
                            act.wait_ge(y_filled, e * NT)
                        act.copy(given[:, :, :], acc_out[:, :, :]).then_inc(given_ready, 1)

            @block.vector
            def _(dve):
                def one_hot(e, x):
                    at = bass.ds(e, 1)
                    if later(e, 2):
                        dve.wait_ge(added, e * NT - NT)
                    dve.tensor_copy(cur[x][:, :], slot[:, :, at].rearrange("p j o -> p (j o)"))
                    dve.tensor_copy(scale[x][:, :], choice[:, :, at].rearrange("p j o -> p (j o)")
                                    ).then_inc(cols_ready, 1)
                    dve.wait_ge(cols_ready, e + 1)
                    if later(e, 2):
                        dve.wait_ge(turned, e * 4 - 4)
                    for j in range(NT):
                        ins = dve.tensor_scalar(hot[x][:, j, :], iota[:, :], cur[x][:, j:j + 1], None, ALU.is_equal)
                    ins.then_inc(hot_ready, 1)

                for i in peeled(dve, E // 2):
                    for x in range(2):
                        e = i * 2 + x
                        one_hot(e, x)
                        for m in range(M):
                            dve.wait_ge(silu_done, e * M + m + 1)
                            if m == 0 and later(e, 1):
                                dve.wait_ge(out_filled, e)
                            dve.tensor_tensor(hid[:, m, :], sil[:, m, :], acc_up[m % 2][:, 1, 0:CAP],
                                              ALU.mult).then_inc(hid_ready, 1)
                        if later(e, 1):
                            dve.wait_ge(added, e * NT)
                        for j in range(NT):
                            dve.wait_ge(y_filled, e * NT + j + 1)
                            dve.scalar_tensor_tensor(out=X[:, j, :], in0=acc_y[j % 2][:, 0:D],
                                                     scalar=scale[x][:, j:j + 1], in1=X[:, j, :],
                                                     op0=ALU.mult, op1=ALU.add).then_inc(added, 1)


def attend_context(chip, X, q0, q1, out0, out1, out_bias, ones, w, heads, ident):
    nc = chip.nc
    HT = min(heads, 2)
    R = HT * S
    N = heads // HT
    BL = 2 if N > 1 else 4
    U = BL * N
    PAIR = 2 * N
    ROUNDS, G = B // BL, B * N
    K1 = q1.shape[0]
    NB = 2 if N > 1 else 4
    with Stage(chip) as st:
        ctx = [st.sbuf(P, KT, CC) for _ in range(NB)]
        ct0, ct1 = [st.sbuf(P, SK) for _ in range(NB)], [st.sbuf(K1, SK) for _ in range(NB)]
        a0, a1 = [st.sbuf(P, heads, S) for _ in range(NB)], [st.sbuf(K1, heads, S) for _ in range(NB)]
        probs = [st.sbuf(R, SK) for _ in range(2)]
        probsT = [st.sbuf(P, KT, R) for _ in range(2)]
        mixed = [st.sbuf(R, CC) for _ in range(2)]
        m0, m1 = st.sbuf(P, heads, P), st.sbuf(C1, heads, P)
        negmax, total, inverse = st.sbuf(R, 4), st.sbuf(R, 4), st.sbuf(R, 4)
        acc_s = [st.psum(R, SK) for _ in range(2)]
        acc_t = st.psum(P, KT, R)
        acc_o = st.psum(R, HALF)
        acc_my = st.psum(P, HALF)
        acc_m0, acc_m1, acc_y = acc_my[:, 0:R], acc_my[0:C1, R:2 * R], acc_my[:, D:2 * D]
        ctx_in = st.sems(NB)
        (ones_ready, staged, scores_ready, max_ready, probs_ready, probs_turned, turned_copied, mixed_filled,
         inverse_ready, mixed_ready, mixed_turned, mixed_copied, y_filled, added) = st.sems(14)
        block = st.block()

        def steps(eng, body):
            for i in peeled(eng, ROUNDS, 2):
                for u in range(U):
                    body(i, u, i * U + u)
            for u in range(5):
                body(ROUNDS, u, G + u)

        def constant_wait(pe):
            if R < P:
                pe.wait_ge(ones_ready, NB)

        def live(g, lag):
            return lag <= g < G + lag if isinstance(g, int) else True

        @block.sync
        def _(sync):
            st.clear_other_set(sync)
            if K1 > C1:
                sync.wait_ge(ones_ready, NB)
            for i in peeled(sync, ROUNDS, 2):
                for b in range(BL):
                    x, n = b % NB, i * BL + b
                    if later(n, NB):
                        sync.wait_ge(mixed_filled, n * N - (NB - 1) * N)
                    one = bass.ds(n, 1)
                    sync.dma_start(ctx[x][:, :, :], w["ctx"][one].rearrange("o p k c -> p (o k) c")).then_inc(ctx_in[x], 16)
                    sync.dma_start(ct0[x][:, :], w["ctxT"][one, 0:P].rearrange("o p k -> p (o k)")).then_inc(ctx_in[x], 16)
                    sync.dma_start(ct1[x][0:C1, :], w["ctxT"][one, P:CC].rearrange("o p k -> p (o k)")
                                   ).then_inc(ctx_in[x], 16)

        @block.gpsimd
        def _(pool):
            for i in peeled(pool, ROUNDS, 2):
                for b in range(BL):
                    x, n = b % NB, i * BL + b
                    if later(n, NB):
                        pool.wait_ge(scores_ready, n * N - (NB - 1) * N)
                    pool.tensor_copy(a0[x][:, :, :], q0[:, :, bass.ds(n * S, S)]).then_inc(staged, 1)
                    pool.tensor_copy(a1[x][:, :, :], q1[:, :, bass.ds(n * S, S)]).then_inc(staged, 1)

        @block.tensor
        def _(pe):
            if K1 > C1:
                pe.wait_ge(ones_ready, NB)

            def body(i, u, g):
                ends = live(g, 4) and (u - 4) % PAIR == PAIR - 1
                p = i * (U // PAIR) + (u - 3 - PAIR) // PAIR
                if ends:
                    pe.wait_ge(mixed_copied, g - 3)
                    for h in range(heads):
                        pe.matmul(acc_y, m0[:, h, :], out0[:, h, :], start=(h == 0), stop=False)
                        pe.matmul(acc_y, m1[:, h, :], out1[:, h, :], start=False, stop=False)
                    pe.matmul(acc_y, ones[:, :], out_bias[:, :], start=False, stop=True).then_inc(y_filled, 1)
                if live(g, 0):
                    b, r = u // N, u % N
                    x = b % NB
                    if r == 0:
                        pe.wait_ge(staged, (i * BL + b) * 2 + 2)
                        pe.wait_ge(ctx_in[x], i * (48 * BL // NB) + (b // NB) * 48 + 48)
                    if later(g, 2):
                        pe.wait_ge(probs_ready, g - 1)
                    for h in range(2):
                        pe.matmul(acc_s[u % 2][:, halves(h)], a0[x][:, r * HT:(r + 1) * HT, :], ct0[x][:, halves(h)],
                                  start=True, stop=False)
                        ins = pe.matmul(acc_s[u % 2][:, halves(h)], a1[x][:, r * HT:(r + 1) * HT, :],
                                        ct1[x][:, halves(h)], start=False, stop=True)
                    ins.then_inc(scores_ready, 1)
                if live(g, 1):
                    constant_wait(pe)
                    pe.wait_ge(probs_ready, g)
                    if later(g, 2):
                        pe.wait_ge(turned_copied, g - 1)
                    for k in range(KT):
                        ins = pe.transpose(acc_t[:, k, :], probs[(u - 1) % 2][:, tile(k)], ident[0:R, 0:R])
                    ins.then_inc(probs_turned, 1)
                if ends:
                    pe.wait_ge(added, p + 1)
                if live(g, 3) and later(g, 4):
                    pe.wait_ge(mixed_copied, g - 3)
                if live(g, 2):
                    b = (u - 2) % U // N
                    pe.wait_ge(turned_copied, g - 1)
                    if later(g, 3):
                        pe.wait_ge(mixed_ready, g - 2)
                    for k in range(KT):
                        ins = pe.matmul(acc_o[:, 0:CC], probsT[u % 2][:, k, :], ctx[b % NB][:, k, :],
                                        start=(k == 0), stop=(k == KT - 1))
                    ins.then_inc(mixed_filled, 1)
                if live(g, 3):
                    constant_wait(pe)
                    pe.wait_ge(mixed_ready, g - 2)
                    pe.transpose(acc_m0, mixed[(u - 3) % 2][:, 0:P], ident[0:R, 0:R])
                    pe.transpose(acc_m1, mixed[(u - 3) % 2][:, P:CC], ident[0:R, 0:R]).then_inc(mixed_turned, 1)
            steps(pe, body)

        @block.scalar
        def _(act):
            def body(i, u, g):
                if live(g, 0):
                    act.wait_ge(max_ready, g + 1)
                    if later(g, 2):
                        act.wait_ge(probs_turned, g - 1)
                    if later(g, 4):
                        act.wait_ge(inverse_ready, g - 3)
                    act.activation(probs[u % 2][:, :], acc_s[u % 2][:, :], ACT.Exp, bias=negmax[:, u % 4:u % 4 + 1],
                                   accum_out=total[:, u % 4:u % 4 + 1]).then_inc(probs_ready, 1)
                if live(g, 3):
                    v = (u - 3) % U
                    h0, at = v % N * HT, (v // N) % 2 * S
                    act.wait_ge(mixed_turned, g - 2)
                    p = i * (U // PAIR) + (u - 3) // PAIR
                    if v % PAIR == 0 and later(p, 1):
                        act.wait_ge(y_filled, p)
                    act.copy(m0[:, h0:h0 + HT, at:at + S], acc_m0.rearrange("p (h s) -> p h s", s=S))
                    act.copy(m1[:, h0:h0 + HT, at:at + S], acc_m1.rearrange("p (h s) -> p h s", s=S)
                             ).then_inc(mixed_copied, 1)
            steps(act, body)

        @block.vector
        def _(dve):
            if K1 > C1:
                for x in range(NB):
                    dve.memset(ct1[x][C1:K1, :], 1.0).then_inc(ones_ready, 1)

            def body(i, u, g):
                if live(g, 0):
                    dve.wait_ge(scores_ready, g + 1)
                    dve.tensor_reduce(negmax[:, u % 4:u % 4 + 1], acc_s[u % 2][:, :], AX.X, ALU.max, negate=True
                                      ).then_inc(max_ready, 1)
                if live(g, 1):
                    dve.wait_ge(probs_turned, g)
                    if later(g, 3):
                        dve.wait_ge(mixed_filled, g - 2)
                    dve.tensor_copy(probsT[(u - 1) % 2][:, :, :], acc_t[:, :, :]).then_inc(turned_copied, 1)
                if live(g, 4) and (u - 4) % PAIR == PAIR - 1:
                    p = i * (U // PAIR) + (u - 3 - PAIR) // PAIR
                    at = bass.ds(p, 1)
                    dve.wait_ge(y_filled, p + 1)
                    dve.tensor_tensor(X[:, at, :].rearrange("p o d -> p (o d)"), X[:, at, :].rearrange("p o d -> p (o d)"),
                                      acc_y, ALU.add).then_inc(added, 1)
                if live(g, 2):
                    v = (u - 2) % 4
                    dve.wait_ge(probs_ready, g - 1)
                    dve.reciprocal(inverse[:, v:v + 1], total[:, v:v + 1]).then_inc(inverse_ready, 1)
                    dve.wait_ge(inverse_ready, g - 1)
                    dve.wait_ge(mixed_filled, g - 1)
                    if later(g, 4):
                        dve.wait_ge(mixed_turned, g - 3)
                    dve.tensor_scalar(mixed[u % 2][:, :], acc_o[:, 0:CC], inverse[:, v:v + 1], None, ALU.mult
                                      ).then_inc(mixed_ready, 1)
            steps(dve, body)


def one_head_xattn(chip, X, xn, xnT, ident, w):
    with ExitStack() as es:
        sb = buffers(chip, es)
        qT, q0, q1 = sb(P, DC, T), sb(P, 1, T), sb(C1 + 1, 1, T)
        Wq, Wk, bq = sb(P, DC, D), sb(P, DC, CC + 1), sb(P, DC)
        out0, out1, bv, ones = sb(P, 1, D), sb(C1, 1, D), sb(1, D), sb(1, P)
        fill(chip, [(ones[:, :], 1.0)], [])
        jobs = []
        for m in range(DC):
            for h in range(2):
                def write(eng, acc, m=m, h=h):
                    return eng.tensor_scalar(qT[:, m, halves(h)], acc, bq[:, m:m + 1], D ** -0.5, ALU.add, ALU.mult)
                jobs.append(([(Wq[:, k, tile(m)], xnT[:, k, halves(h)]) for k in range(DC)], (P, HALF), "dve", write))
        matmul_jobs(chip, jobs, [(Wq[:, :, :], w["Wq"]), (bq[:, :], w["bq"]), (Wk[:, :, :], w["Wk"]),
                                 (out0[:, 0, :], w["Wv"][0:P]), (out1[:, 0, :], w["Wv"][P:CC]),
                                 (bv[:, :], w["bv"])])
        jobs = []
        for h in range(2):
            for dst, c0, c1 in ((q0, 0, P), (q1, P, CC + 1)):
                jobs.append(([(Wk[:, k, c0:c1], qT[:, k, halves(h)]) for k in range(DC)], (c1 - c0, HALF),
                             ("act", "dve")[h], copy_out(dst[:, 0, halves(h)])))
        matmul_jobs(chip, jobs, [])
        attend_context(chip, X, q0, q1, out0, out1, bv, ones, w, 1, ident)


def eight_head_xattn(chip, X, xn, xnT, ident, w):
    HEADS, DH = 8, 64
    INNER = HEADS * DH
    MC = INNER // P
    with ExitStack() as es:
        sb = buffers(chip, es)
        q0, q1 = sb(P, HEADS, T), sb(C1, HEADS, T)
        out0, out1, bo, ones = sb(P, HEADS, D), sb(C1, HEADS, D), sb(1, D), sb(1, P)
        fill(chip, [(ones[:, :], 1.0)], [])
        with ExitStack() as inner:
            ib = buffers(chip, inner)
            qT, Wq = ib(P, MC, T), ib(P, DC, INNER)
            WkT, WvT, Wo = ib(P, MC, CC), ib(P, MC, CC), ib(P, MC, D)
            jobs = []
            for m in range(MC):
                for h in range(2):
                    def write(eng, acc, m=m, h=h):
                        dst = qT[:, m, halves(h)]
                        if is_scalar_engine(eng):
                            return eng.activation(dst, acc, ACT.Copy, scale=DH ** -0.5)
                        return eng.tensor_scalar(dst, acc, DH ** -0.5, None, ALU.mult)
                    jobs.append(([(Wq[:, k, tile(m)], xnT[:, k, halves(h)]) for k in range(DC)], (P, HALF),
                                 ("act", "dve")[h], write))
            matmul_jobs(chip, jobs, [(Wq[:, :, :], w["Wq"]), (WkT[:, :, :], w["WkT"]), (WvT[:, :, :], w["WvT"]),
                                     (Wo[:, :, :], w["Wo"]), (bo[:, :], w["bo"])])
            jobs = []
            for n in range(HEADS):
                at = slice((n % 2) * DH, (n % 2) * DH + DH)
                for t, (qd, od, c0, c1) in enumerate(((q0, out0, 0, P), (q1, out1, P, CC))):
                    for h in range(2):
                        jobs.append(([(WkT[at, n // 2, c0:c1], qT[at, n // 2, halves(h)])], (c1 - c0, HALF),
                                     ("act", "dve")[h], copy_out(qd[:, n, halves(h)])))
                    jobs.append(([(WvT[at, n // 2, c0:c1], Wo[at, n // 2, :])], (c1 - c0, D),
                                 ("act", "dve")[t], copy_out(od[:, n, :])))
            matmul_jobs(chip, jobs, [])
        attend_context(chip, X, q0, q1, out0, out1, bo, ones, w, HEADS, ident)


def sixteen_head_xattn(chip, X, xn, xnT, ident, w):
    nc = chip.nc
    HEADS, DH = 16, 16
    N = HEADS // 2
    G = B * N
    BL = 2
    U = BL * N
    R = N // DC
    RING = 2 * R
    LAST = R + 4
    ROUNDS = B // BL
    with ExitStack() as es:
        sb = buffers(chip, es)
        qT, Wq, bq = sb(P, DC, T), sb(P, DC, D), sb(P, DC)
        Wk0, Wk1, bk = sb(P, D), sb(C1, D), sb(P, DC)
        Wv0, Wv1 = sb(P, D), sb(C1 + 1, D)
        Wo, bo, ones = sb(P, DC, D), sb(1, D), sb(1, P)
        pairs_mask = sb(P, N // DC, 2)
        own = sb(P, 2 * DH)
        fill(chip, [(ones[:, :], 1.0)], [])
        jobs = []
        for m in range(DC):
            for h in range(2):
                def write(eng, acc, m=m, h=h):
                    return eng.tensor_scalar(qT[:, m, halves(h)], acc, bq[:, m:m + 1], DH ** -0.5, ALU.add, ALU.mult)
                jobs.append(([(Wq[:, k, tile(m)], xnT[:, k, halves(h)]) for k in range(DC)], (P, HALF), "dve", write))
        matmul_jobs(chip, jobs, [(Wq[:, :, :], w["Wq"]), (bq[:, :], w["bq"]), (Wk0[:, :], w["Wk"][0:P]),
                                 (Wk1[:, :], w["Wk"][P:CC]), (bk[:, :], w["bk"]), (Wv0[:, :], w["Wv"][0:P]),
                                 (Wv1[:, :], w["Wv"][P:CC + 1]), (Wo[:, :, :], w["Wo"]), (bo[:, :], w["bo"]),
                                 (pairs_mask[:, :, :], w["pairs_mask"]), (own[:, :], w["own_channels"])])
        with Stage(chip) as st:
            ct0, ct1 = [st.sbuf(P, SK) for _ in range(2)], [st.sbuf(C1 + 1, SK) for _ in range(2)]
            kT = [st.sbuf(P, DC, SK) for _ in range(2)]
            v = [st.sbuf(P, KT, D) for _ in range(2)]
            a = [st.sbuf(P, N, 2, S) for _ in range(2)]
            probs = [st.sbuf(P, SK) for _ in range(2)]
            probsT = st.sbuf(P, RING, KT, P)
            total, inverse = st.sbuf(P, RING), st.sbuf(P, R)
            spread = st.sbuf(P, P)
            scale, scaled = st.sbuf(P, P), st.sbuf(P, P)
            mT = st.sbuf(P, DC, P)
            negmax = st.sbuf(P, 2)
            acc_s = [st.psum(P, SK) for _ in range(2)]
            acc_t = [st.psum(P, HALF) for _ in range(2)]
            acc_kv = st.psum(P, HALF)
            acc_o = st.psum(P, HALF)
            acc_scale = acc_o[:, P:2 * P]
            acc_y = acc_t[1][:, 0:D]
            ctx_in = st.sems(2)
            (ones_ready, staged, scores_ready, max_ready, probs_ready, probs_turned, turned_copied, mixed_filled,
             inverse_ready, spread_ready, scale_ready, scaled_ready, mixed_ready, y_filled, added, kv_filled, kv_ready
             ) = st.sems(17)
            block = st.block()

            def steps(eng, body):
                for i in peeled(eng, ROUNDS, 2, 1):
                    for u in range(U):
                        body(i, u, i * U + u)
                for u in range(LAST - R + 2):
                    body(ROUNDS, u, G + u)

            def live(g, lag):
                return lag <= g < G + lag if isinstance(g, int) else True

            def group(i, u, lag):
                return i * (U // R) + (u - lag) // R

            def q_slot(u):
                return (u - R - 1) % RING // R * R

            def is_first(u, lag):
                return (u - lag) % R == 0

            @block.sync
            def _(sync):
                st.clear_other_set(sync)
                sync.wait_ge(ones_ready, 2)
                for i in peeled(sync, ROUNDS):
                    for x in range(BL):
                        n = i * BL + x
                        if later(n, 2):
                            sync.wait_ge(kv_filled, n * 8 - 8)
                        one = bass.ds(n, 1)
                        sync.dma_start(ct0[x][:, :], w["ctxT"][one, 0:P].rearrange("o p k -> p (o k)")
                                       ).then_inc(ctx_in[x], 16)
                        sync.dma_start(ct1[x][0:C1, :], w["ctxT"][one, P:CC].rearrange("o p k -> p (o k)")
                                       ).then_inc(ctx_in[x], 16)

            @block.gpsimd
            def _(pool):
                def stage(i, x):
                    n = i * BL + x
                    if later(n, 2):
                        pool.wait_ge(scores_ready, n * N - N)
                    for c in range(DC):
                        for s in range(2):
                            pool.tensor_tensor(
                                a[x][:, c * R:(c + 1) * R, s, :],
                                qT[:, c:c + 1, bass.ds(n * S, S)].broadcast_to([P, R, S]),
                                pairs_mask[:, :, s:s + 1].broadcast_to([P, R, S]), ALU.mult).then_inc(staged, 1)

                def body(i, u, g):
                    if u % N == 4 and (not isinstance(g, int) or g < G - N):
                        stage(i + (u // N + 1) // BL, 1 - u // N)
                    if is_first(u, R + 1) and live(g, R + 1):
                        q = group(i, u, R + 1)
                        if later(q, 1):
                            pool.wait_ge(mixed_filled, q)
                        pool.wait_ge(inverse_ready, q + 1)
                        pool.tensor_tensor(spread[:, :].rearrange("p (r d) -> p r d", r=R),
                                           inverse[:, :].unsqueeze(2).broadcast_to([P, R, 2 * DH]),
                                           own[:, :].unsqueeze(1).broadcast_to([P, R, 2 * DH]), ALU.mult
                                           ).then_inc(spread_ready, 1)
                stage(0, 0)
                steps(pool, body)

            def project(pe, x, t, done):
                if t < 4:
                    m, h = t // 2, t % 2
                    pe.matmul(acc_kv[:, :], Wk0[:, tile(m)], ct0[x][:, halves(h)], start=True, stop=False)
                    ins = pe.matmul(acc_kv[:, :], Wk1[:, tile(m)], ct1[x][0:C1, halves(h)], start=False, stop=True)
                else:
                    for s in range(2):
                        k = (t - 4) * 2 + s
                        pe.matmul(acc_kv[:, s * D:(s + 1) * D], ct0[x][:, tile(k)], Wv0[:, :], start=True, stop=False)
                        ins = pe.matmul(acc_kv[:, s * D:(s + 1) * D], ct1[x][:, tile(k)], Wv1[:, :],
                                        start=False, stop=True)
                ins.then_inc(kv_filled, 1)

            def project_out(act, x, t):
                if t < 4:
                    m, h = t // 2, t % 2
                    return act.activation(kT[x][:, m, halves(h)], acc_kv[:, :], ACT.Identity, bias=bk[:, m:m + 1])
                k = (t - 4) * 2
                return act.copy(v[x][:, k:k + 2, :], acc_kv[:, :].rearrange("p (k d) -> p k d", k=2))

            @block.tensor
            def _(pe):
                pe.wait_ge(ones_ready, 2)
                pe.wait_ge(ctx_in[0], 32)
                for t in range(8):
                    if t:
                        pe.wait_ge(kv_ready, t)
                    project(pe, 0, t, t)

                def body(i, u, g):
                    x, r = u // N, u % N
                    if live(g, 0):
                        if r == 0:
                            pe.wait_ge(staged, (i * BL + x) * 4 + 4)
                            pe.wait_ge(kv_ready, (i * BL + x) * 8 + 8)
                        if later(g, 2):
                            pe.wait_ge(probs_ready, g - 1)
                        for h in range(2):
                            ins = pe.matmul(acc_s[u % 2][:, halves(h)], a[x][:, r, :, :], kT[x][:, r // 4, halves(h)],
                                            start=True, stop=True)
                        ins.then_inc(scores_ready, 1)
                    if live(g, 1):
                        pe.wait_ge(probs_ready, g)
                        for s in range(2):
                            if later(g, 2):
                                pe.wait_ge(turned_copied, 2 * g - 3 + s)
                            if s == 1 and (u - LAST - 2) % U == U - R and later(g, U + LAST - R + 2):
                                pe.wait_ge(added, i + (u - LAST - 2 - (U - R)) // U + 1)
                            for k in range(4):
                                ins = pe.transpose(acc_t[s][:, tile(k)], probs[(u - 1) % 2][:, tile(4 * s + k)],
                                                   ident[:, :])
                            ins.then_inc(probs_turned, 1)
                    if live(g, R + 1):
                        j, q = (u - R - 1) % R, group(i, u, R + 1)
                        slot, xq = q_slot(u), (u - R - 1) % U // N
                        if j == 0:
                            pe.wait_ge(turned_copied, 2 * g - 2)
                            if later(q, 1):
                                pe.wait_ge(mixed_ready, q)
                        for k in range(2 * j, 2 * j + 2):
                            for t in range(R):
                                c0 = (u - R - 1) % N // R * P + t * 2 * DH
                                ins = pe.matmul(acc_o[t * 2 * DH:(t + 1) * 2 * DH, 0:P], v[xq][:, k, c0:c0 + 2 * DH],
                                                probsT[:, slot + t, k, :], start=(k == 0), stop=(k == KT - 1))
                        if j == R - 1:
                            pe.wait_ge(spread_ready, q + 1)
                            ins = pe.matmul(acc_scale, spread[:, :], ident[:, :], start=True, stop=True)
                            ins.then_inc(mixed_filled, 1)
                    if live(g, 0) and (not isinstance(g, int) or g < G - N):
                        if r == 0:
                            pe.wait_ge(ctx_in[1 - x], (i + (1 if x == 1 else 0)) * 32 + 32)
                        pe.wait_ge(kv_ready, g + 8)
                        project(pe, 1 - x, r, g)
                    if (u - LAST - 1) % U == U - R and live(g, LAST + 1 + U - R):
                        p = i + (u - LAST - 1 - (U - R)) // U
                        pe.wait_ge(mixed_ready, p * (U // R) + U // R)
                        if live(g, 1):
                            pe.wait_ge(turned_copied, 2 * g)
                        for c in range(DC):
                            pe.matmul(acc_y, mT[:, c, :], Wo[:, c, :], start=(c == 0), stop=False)
                        pe.matmul(acc_y, ones[:, :], bo[:, :], start=False, stop=True).then_inc(y_filled, 1)
                steps(pe, body)

            @block.scalar
            def _(act):
                for t in range(8):
                    act.wait_ge(kv_filled, t + 1)
                    project_out(act, 0, t).then_inc(kv_ready, 1)

                def body(i, u, g):
                    x, r = u // N, u % N
                    if live(g, 0):
                        act.wait_ge(max_ready, g + 1)
                        if later(g, 2):
                            act.wait_ge(probs_turned, 2 * g - 2)
                        if u % R == 0 and later(g, RING):
                            act.wait_ge(inverse_ready, group(i, u, RING) + 1)
                        act.activation(probs[u % 2][:, :], acc_s[u % 2][:, :], ACT.Exp,
                                       bias=negmax[:, u % 2:u % 2 + 1], accum_out=total[:, u % RING:u % RING + 1]
                                       ).then_inc(probs_ready, 1)
                    if live(g, 0) and (not isinstance(g, int) or g < G - N):
                        act.wait_ge(kv_filled, g + 9)
                        if later(g, N):
                            if r < 4:
                                act.wait_ge(scores_ready, i * U + x * N)
                            elif r == 4:
                                act.wait_ge(mixed_filled, (i * BL + x) * (N // R))
                        project_out(act, 1 - x, r).then_inc(kv_ready, 1)
                steps(act, body)

            @block.vector
            def _(dve):
                for x in range(2):
                    dve.memset(ct1[x][C1:C1 + 1, :], 1.0).then_inc(ones_ready, 1)

                def body(i, u, g):
                    if live(g, 0):
                        dve.wait_ge(scores_ready, g + 1)
                        if later(g, 2):
                            dve.wait_ge(probs_ready, g - 1)
                        dve.tensor_reduce(negmax[:, u % 2:u % 2 + 1], acc_s[u % 2][:, :], AX.X, ALU.max, negate=True
                                          ).then_inc(max_ready, 1)
                    if live(g, 1):
                        for s in range(2):
                            dve.wait_ge(probs_turned, 2 * g - 1 + s)
                            if is_first(u, 1) and later(g, RING + 1) and s == 0:
                                dve.wait_ge(mixed_filled, group(i, u, RING + 1) + 1)
                            dve.tensor_copy(probsT[:, (u - 1) % RING, 4 * s:4 * s + 4, :],
                                            acc_t[s][:, :].rearrange("p (k r) -> p k r", r=P)
                                            ).then_inc(turned_copied, 1)
                    if is_first(u, R + 1) and live(g, R + 1):
                        q = group(i, u, R + 1)
                        c = (u - R - 1) % RING
                        dve.wait_ge(probs_ready, q * R + R)
                        if later(q, 1):
                            dve.wait_ge(spread_ready, q)
                        dve.reciprocal(inverse[:, :], total[:, c:c + R]).then_inc(inverse_ready, 1)
                    if is_first(u, LAST) and live(g, LAST):
                        q = group(i, u, LAST)
                        c, xb = (u - LAST) % N // R, (u - LAST) % U // N
                        dve.wait_ge(mixed_filled, q + 1)
                        dve.tensor_copy(scale[:, :], acc_scale).then_inc(scale_ready, 1)
                        dve.wait_ge(scale_ready, q + 1)
                        dve.tensor_tensor(scaled[:, :], acc_o[:, 0:P], scale[:, :], ALU.mult).then_inc(scaled_ready, 1)
                        dve.wait_ge(scaled_ready, q + 1)
                        dve.tensor_tensor(mT[:, c, xb * S:(xb + 1) * S], scaled[:, 0:S], scaled[:, S:2 * S], ALU.add
                                          ).then_inc(mixed_ready, 1)
                    if (u - LAST - 1) % U == U - R and live(g, LAST + 1 + U - R):
                        p = i + (u - LAST - 1 - (U - R)) // U
                        at = bass.ds(p, 1)
                        dve.wait_ge(y_filled, p + 1)
                        dve.tensor_tensor(X[:, at, :].rearrange("p o d -> p (o d)"),
                                          X[:, at, :].rearrange("p o d -> p (o d)"), acc_y, ALU.add
                                          ).then_inc(added, 1)
                steps(dve, body)


def log1p_coefficients():
    import numpy as np
    n = 64
    q = (1 - np.cos((np.arange(n) + 0.5) * np.pi / n)) / 18
    r = np.sqrt(q)
    fit = np.polynomial.Polynomial.fit(q, 2 * np.arctanh(r) / r, 4, domain=[0, 1 / 9]).convert()
    return [float(c) for c in fit.coef]


def selective_scan(chip, X, xn, xnT, ident, w):
    nc = chip.nc
    CH, NS = 512, 16
    C = CH // P
    with ExitStack() as es:
        sb = buffers(chip, es)
        u, gate, delta, du = (sb(P, C, T) for _ in range(4))
        A, Dp, cw, cb, dtb = sb(P, NS, C), sb(P, C), sb(P, C, 3), sb(P, C), sb(P, C)
        rows_dram = nc.dram_tensor("state_rows", [2 * NS, T], F32, kind="Internal").ap()

        with ExitStack() as inner:
            ib = buffers(chip, inner)
            up, Win = ib(P, C, B, S + 2), ib(P, DC, 2 * CH)
            fill(chip, [(up[:, :, :, 0:1], 0.0), (up[:, :, :, S + 1:S + 2], 0.0)], [])
            jobs = []
            for m in range(2 * C):
                for h in range(2):
                    def write(eng, acc, m=m, h=h):
                        if m < C:
                            return eng.tensor_copy(up[:, m, 8 * h:8 * h + 8, 1:S + 1],
                                                   acc.rearrange("p (b s) -> p b s", s=S))
                        return eng.activation(gate[:, m - C, halves(h)], acc, ACT.Silu)
                    jobs.append(([(Win[:, k, tile(m)], xnT[:, k, halves(h)]) for k in range(DC)], (P, HALF),
                                 "dve" if m < C else "act", write))
            matmul_jobs(chip, jobs, [(Win[:, :, :], w["in_proj_w"]), (cw[:, :, :], w["conv_w"]), (cb[:, :], w["conv_b"]),
                                     (Dp[:, :], w["D_param"]), (dtb[:, :], w["dt_proj_b"]), (A[:, :, :], w["A_log"])])
            with Stage(chip) as st:
                steps, conv_done, a_ready = st.sems(3)
                block = st.block()

                @block.sync
                def _(sync):
                    st.clear_other_set(sync)

                @block.vector
                def _(dve):
                    c = Chain(dve, steps)
                    for m in range(C):
                        t = delta[:, m, :].rearrange("p (b s) -> p b s", s=S)
                        c.link(dve.tensor_scalar(t, up[:, m, :, 0:S], cw[:, m, 0:1], cb[:, m:m + 1], ALU.mult, ALU.add))
                        for k in (1, 2):
                            ins = dve.scalar_tensor_tensor(out=t, in0=up[:, m, :, k:k + S], scalar=cw[:, m, k:k + 1],
                                                           in1=t, op0=ALU.mult, op1=ALU.add)
                            if k == 1:
                                c.link(ins)
                        ins.then_inc(conv_done, 1)
                    dve.wait_ge(a_ready, 1)
                    dve.tensor_scalar(A[:, :, :], A[:, :, :], -1.0, None, ALU.mult)

                @block.scalar
                def _(act):
                    act.activation(A[:, :, :], A[:, :, :], ACT.Exp).then_inc(a_ready, 1)
                    for m in range(C):
                        act.wait_ge(conv_done, m + 1)
                        act.activation(u[:, m, :], delta[:, m, :], ACT.Silu)

        with ExitStack() as inner:
            ib = buffers(chip, inner)
            low, Wx, Wdt, bc = ib(P, C, T), ib(P, C, CH + 2 * NS), ib(P, C, CH), ib(2 * NS, T)
            jobs = []
            for h in range(2):
                for m in range(C + 1):
                    r = P if m < C else 2 * NS
                    dst = low[:, m, halves(h)] if m < C else bc[:, halves(h)]
                    jobs.append(([(Wx[:, k, m * P:m * P + r], u[:, k, halves(h)]) for k in range(C)], (r, HALF),
                                 ("act", "dve")[m % 2], copy_out(dst)))
            matmul_jobs(chip, jobs, [(Wx[:, :, :], w["x_proj_w"]), (Wdt[:, :, :], w["dt_proj_w"])])
            jobs = []
            for m in range(C):
                for h in range(2):
                    def write(eng, acc, m=m, h=h):
                        b = dtb[:, m:m + 1]
                        if is_scalar_engine(eng):
                            return eng.activation(delta[:, m, halves(h)], acc, ACT.Identity, bias=b)
                        return eng.tensor_scalar(delta[:, m, halves(h)], acc, b, None, ALU.add)
                    jobs.append(([(Wdt[:, k, tile(m)], low[:, k, halves(h)]) for k in range(C)], (P, HALF),
                                 ("act", "dve")[h], write))
            matmul_jobs(chip, jobs, [(rows_dram, bc[:, :])])
        with ExitStack() as inner:
            ib = buffers(chip, inner)
            e, r, q, p = (ib(P, C, T) for _ in range(4))
            c0, c1, c2, c3, c4 = log1p_coefficients()
            with Stage(chip) as st:
                steps, e_ready = st.sems(2)
                block = st.block()

                @block.sync
                def _(sync):
                    st.clear_other_set(sync)

                @block.scalar
                def _(act):
                    for m in range(C):
                        act.activation(e[:, m, :], delta[:, m, :], ACT.Abs).then_inc(e_ready, 1)
                        act.wait_ge(e_ready, 2 * m + 1)
                        act.activation(e[:, m, :], e[:, m, :], ACT.Exp, scale=-1.0).then_inc(e_ready, 1)

                @block.vector
                def _(dve):
                    c = Chain(dve, steps)

                    def stt(out, in0, scalar, in1, op0, op1):
                        return dve.scalar_tensor_tensor(out=out, in0=in0, scalar=scalar, in1=in1, op0=op0, op1=op1)
                    for m in range(C):
                        dve.wait_ge(e_ready, 2 * m + 2)
                        em, rm, qm, pm, z = (t[:, m, :] for t in (e, r, q, p, delta))
                        c.link(dve.tensor_scalar(rm, em, 2.0, None, ALU.add))
                        c.link(dve.reciprocal(rm, rm))
                        c.link(dve.tensor_tensor(rm, rm, em, ALU.mult))
                        c.link(dve.tensor_tensor(qm, rm, rm, ALU.mult))
                        c.link(dve.tensor_scalar(pm, qm, c4, None, ALU.mult))
                        for k in (c3, c2, c1):
                            c.link(stt(pm, pm, k, qm, ALU.add, ALU.mult))
                        c.link(stt(pm, pm, c0, rm, ALU.add, ALU.mult))
                        c.link(stt(z, z, 0.0, pm, ALU.max, ALU.add))
                        dve.tensor_tensor(du[:, m, :], z, u[:, m, :], ALU.mult)

        ROUNDS = NS // 2
        with Stage(chip) as st:
            brow, crow = ([st.sbuf(P, T) for _ in range(2)] for _ in range(2))
            acur = [st.sbuf(P, C) for _ in range(2)]
            decay, drive, state, out = ([st.sbuf(P, T) for _ in range(2)] for _ in range(4))
            acc = [[st.psum(P, HALF) for _ in range(2)] for _ in range(C)]
            rows_in = st.sems(2)
            a_ready, exp_done, decay_ready, drive_ready, scanned, out_ready, summed, y_steps = st.sems(8)
            block = st.block()

            def rounds(eng):
                for i in peeled(eng, ROUNDS, 1, 1):
                    for x in range(2):
                        for c in range(C):
                            yield i, x, i * 2 + x, c, (i * 2 + x) * C + c

            @block.sync
            def _(sync):
                st.clear_other_set(sync)
                for i in peeled(sync, ROUNDS, 1, 1):
                    for x in range(2):
                        s = i * 2 + x
                        if later(s, 2):
                            sync.wait_ge(out_ready, s * C - C)
                        for dst, base in ((brow, 0), (crow, NS)):
                            sync.dma_start(dst[x][:, :], rows_dram[bass.ds(s + base, 1), :].broadcast_to([P, T])
                                           ).then_inc(rows_in[x], 16)

            @block.gpsimd
            def _(pool):
                for i, x, s, c, n in rounds(pool):
                    if c == 0:
                        if later(s, 2):
                            pool.wait_ge(exp_done, s * C - C)
                        pool.tensor_copy(acur[x][:, :], A[:, bass.ds(s, 1), :].rearrange("p o c -> p (o c)")
                                         ).then_inc(a_ready, 1)
                        pool.wait_ge(rows_in[x], i * 32 + 32)
                    pool.wait_ge(scanned, n + 1)
                    if later(n, 2):
                        pool.wait_ge(summed, n - 1)
                    pool.tensor_tensor(out[c % 2][:, :], state[c % 2][:, :], crow[x][:, :], ALU.mult
                                       ).then_inc(out_ready, 1)

            @block.scalar
            def _(act):
                for i, x, s, c, n in rounds(act):
                    if c == 0:
                        act.wait_ge(a_ready, s + 1)
                    if later(n, 2):
                        act.wait_ge(scanned, n - 1)
                    act.activation(decay[c % 2][:, :], delta[:, c, :], ACT.Exp, scale=acur[x][:, c:c + 1]
                                   ).then_inc(exp_done, 1)

            @block.vector
            def _(dve):
                for i, x, s, c, n in rounds(dve):
                    if c == 0:
                        dve.wait_ge(rows_in[x], i * 32 + 32)
                    if later(n, 2):
                        dve.wait_ge(scanned, n - 1)
                    dve.tensor_tensor(drive[c % 2][:, :], du[:, c, :], brow[x][:, :], ALU.mult).then_inc(drive_ready, 1)
                    dve.wait_ge(exp_done, n + 1)
                    dve.memset(decay[c % 2][:, :].rearrange("p (b s) -> p b s", s=S)[:, :, 0:1], 0.0
                               ).then_inc(decay_ready, 1)
                    dve.wait_ge(drive_ready, n + 1)
                    dve.wait_ge(decay_ready, n + 1)
                    if later(n, 2):
                        dve.wait_ge(out_ready, n - 1)
                    dve.tensor_tensor_scan(state[c % 2][:, :], decay[c % 2][:, :], drive[c % 2][:, :], 0.0,
                                           ALU.mult, ALU.add).then_inc(scanned, 1)
                dve.wait_ge(summed, NS * C)
                ch = Chain(dve, y_steps)
                for c in range(C):
                    for h in range(2):
                        t = u[:, c, halves(h)]
                        ch.link(dve.scalar_tensor_tensor(out=t, in0=t, scalar=Dp[:, c:c + 1], in1=acc[c][h][:, :],
                                                         op0=ALU.mult, op1=ALU.add))
                    dve.tensor_tensor(u[:, c, :], u[:, c, :], gate[:, c, :], ALU.mult)

            @block.tensor
            def _(pe):
                for i, x, s, c, n in rounds(pe):
                    pe.wait_ge(out_ready, n + 1)
                    first = isinstance(s, int) and s == 0
                    last = isinstance(s, int) and s == NS - 1
                    for h in range(2):
                        ins = pe.matmul(acc[c][h][:, :], ident[:, :], out[c % 2][:, halves(h)], start=first, stop=last)
                    ins.then_inc(summed, 1)

        with ExitStack() as inner:
            Wo = buffers(chip, inner)(P, C, D)
            jobs = []
            for j in range(NT):
                def write(eng, acc, j=j):
                    return eng.tensor_tensor(X[:, j, :], X[:, j, :], acc, ALU.add)
                jobs.append(([(u[:, k, tile(j)], Wo[:, k, :]) for k in range(C)], (P, D), "dve", write))
            matmul_jobs(chip, jobs, [(Wo[:, :, :], w["out_proj_w"])])


def turn_to_features(chip, pairs, ident):
    with Stage(chip) as st:
        banks = [st.psum(P, HALF) for _ in range(6)]
        turned, act_done, dve_done = st.sems(3)
        block = st.block()
        units = [(src, dst, c, h) for src, dst in pairs for c in range(DC) for h in range(2)]

        @block.sync
        def _(sync):
            st.clear_other_set(sync)

        @block.tensor
        def _(pe):
            for n, (src, dst, c, h) in enumerate(units):
                if n >= 6:
                    pe.wait_ge((act_done, dve_done)[n % 2], (n - 6) // 2 + 1)
                for q in range(4):
                    ins = pe.transpose(banks[n % 6][:, tile(q)], src[:, 4 * h + q, tile(c)], ident[:, :])
                ins.then_inc(turned, 1)

        @block.scalar
        def _(act):
            for n, (src, dst, c, h) in enumerate(units):
                if n % 2 == 0:
                    act.wait_ge(turned, n + 1)
                    act.copy(dst[:, c, halves(h)], banks[n % 6][:, :]).then_inc(act_done, 1)

        @block.vector
        def _(dve):
            for n, (src, dst, c, h) in enumerate(units):
                if n % 2 == 1:
                    dve.wait_ge(turned, n + 1)
                    dve.tensor_copy(dst[:, c, halves(h)], banks[n % 6][:, :]).then_inc(dve_done, 1)


def local_attention(chip, X, xn, xnT, ident, w):
    nc = chip.nc
    DH = 16
    N = D // DH // 2
    BL = 2
    ROUNDS = B // BL
    with ExitStack() as es:
        sb = buffers(chip, es)
        v = sb(S, B, D)
        qT, kT, Wp = sb(P, DC, T), sb(P, DC, T), sb(P, DC, D)
        pairs_mask, own, fold, causal = sb(P, N // DC, 2), sb(P, 2), sb(P, S), sb(P, S)
        with ExitStack() as inner:
            ib = buffers(chip, inner)
            W, lnw = ib(P, DC, 3 * D), ib(P, D)
            qk = [ib(P, NT, D) for _ in range(2)]
            sq = ib(P, NT, D)
            ms, std = ib(P, 2, NT), ib(P, 2, NT)
            jobs = []
            for n in range(2):
                for j in range(NT):
                    jobs.append(([(xnT[:, k, tile(j)], W[:, k, n * D:(n + 1) * D]) for k in range(DC)], (P, D),
                                 ("act", "dve")[n], copy_out(qk[n][:, j, :])))
            for b in range(B):
                jobs.append(([(xnT[:, k, b * S:(b + 1) * S], W[:, k, 2 * D:]) for k in range(DC)], (S, D),
                             ("act", "dve")[b % 2], copy_out(v[:, b, :])))
            matmul_jobs(chip, jobs, [(W[:, :, :], w["w_qkv"]), (Wp[:, :, :], w["w_proj"]),
                                     (lnw[:, :], w["ln_w"].partition_broadcast(P)),
                                     (pairs_mask[:, :, :], w["pairs_mask"]), (own[:, :], w["own"]),
                                     (fold[:, :], w["fold"]), (causal[:, :], w["causal"])])
            with Stage(chip) as st:
                steps, mean_ready, std_ready = st.sems(3)
                block = st.block()

                @block.sync
                def _(sync):
                    st.clear_other_set(sync)

                @block.vector
                def _(dve):
                    c = Chain(dve, steps)
                    for n in range(2):
                        c.link(dve.tensor_tensor(sq[:, :, :], qk[n][:, :, :], qk[n][:, :, :], ALU.mult))
                        c.link(dve.tensor_reduce(ms[:, n, :], sq[:, :, :], AX.X, ALU.add))
                    dve.tensor_scalar(ms[:, :, :], ms[:, :, :], 1.0 / D, 1e-6, ALU.mult, ALU.add).then_inc(mean_ready, 1)
                    dve.wait_ge(std_ready, 1)
                    c.link(dve.reciprocal(std[:, :, :], std[:, :, :]))
                    for n in range(2):
                        c.link(dve.tensor_tensor(qk[n][:, :, :], qk[n][:, :, :],
                                                 std[:, n, :].unsqueeze(2).broadcast_to([P, NT, D]), ALU.mult))
                        dve.tensor_tensor(qk[n][:, :, :], qk[n][:, :, :],
                                          lnw[:, :].unsqueeze(1).broadcast_to([P, NT, D]), ALU.mult)

                @block.scalar
                def _(act):
                    act.wait_ge(mean_ready, 1)
                    act.activation(std[:, :, :], ms[:, :, :], ACT.Sqrt).then_inc(std_ready, 1)
            turn_to_features(chip, ((qk[0], qT), (qk[1], kT)), ident)

        with Stage(chip) as st:
            a = [st.sbuf(P, N, 2, S) for _ in range(2)]
            sc = [st.sbuf(P, N, S) for _ in range(2)]
            probsT = [st.sbuf(S, N, P) for _ in range(2)]
            mx, total = ([st.sbuf(P, N) for _ in range(2)] for _ in range(2))
            side = st.sbuf(P, N, 2)
            mixed = [st.sbuf(P, N, 2, DH) for _ in range(2)]
            mT = st.sbuf(P, DC, P)
            acc_s = [st.psum(P, N, S) for _ in range(2)]
            acc_t = st.psum(S, N, P)
            acc_o, acc_f, acc_y = st.psum(P, HALF), st.psum(P, HALF), st.psum(P, HALF)
            (always, staged, scored, shifted, exp_done, turned, turned_copied, mixed_filled, mixed_ready, folded,
             folded_copied, y_filled, added, score_steps, norm_steps, side_steps) = st.sems(16)
            block = st.block()

            def steps(eng, body):
                for i in peeled(eng, ROUNDS, 3):
                    for x in range(BL):
                        body(i, x, i * BL + x)
                for x in range(2):
                    body(ROUNDS, x, B + x)

            def live(g, lag):
                return lag <= g < B + lag if isinstance(g, int) else True

            @block.sync
            def _(sync):
                st.clear_other_set(sync)

            @block.gpsimd
            def _(pool):
                for i in peeled(pool, ROUNDS, 3):
                    for x in range(BL):
                        n = i * BL + x
                        if later(n, 2):
                            pool.wait_ge(scored, n - 1)
                        for c in range(DC):
                            for s in range(2):
                                q = N // DC
                                pool.tensor_tensor(
                                    a[x][:, c * q:(c + 1) * q, s, :],
                                    qT[:, c:c + 1, bass.ds(n * S, S)].broadcast_to([P, q, S]),
                                    pairs_mask[:, :, s:s + 1].broadcast_to([P, q, S]), ALU.mult).then_inc(staged, 1)

            @block.tensor
            def _(pe):
                pe.wait_ge(always, 1)

                def body(i, x, g):
                    if live(g, 0):
                        pe.wait_ge(staged, g * 4 + 4)
                        if later(g, 2):
                            pe.wait_ge(shifted, g - 1)
                        for r in range(N):
                            ins = pe.matmul(acc_s[x % 2][:, r, :], a[x % 2][:, r, :, :],
                                            kT[:, r // 4, bass.ds(g * S, S)], start=True, stop=True)
                        ins.then_inc(scored, 1)
                    if live(g, 1):
                        pe.wait_ge(always, 1)
                        pe.wait_ge(exp_done, g)
                        if later(g, 2):
                            pe.wait_ge(turned_copied, g - 1)
                        for r in range(N):
                            ins = pe.transpose(acc_t[:, r, :], sc[(x + 1) % 2][:, r, :], ident[:, :])
                        ins.then_inc(turned, 1)
                    if live(g, 2):
                        pe.wait_ge(turned_copied, g - 1)
                        if later(g, 3):
                            pe.wait_ge(mixed_ready, g - 2)
                        at = bass.ds(g - 2, 1)
                        pe.wait_ge(always, 1)
                        for r in range(N):
                            ins = pe.matmul(acc_o[:, r * 2 * DH:(r + 1) * 2 * DH], probsT[x % 2][:, r, :],
                                            v[:, at, r * 2 * DH:(r + 1) * 2 * DH], start=True, stop=True)
                        ins.then_inc(mixed_filled, 1)
                        pe.wait_ge(mixed_ready, g - 1)
                        if later(g, 3):
                            pe.wait_ge(folded_copied, g - 2)
                        for c in range(DC):
                            ins = pe.matmul(acc_f[:, c * S:(c + 1) * S], mixed[x % 2][:, 4 * c:4 * c + 4, :, :],
                                            fold[:, :], start=True, stop=True)
                        ins.then_inc(folded, 1)
                        if x % 2 == 1:
                            pe.wait_ge(folded_copied, g - 1)
                            if later(g, 4):
                                pe.wait_ge(added, i - 1)
                            for c in range(DC):
                                ins = pe.matmul(acc_y[:, 0:D], mT[:, c, :], Wp[:, c, :], start=(c == 0),
                                                stop=(c == DC - 1))
                            ins.then_inc(y_filled, 1)
                steps(pe, body)

            @block.scalar
            def _(act):
                def body(i, x, g):
                    if live(g, 0):
                        act.wait_ge(shifted, g + 1)
                        act.activation(sc[x % 2][:, :, :], sc[x % 2][:, :, :], ACT.Exp).then_inc(exp_done, 1)
                    if live(g, 1):
                        act.wait_ge(turned, g)
                        if later(g, 3):
                            act.wait_ge(mixed_filled, g - 2)
                        act.copy(probsT[(x + 1) % 2][:, :, :], acc_t[:, :, :]).then_inc(turned_copied, 1)
                steps(act, body)

            @block.vector
            def _(dve):
                dve.memset(total[0][:, :], 0.0).then_inc(always, 1)

                def body(i, x, g):
                    if live(g, 0):
                        t, m = sc[x % 2], mx[x % 2]
                        c = Chain(dve, score_steps, g * 2)
                        dve.wait_ge(scored, g + 1)
                        if later(g, 2):
                            dve.wait_ge(turned, g - 1)
                        c.link(dve.scalar_tensor_tensor(out=t[:, :, :], in0=acc_s[x % 2][:, :, :], scalar=DH ** -0.5,
                                                        in1=causal[:, :].unsqueeze(1).broadcast_to([P, N, S]),
                                                        op0=ALU.mult, op1=ALU.add))
                        c.link(dve.tensor_reduce(m[:, :], t[:, :, :], AX.X, ALU.max))
                        dve.tensor_tensor(t[:, :, :], t[:, :, :], m[:, :].unsqueeze(2).broadcast_to([P, N, S]),
                                          ALU.subtract).then_inc(shifted, 1)
                    if live(g, 1):
                        y = (x + 1) % 2
                        c = Chain(dve, norm_steps, g * 2 - 2)
                        dve.wait_ge(exp_done, g)
                        c.link(dve.tensor_reduce(total[y][:, :], sc[y][:, :, :], AX.X, ALU.add))
                        c.link(dve.reciprocal(total[y][:, :], total[y][:, :]))
                    if live(g, 2):
                        y = x % 2
                        c = Chain(dve, side_steps, g - 2)
                        c.link(dve.tensor_tensor(side[:, :, :], total[y][:, :].unsqueeze(2).broadcast_to([P, N, 2]),
                                                 own[:, :].unsqueeze(1).broadcast_to([P, N, 2]), ALU.mult))
                        dve.wait_ge(mixed_filled, g - 1)
                        if later(g, 4):
                            dve.wait_ge(folded, g - 3)
                        dve.tensor_tensor(mixed[y][:, :, :, :].rearrange("p r s d -> p (r s) d"),
                                          acc_o[:, 0:D].rearrange("p (r d) -> p r d", d=DH),
                                          side[:, :, :].rearrange("p r s -> p (r s)").unsqueeze(2).broadcast_to(
                                              [P, 2 * N, DH]), ALU.mult).then_inc(mixed_ready, 1)
                        dve.wait_ge(folded, g - 1)
                        if y == 0 and later(g, 4):
                            dve.wait_ge(y_filled, i - 1)
                        dve.tensor_copy(mT[:, :, y * S:(y + 1) * S], acc_f[:, 0:DC * S].rearrange("p (c s) -> p c s", c=DC)
                                        ).then_inc(folded_copied, 1)
                        if y == 1:
                            at = bass.ds(i - 1, 1)
                            dve.wait_ge(y_filled, i)
                            dve.tensor_tensor(X[:, at, :].rearrange("p o d -> p (o d)"),
                                              X[:, at, :].rearrange("p o d -> p (o d)"), acc_y[:, 0:D], ALU.add
                                              ).then_inc(added, 1)
                steps(dve, body)


def program(nc, w, out, stages):
    chip = Chip(nc)
    with ExitStack() as es:
        X = es.enter_context(nc.sbuf_tensor("x_tokens", [P, NT, D], F32))
        xn = es.enter_context(nc.sbuf_tensor("xn_tokens", [P, NT, D], F32))
        xnT = es.enter_context(nc.sbuf_tensor("xn_features", [P, DC, T], F32))
        ident = es.enter_context(nc.sbuf_tensor("identity", [P, P], F32))
        with Stage(chip) as st:
            loaded = st.sem()
            block = st.block()

            @block.sync
            def _(sync):
                st.clear_other_set(sync)
                sync.dma_start(X[:, :, :], w["x"]).then_inc(loaded, 16)
                sync.dma_start(ident[:, :], w["identity"]).then_inc(loaded, 16)
                sync.wait_ge(loaded, 32)

        def sub(prefix):
            own = {k[len(prefix):]: v for k, v in w.items() if k.startswith(prefix)}
            return {**own, "ctx": w["ctx"], "ctxT": w["ctxT"]}

        for s in stages:
            layer_norm(chip, X, xnT, ident, keep=xn)
            LAYERS[s](chip, X, xn, xnT, ident, sub(s + "_"))

        with Stage(chip) as st:
            stored = nc.alloc_semaphore("x_stored")
            block = st.block()

            @block.sync
            def _(sync):
                st.clear_other_set(sync)
                sync.dma_start(out, X[:, :, :]).then_inc(stored, 16)
                sync.wait_ge(stored, 16)


LAYERS = {"L0_attn": local_attention, "L3_attn": selective_scan, "L1_xattn": sixteen_head_xattn, "L0_xattn": one_head_xattn, "L2_xattn": eight_head_xattn, "L3_xattn": eight_head_xattn, "L0_ffn": shared_and_routed, "L1_ffn": top1_experts, "L2_ffn": capacity_experts, "L2_attn": lru, "L3_ffn": binary_mlp, "L1_attn": conv_pool_mlp}
STAGES = ["L0_xattn", "L0_attn", "L0_ffn", "L1_xattn", "L1_attn", "L1_ffn", "L2_xattn", "L2_attn", "L2_ffn", "L3_xattn", "L3_attn", "L3_ffn"]


def layouts(inputs):
    import numpy as np
    a = {k: np.asarray(v) for k, v in inputs.items()}

    def kpn(m):
        return m.reshape(-1, P, m.shape[-1]).transpose(1, 0, 2)

    o = {"x": kpn(a["x"].reshape(T, D)), "identity": np.eye(P, dtype=np.float32)}
    for n in ("theta_log", "nu_log", "gamma_log"):
        o["L2_attn_" + n] = a["L2_attn_" + n].reshape(P, 1)
    for n in ("B_re", "B_im"):
        o["L2_attn_" + n] = kpn(a["L2_attn_" + n].T)
    for n in ("C_re", "C_im"):
        o["L2_attn_" + n] = a["L2_attn_" + n].T
    o["L2_attn_D"] = a["L2_attn_D"]
    for n in ("k0", "k1", "k2"):
        o["L3_ffn_" + n] = np.ascontiguousarray(kpn(a["L3_ffn_" + n])).view(np.int32)
    for n in ("s0", "s1", "s2"):
        o["L3_ffn_" + n] = a["L3_ffn_" + n].reshape(1)

    def cols(v):
        return v.reshape(-1, P).T

    p = "L1_attn_"
    o[p + "conv_w"] = a[p + "conv_w"].reshape(4, 64, 64, 4).transpose(0, 2, 3, 1)
    o[p + "conv_b"] = cols(a[p + "conv_b"])
    for n in ("conv", "attn", "boom"):
        for x in "gb":
            o[f"{p}ln_{n}_{x}"] = cols(a[f"{p}ln_{n}_{x}"])
    for x in "qkv":
        o[p + "W" + x] = kpn(a[p + "W" + x].T)
        o[p + "b" + x] = cols(a[p + "b" + x])
    o[p + "inv_len"] = (1.0 / np.arange(1, S + 1)).astype(np.float32)
    o[p + "Wb"], o[p + "Wu"] = kpn(a[p + "Wb"].T), kpn(a[p + "Wu"].T)
    o[p + "bb"], o[p + "bu"] = cols(a[p + "bb"]), a[p + "bu"].reshape(1, D)
    c = a["ctx_768"]
    o["ctx"], o["ctxT"] = c.reshape(B, KT, P, CC).transpose(0, 2, 1, 3), c.transpose(0, 2, 1)
    p = "L0_xattn_"
    o[p + "Wq"], o[p + "bq"] = kpn(a[p + "Wq"].T), cols(a[p + "bq"])
    o[p + "Wk"] = kpn(np.concatenate([a[p + "Wk"], a[p + "bk"].reshape(D, 1)], axis=1))
    o[p + "Wv"], o[p + "bv"] = a[p + "Wv"].T, a[p + "bv"].reshape(1, D)
    for p in ("L2_xattn_", "L3_xattn_"):
        o[p + "Wq"], o[p + "Wo"], o[p + "bo"] = kpn(a[p + "Wq"]), kpn(a[p + "Wo"]), a[p + "bo"].reshape(1, D)
        o[p + "WkT"], o[p + "WvT"] = kpn(a[p + "Wk"].T), kpn(a[p + "Wv"].T)
    p = "L1_xattn_"
    H1, DH = 16, 16
    o[p + "Wq"], o[p + "bq"] = kpn(a[p + "Wq"].T), cols(a[p + "bq"])
    wkv, bkv = a[p + "Wkv"].reshape(H1, 2, DH, CC), a[p + "bkv"].reshape(H1, 2, DH)
    o[p + "Wk"], o[p + "bk"] = wkv[:, 0].reshape(D, CC).T, cols(bkv[:, 0].reshape(D))
    o[p + "Wv"] = np.concatenate([wkv[:, 1].reshape(D, CC).T, bkv[:, 1].reshape(1, D)])
    o[p + "Wo"], o[p + "bo"] = kpn(a[p + "Wo"].T), a[p + "bo"].reshape(1, D)
    o[p + "pairs_mask"] = (np.arange(P)[:, None] // DH == np.arange(P // DH)[None]).astype(np.float32).reshape(P, 4, 2)
    o[p + "own"] = (np.arange(P)[:, None] // S == np.arange(2)[None]).astype(np.float32)
    o[p + "fold"] = np.concatenate([np.eye(S, dtype=np.float32)] * 2)
    o[p + "own_channels"] = np.repeat(o[p + "own"], DH, axis=1)
    q = "L0_attn_"
    for n in ("pairs_mask", "own", "fold"):
        o[q + n] = o[p + n]
    o[q + "causal"] = np.where(np.arange(S)[None] <= np.arange(P)[:, None] % S, 0.0, -1e30).astype(np.float32)
    o[q + "w_qkv"], o[q + "w_proj"], o[q + "ln_w"] = kpn(a[q + "w_qkv"]), kpn(a[q + "w_proj"]), a[q + "ln_w"]
    p = "L3_attn_"
    for n in ("in_proj_w", "x_proj_w", "dt_proj_w", "out_proj_w"):
        o[p + n] = kpn(a[p + n])
    for n in ("conv_b", "dt_proj_b", "D_param"):
        o[p + n] = cols(a[p + n])
    o[p + "conv_w"] = a[p + "conv_w"].reshape(4, P, 3).transpose(1, 0, 2)
    o[p + "A_log"] = a[p + "A_log"].reshape(4, P, 16).transpose(1, 2, 0)
    lower = np.tril(np.ones((E, E), np.float32), -1).reshape(E * E)

    def per_expert(m):
        return m.reshape(E, -1, P, m.shape[-1]).transpose(0, 2, 1, 3)

    p = "L0_ffn_"
    o[p + "lower"] = o["L1_ffn_lower"] = o["L2_ffn_lower"] = lower
    o[p + "gate_w"] = kpn(a[p + "gate_w"].T)
    o[p + "w1"], o[p + "w3"] = per_expert(a[p + "w1"]), per_expert(a[p + "w3"])
    whole = a[p + "w2"].shape[1] // P * P
    o[p + "w2"], o[p + "w2_tail"] = per_expert(a[p + "w2"][:, :whole]), a[p + "w2"][:, whole:]
    for n in ("sw1", "sw2", "sw3"):
        o[p + n] = kpn(a[p + n])
    p = "L1_ffn_"
    o[p + "router_W"], o[p + "router_b"] = kpn(a[p + "router_W"]), a[p + "router_b"].reshape(1, E)
    o[p + "W1"], o[p + "W2"] = per_expert(a[p + "W1"]), per_expert(a[p + "W2"])
    o[p + "b1"] = a[p + "b1"].reshape(E, -1, P).transpose(0, 2, 1)
    o[p + "b2"] = a[p + "b2"]
    p = "L2_ffn_"
    o[p + "Wg"], o[p + "bg"] = kpn(a[p + "Wg"]), a[p + "bg"].reshape(1, E)
    for n in ("W1", "W2", "W3"):
        o[p + n] = per_expert(a[p + n])
    o[p + "tri"] = np.triu(np.ones((P, P), np.float32))
    o[p + "iota"] = np.arange(1, int(T / E * 1.25) + 1, dtype=np.float32)
    for q in ("L0_ffn_", "L1_ffn_"):
        o[q + "tri"], o[q + "iota_slot"] = o[p + "tri"], np.arange(1, P + 1, dtype=np.float32)
        o[q + "tile_rows"] = P * np.arange(TILES, dtype=np.float32)
        o[q + "tile_no"], o[q + "expert_no"] = np.arange(TILES, dtype=np.float32), np.arange(E, dtype=np.float32)
    return o


def kernel(**inputs):
    import numpy as np
    import concourse.bacc as bacc
    from concourse.bass_utils import run_bass_kernel_spmd as run

    nc = bacc.Bacc("TRN2", target_bir_lowering=False, num_devices=1)
    arrays, w = {}, {}
    for name, a in layouts(inputs).items():
        a = np.ascontiguousarray(a)
        arrays[f"in_{name}"] = a
        w[name] = nc.dram_tensor(f"in_{name}", a.shape, mybir.dt.from_np(a.dtype), kind="ExternalInput").ap()
    out = nc.dram_tensor("out_0", (P, NT, D), F32, kind="ExternalOutput").ap()
    program(nc, w, out, STAGES)
    r = run(nc, [arrays], core_ids=[0])
    got = np.asarray(r.results[0]["out_0"])
    return got.transpose(1, 0, 2).reshape(B, S, D)
```

```python
import concourse.bass as bass
from concourse import mybir
from contextlib import ExitStack

F32 = mybir.dt.float32
BF16 = mybir.dt.bfloat16
U8 = mybir.dt.uint8
I32 = mybir.dt.int32
ALU = mybir.AluOpType
ACT = mybir.ActivationFunctionType
AX = mybir.AxisListType

P = 128
B, S, D = 16, 64, 256
T = B * S
NT = T // P
DC = D // P
SK, CC = 1024, 192
C1 = CC - P
KT = SK // P
HALF = 512


class Chip:

    SEMS = 24

    def __init__(self, nc):
        self.nc = nc
        self.sets = [[nc.alloc_semaphore(f"stage_{s}_{n}") for n in range(self.SEMS)] for s in range(2)]
        self.stages = self.names = 0
        self.folded = nc.alloc_semaphore("residual_folded")
        self.abs_ready = nc.alloc_semaphore("abs_ready")


class Stage:

    def __init__(self, chip):
        self.chip, self.nc = chip, chip.nc
        self.mine = list(chip.sets[chip.stages % 2])
        self.other = chip.sets[(chip.stages + 1) % 2]
        self.first = chip.stages == 0
        chip.stages += 1
        self.stack = ExitStack()

    def __enter__(self):
        self.stack.__enter__()
        return self

    def __exit__(self, *e):
        return self.stack.__exit__(*e)

    def sbuf(self, *shape, dtype=F32):
        self.chip.names = n = self.chip.names + 1
        return self.stack.enter_context(self.nc.sbuf_tensor(f"buf{n}", list(shape), dtype))

    def psum(self, *shape):
        self.chip.names = n = self.chip.names + 1
        return self.stack.enter_context(self.nc.psum_tensor(f"acc{n}", list(shape), F32))

    def sems(self, n):
        return [self.mine.pop() for _ in range(n)]

    def sem(self):
        return self.mine.pop()

    def block(self):
        return self.stack.enter_context(self.nc.Block(no_gpsimd_drain=True))

    def clear_other_set(self, sync):
        if not self.first:
            nums = [s.num for s in self.other]
            assert max(nums) - min(nums) == len(nums) - 1
            sync.sem_clear(range(min(nums), max(nums) + 1))


def begin(chip, X, xn, xnT, ident, loads, sets=()):
    layer_norm(chip, X, xnT, ident, keep=xn, sets=sets, loads=loads)


class Chain:

    def __init__(self, eng, sem, base=0):
        self.eng, self.sem, self.base, self.n = eng, sem, base, 0

    def link(self, ins):
        self.n += 1
        ins.then_inc(self.sem, 1)
        self.eng.wait_ge(self.sem, self.base + self.n)


def layer_norm(chip, src, dstT, ident, eps=1e-5, keep=None, gain=None, sets=(), loads=()):
    nc = chip.nc
    with Stage(chip) as st:
        stats = st.sbuf(P, NT, 6)
        mv = st.sbuf(P, NT, 2)
        std = st.sbuf(P, NT)
        rstd = st.sbuf(P, NT)
        xn = keep if keep is not None else st.sbuf(P, NT, D)
        turned = [[st.psum(P, HALF) for h in range(2)] for c in range(DC)]
        steps, var_ready, std_ready, xn_ready, turned_ready, gain_in, cleared, loaded = st.sems(8)
        if gain is not None:
            gb = st.sbuf(P, 2, DC)
        block = st.block()

        def dst(c, h):
            return dstT(c, h) if callable(dstT) else dstT[:, c, h * HALF:(h + 1) * HALF]

        @block.sync
        def _(sync):
            st.clear_other_set(sync)
            if gain is not None:
                for n in range(2):
                    sync.dma_start(gb[:, n, :], gain[n]).then_inc(gain_in, 16)
            if sets:
                sync.wait_ge(cleared, len(sets))
            for to, source in loads[0::2]:
                sync.dma_start(to, source).then_inc(loaded, 16)
            if loads:
                sync.wait_ge(loaded, 16 * len(loads))

        @block.vector
        def _(dve):
            for buffer, value in sets:
                dve.memset(buffer, value).then_inc(cleared, 1)
            c = Chain(dve, steps)
            for j in range(NT):
                ins = dve.bn_stats(stats[:, j, :], src[:, j, :])
                if j == NT - 1:
                    c.link(ins)
            for j in range(NT):
                ins = dve.bn_aggr(mv[:, j, :], stats[:, j, :])
                if j == NT - 1:
                    c.link(ins)
            dve.tensor_scalar(rstd[:, :], mv[:, :, 1], eps, None, ALU.add).then_inc(var_ready, 1)
            dve.wait_ge(std_ready, 1)
            c.link(dve.reciprocal(rstd[:, :], std[:, :]))
            for j in range(NT):
                dve.tensor_scalar(xn[:, j, :], src[:, j, :], mv[:, j, 0:1], rstd[:, j:j + 1],
                                  ALU.subtract, ALU.mult).then_inc(xn_ready, 1)
            if gain is not None:
                dve.wait_ge(gain_in, 32)
            for h in range(2):
                dve.wait_ge(turned_ready, 4 * h + 4)
                if gain is None:
                    dve.tensor_copy(dst(1, h), turned[1][h][:, :])
                else:
                    dve.tensor_scalar(dst(1, h), turned[1][h][:, :] if not callable(dstT) else
                                      turned[1][h][:, :].rearrange("p (b s) -> p b s", s=S),
                                      gb[:, 0, 1:2], gb[:, 1, 1:2], ALU.mult, ALU.add)

        @block.scalar
        def _(act):
            if sets and loads:
                act.wait_ge(cleared, len(sets))
            for to, source in loads[1::2]:
                act.dma_start(to, source).then_inc(loaded, 16)
            act.wait_ge(var_ready, 1)
            act.activation(std[:, :], rstd[:, :], ACT.Sqrt).then_inc(std_ready, 1)
            if gain is not None:
                act.wait_ge(gain_in, 32)
            for h in range(2):
                act.wait_ge(turned_ready, 4 * h + 4)
                if gain is None:
                    act.copy(dst(0, h), turned[0][h][:, :])
                else:
                    act.activation(dst(0, h), turned[0][h][:, :] if not callable(dstT) else
                                   turned[0][h][:, :].rearrange("p (b s) -> p b s", s=S),
                                   ACT.Identity, bias=gb[:, 1, 0:1], scale=gb[:, 0, 0:1])

        @block.tensor
        def _(pe):
            for j in range(NT):
                pe.wait_ge(xn_ready, j + 1)
                for c in range(DC):
                    ins = pe.transpose(turned[c][j // 4][:, (j % 4) * P:(j % 4 + 1) * P],
                                       xn[:, j, c * P:(c + 1) * P], ident[:, :])
                ins.then_inc(turned_ready, 1)


def matmul_jobs(chip, jobs, loads, setup=None, nbanks=6, then=None):
    nc = chip.nc
    with Stage(chip) as st:
        banks = [st.psum(P, HALF) for _ in range(nbanks)]
        loaded, prepared, filled, act_done, dve_done, steps, act_steps, pool_steps = st.sems(8)
        done = {"act": act_done, "dve": dve_done, "steps": steps, "act_steps": act_steps, "pool_steps": pool_steps}
        then = then or {}
        turn, counts = [], {"act": 0, "dve": 0}
        for _, _, on, _ in jobs:
            counts[on] += 1
            turn.append(counts[on])
        block = st.block()

        @block.sync
        def _(sync):
            st.clear_other_set(sync)
            for dst, src in loads[0::2]:
                sync.dma_start(dst, src).then_inc(loaded, 16)

        @block.tensor
        def _(pe):
            if loads:
                pe.wait_ge(loaded, 16 * len(loads))
            if setup is not None:
                pe.wait_ge(prepared, 1)
            for n, (pairs, (r, w), on, write) in enumerate(jobs):
                if n >= nbanks:
                    before = jobs[n - nbanks][2]
                    pe.wait_ge(done[before], turn[n - nbanks])
                for k, (lhsT, rhs) in enumerate(pairs):
                    ins = pe.matmul(banks[n % nbanks][0:r, 0:w], lhsT, rhs, start=(k == 0),
                                    stop=(k == len(pairs) - 1))
                ins.then_inc(filled, 1)

        @block.scalar
        def _(act):
            for dst, src in loads[1::2]:
                act.dma_start(dst, src).then_inc(loaded, 16)
            if loads:
                act.wait_ge(loaded, 16 * len(loads))
            for n, (pairs, (r, w), on, write) in enumerate(jobs):
                if on == "act":
                    act.wait_ge(filled, n + 1)
                    write(act, banks[n % nbanks][0:r, 0:w]).then_inc(act_done, 1)
            if "act" in then:
                then["act"](act, done)

        @block.vector
        def _(dve):
            if loads:
                dve.wait_ge(loaded, 16 * len(loads))
            if setup is not None:
                chain = Chain(dve, steps)
                setup(dve, chain)
                chain.link(dve.engine_nop())
                dve.sem_inc(prepared, 1)
            for n, (pairs, (r, w), on, write) in enumerate(jobs):
                if on == "dve":
                    dve.wait_ge(filled, n + 1)
                    write(dve, banks[n % nbanks][0:r, 0:w]).then_inc(dve_done, 1)
            if "dve" in then:
                then["dve"](dve, done)

        if "pool" in then:
            @block.gpsimd
            def _(pool):
                then["pool"](pool, done)


def copy_out(dst):
    def write(eng, acc):
        return eng.copy(dst, acc) if is_scalar_engine(eng) else eng.tensor_copy(dst, acc)
    return write


def is_scalar_engine(eng):
    return eng.engine == mybir.EngineType.Activation


def halves(h):
    return slice(h * HALF, (h + 1) * HALF)


def lru(chip, X, xn, xnT, ident, w):
    nc = chip.nc
    HID = 128
    with ExitStack() as es:
        def sb(*shape):
            chip.names = n = chip.names + 1
            return es.enter_context(nc.sbuf_tensor(f"lru{n}", list(shape), F32))
        Bre, Bim = sb(P, DC, HID), sb(P, DC, HID)
        Cre, Cim, Drow = sb(P, D), sb(P, D), sb(P, D)
        par = sb(P, 3)
        re = [sb(P, T), sb(P, T)]
        im = [sb(P, T), sb(P, T)]
        g = sb(P, 1)
        lam = sb(P, 6, 3)
        tmp = sb(P, 8)
        big = sb(P, T)
        begin(chip, X, xn, xnT, ident,
              [(par[:, n:n + 1], w[name]) for n, name in enumerate(("theta_log", "nu_log", "gamma_log"))] +
              [(Bre[:], w["B_re"]), (Bim[:], w["B_im"]), (Cre[:, :], w["C_re"]), (Cim[:, :], w["C_im"]),
               (Drow[:, :], w["D"].partition_broadcast(P))])
        with Stage(chip) as st:
            dsteps, ready, back = st.sems(3)
            block = st.block()

            @block.sync
            def _(sync):
                st.clear_other_set(sync)

            @block.scalar
            def _(act):
                act.activation(tmp[:, 0:1], par[:, 0:1], ACT.Exp)
                act.activation(tmp[:, 1:2], par[:, 1:2], ACT.Exp).then_inc(ready, 1)
                act.wait_ge(ready, 1)
                act.activation(tmp[:, 2:3], tmp[:, 1:2], ACT.Exp, scale=-1.0)
                act.activation(g[:, :], par[:, 2:3], ACT.Exp).then_inc(ready, 1)
                act.wait_ge(back, 1)
                act.activation(tmp[:, 6:7], tmp[:, 4:5], ACT.Sin)
                act.activation(tmp[:, 7:8], tmp[:, 5:6], ACT.Sin).then_inc(ready, 1)

            @block.vector
            def _(dve):
                c = Chain(dve, dsteps)
                dve.wait_ge(ready, 2)
                c.link(dve.tensor_scalar(tmp[:, 3:4], tmp[:, 0:1], 0.15915494309189535, 12582912.0,
                                         ALU.mult, ALU.add))
                c.link(dve.tensor_scalar(tmp[:, 3:4], tmp[:, 3:4], -12582912.0, None, ALU.add))
                for part in (6.28125, 0.0019350051879882812, 3.0199e-07):
                    c.link(dve.scalar_tensor_tensor(out=tmp[:, 0:1], in0=tmp[:, 3:4], scalar=-part,
                                                    in1=tmp[:, 0:1], op0=ALU.mult, op1=ALU.add))
                c.link(dve.tensor_scalar(tmp[:, 4:5], tmp[:, 0:1], 3.1415925, -3.1415925, ALU.min, ALU.max))
                c.link(dve.tensor_scalar(tmp[:, 5:6], tmp[:, 4:5], -1.0, None, ALU.mult))
                c.link(dve.tensor_tensor(tmp[:, 5:6], tmp[:, 5:6], tmp[:, 4:5], ALU.min))
                dve.tensor_scalar(tmp[:, 5:6], tmp[:, 5:6], 1.5707963267948966, None,
                                  ALU.add).then_inc(back, 1)
                dve.wait_ge(ready, 3)
                c.link(dve.tensor_tensor(lam[:, 0, 0:1], tmp[:, 7:8], tmp[:, 2:3], ALU.mult))
                c.link(dve.tensor_tensor(lam[:, 0, 1:2], tmp[:, 6:7], tmp[:, 2:3], ALU.mult))
                for k in range(6):
                    a, b = lam[:, k, 0:1], lam[:, k, 1:2]
                    c.link(dve.tensor_scalar(lam[:, k, 2:3], b, -1.0, None, ALU.mult))
                    if k < 5:
                        a2, b2 = lam[:, k + 1, 0:1], lam[:, k + 1, 1:2]
                        c.link(dve.tensor_tensor(tmp[:, 6:7], b, b, ALU.mult))
                        c.link(dve.scalar_tensor_tensor(out=a2, in0=a, scalar=a, in1=tmp[:, 6:7],
                                                        op0=ALU.mult, op1=ALU.subtract))
                        c.link(dve.tensor_tensor(b2, a, b, ALU.mult))
                        c.link(dve.tensor_scalar(b2, b2, 2.0, None, ALU.mult))
        jobs = []
        for dst, wt in ((re[0], Bre), (im[0], Bim)):
            for h in range(2):
                def write(eng, acc, dst=dst, h=h):
                    return eng.activation(dst[:, halves(h)], acc, ACT.Copy, scale=g[:, 0:1])
                jobs.append(([(wt[:, k, :], xnT[:, k, halves(h)]) for k in range(DC)], (P, HALF), "act", write))
        matmul_jobs(chip, jobs, [])
        with Stage(chip) as st:
            dsteps = st.sem()
            block = st.block()

            @block.sync
            def _(sync):
                st.clear_other_set(sync)

            @block.vector
            def _(dve):
                c = Chain(dve, dsteps)
                for k in range(6):
                    s = 1 << k
                    v = [[t[i][:, :].rearrange("p (b s) -> p b s", s=S) for i in (k % 2, 1 - k % 2)] for t in (re, im)]
                    a, b, nb = (lam[:, k, n:n + 1] for n in range(3))
                    (r0, r1), (i0, i1) = v
                    for (src, dst, other, coef) in ((r0, r1, i0, nb), (i0, i1, r0, b)):
                        dve.tensor_copy(dst[:, :, 0:s], src[:, :, 0:s])
                        c.link(dve.scalar_tensor_tensor(out=dst[:, :, s:S], in0=src[:, :, 0:S - s], scalar=a,
                                                        in1=src[:, :, s:S], op0=ALU.mult, op1=ALU.add))
                        c.link(dve.scalar_tensor_tensor(out=dst[:, :, s:S], in0=other[:, :, 0:S - s], scalar=coef,
                                                        in1=dst[:, :, s:S], op0=ALU.mult, op1=ALU.add))
                c.link(dve.tensor_scalar(im[1][:, :], im[0][:, :], -1.0, None, ALU.mult))
                for j in range(NT):
                    c.link(dve.tensor_tensor(big[:, 0:D], xn[:, j, :], Drow[:, :], ALU.mult))
                    c.link(dve.tensor_tensor(X[:, j, :], X[:, j, :], big[:, 0:D], ALU.add))
        jobs = []
        for j in range(NT):
            def write(eng, acc, j=j):
                return eng.tensor_tensor(X[:, j, :], X[:, j, :], acc, ALU.add)
            t = slice(j * P, (j + 1) * P)
            jobs.append(([(re[0][:, t], Cre[:, :]), (im[1][:, t], Cim[:, :])], (P, D), "dve", write))
        matmul_jobs(chip, jobs, [])


def turn_to_tokens(chip, srcT, ident, write):
    with Stage(chip) as st:
        banks = [st.psum(P, HALF) for _ in range(4)]
        turned, written = st.sems(2)
        block = st.block()

        @block.sync
        def _(sync):
            st.clear_other_set(sync)

        @block.tensor
        def _(pe):
            for j in range(NT):
                if j >= 4:
                    pe.wait_ge(written, j - 3)
                for c in range(DC):
                    ins = pe.transpose(banks[j % 4][:, c * P:(c + 1) * P],
                                       srcT[:, c, j * P:(j + 1) * P], ident[:, :])
                ins.then_inc(turned, 1)

        @block.vector
        def _(dve):
            for j in range(NT):
                dve.wait_ge(turned, j + 1)
                write(dve, j, banks[j % 4][:, 0:D]).then_inc(written, 1)


def buffers(chip, es):
    def sb(*shape, dtype=F32):
        chip.names = n = chip.names + 1
        return es.enter_context(chip.nc.sbuf_tensor(f"buf{n}", list(shape), dtype))
    return sb


def tile(j):
    return slice(j * P, (j + 1) * P)


def binary_mlp(chip, X, xn, xnT, ident, w):
    F = 1024
    FC = F // P
    with ExitStack() as es:
        sb = buffers(chip, es)
        W0, W1, W2 = sb(P, DC, F), sb(P, FC, F), sb(P, FC, D)
        h1, h2 = sb(P, FC, T), sb(P, FC, T)
        sc = sb(P, 3)
        with ExitStack() as inner:
            ib = buffers(chip, inner)
            words = ib(P, 4, F // 4, dtype=I32), ib(P, FC, F // 4, dtype=I32), ib(P, FC, D // 4, dtype=I32)
            k0, k1, k2 = (b[:, :, :].bitcast(U8) for b in words)
            begin(chip, X, xn, xnT, ident, [(words[n][:, :, :], w[f"k{n}"]) for n in range(3)] +
                  [(sc[:, n:n + 1], w[f"s{n}"].partition_broadcast(P)) for n in range(3)])
            with Stage(chip) as st:
                steps = st.sem()
                block = st.block()

                @block.sync
                def _(sync):
                    st.clear_other_set(sync)

                @block.scalar
                def _(act):
                    act.activation(W2[:, :, :], k2[:, :, :], ACT.Copy, scale=2.0, bias=-1.0)
                    act.activation(W1[:, 0:4, :], k1[:, 0:4, :], ACT.Copy, scale=2.0, bias=-1.0)

                @block.vector
                def _(dve):
                    c = Chain(dve, steps)
                    c.link(dve.tensor_tensor(W0[:, :, :], k0[:, 0:2, :], k0[:, 2:4, :], ALU.subtract))
                    dve.tensor_scalar(W0[:, :, :], W0[:, :, :], 2.0, None, ALU.mult)
                    dve.tensor_scalar(W1[:, 4:8, :], k1[:, 4:8, :], 2.0, -1.0, ALU.mult, ALU.add)
                    c.link(dve.tensor_scalar(sc[:, 0:2], sc[:, 0:2], 2.0, None, ALU.mult))

        def relu_to(dst, n):
            def write(eng, acc):
                if is_scalar_engine(eng):
                    return eng.activation(dst, acc, ACT.Relu, scale=sc[:, n:n + 1])
                return eng.tensor_scalar(dst, acc, sc[:, n:n + 1], 0.0, ALU.mult, ALU.max)
            return write

        jobs = []
        for n, (wt, src, kc, dst) in enumerate(((W0, xnT, DC, h1), (W1, h1, FC, h2))):
            for h in range(2):
                for m in range(FC):
                    jobs.append(([(wt[:, k, tile(m)], src[:, k, halves(h)]) for k in range(kc)], (P, HALF),
                                 ("act", "dve")[m % 2], relu_to(dst[:, m, halves(h)], n)))
            matmul_jobs(chip, jobs, [])
            jobs = []
        for j in range(NT):
            def write(eng, acc, j=j):
                return eng.scalar_tensor_tensor(out=X[:, j, :], in0=acc, scalar=sc[:, 2:3], in1=X[:, j, :],
                                                op0=ALU.mult, op1=ALU.add)
            jobs.append(([(h2[:, k, tile(j)], W2[:, k, :]) for k in range(FC)], (P, D), "dve", write))
        matmul_jobs(chip, jobs, [])


def conv_pool_mlp(chip, X, xn, xnT, ident, w):
    K, F = 4, 1024
    FC = F // P
    PAD = K - 1
    with ExitStack() as es:
        sb = buffers(chip, es)
        H = sb(P, NT, D)
        aT = sb(P, DC, T)
        ones = sb(1, P)
        Wb, Wu, W = sb(P, DC, F), sb(P, FC, D), sb(P, 3, DC, D)
        bqkv, inv, bb, bu = sb(P, 3, DC), sb(P, S), sb(P, FC), sb(1, D)
        with ExitStack() as inner:
            ib = buffers(chip, inner)
            hp = ib(P, DC, B, S + PAD)
            cw, cb = ib(P, DC, K, P), ib(P, DC)
            begin(chip, X, xn, xnT, ident,
                  [(cw[(g % 2) * 64:(g % 2) * 64 + 64, g // 2, :, (g % 2) * 64:(g % 2) * 64 + 64], w["conv_w"][g])
                   for g in range(4)] + [(cb[:, :], w["conv_b"])] +
                  [(W[:, n, :, :], w["W" + x]) for n, x in enumerate("qkv")] +
                  [(bqkv[:, n, :], w["b" + x]) for n, x in enumerate("qkv")] +
                  [(inv[:, :], w["inv_len"].partition_broadcast(P)), (Wb[:, :, :], w["Wb"]), (Wu[:, :, :], w["Wu"]),
                   (bb[:, :], w["bb"]), (bu[:, :], w["bu"])],
                  [(cw[:, :, :, :], 0.0), (hp[:, :, :, 0:PAD], 0.0), (ones[:, :], 1.0)])
            layer_norm(chip, xn, lambda c, h: hp[:, c, h * 8:h * 8 + 8, PAD:], ident,
                       gain=(w["ln_conv_g"], w["ln_conv_b"]))
            convT = ib(P, DC, T)
            jobs = []
            for c in range(DC):
                for h in range(2):
                    def write(eng, acc, c=c, h=h):
                        return eng.activation(convT[:, c, halves(h)], acc, ACT.Identity, bias=cb[:, c:c + 1])
                    jobs.append(([(cw[:, c, k, :], hp[:, c, 8 * h:8 * h + 8, k:k + S]) for k in range(K)],
                                 (P, HALF), "act", write))
            matmul_jobs(chip, jobs, [])
            turn_to_tokens(chip, convT, ident,
                           lambda dve, j, acc: dve.tensor_tensor(H[:, j, :], xn[:, j, :], acc, ALU.add))
        layer_norm(chip, H, aT, ident, gain=(w["ln_attn_g"], w["ln_attn_b"]))
        with ExitStack() as inner:
            ib = buffers(chip, inner)
            q, k, v = (ib(P, DC, T) for _ in range(3))
            keep = ib(P, T)
            jobs = []
            for n, dst in enumerate((q, k, v)):
                for m in range(DC):
                    for h in range(2):
                        def write(eng, acc, dst=dst, n=n, m=m, h=h):
                            b = bqkv[:, n, m:m + 1]
                            if is_scalar_engine(eng):
                                return eng.activation(dst[:, m, halves(h)], acc, ACT.Identity, bias=b)
                            return eng.tensor_scalar(dst[:, m, halves(h)], acc, b, None, ALU.add)
                        jobs.append(([(W[:, n, c, tile(m)], aT[:, c, halves(h)]) for c in range(DC)], (P, HALF),
                                     ("act", "dve")[h], write))
            matmul_jobs(chip, jobs, [])
            with Stage(chip) as st:
                steps = st.sem()
                block = st.block()

                @block.sync
                def _(sync):
                    st.clear_other_set(sync)

                @block.vector
                def _(dve):
                    c = Chain(dve, steps)
                    c.link(dve.memset(keep[:, :], 1.0))
                    c.link(dve.memset(keep[:, :].rearrange("p (b s) -> p b s", s=S)[:, :, 0:1], 0.0))

                    def by_length(t, m):
                        v3 = t[:, m, :].rearrange("p (b s) -> p b s", s=S)
                        c.link(dve.tensor_tensor(v3, v3, inv[:, :].unsqueeze(1).broadcast_to([P, B, S]), ALU.mult))

                    for m in range(DC):
                        c.link(dve.tensor_tensor_scan(q[:, m, :], keep[:, :], q[:, m, :], 0.0, ALU.mult, ALU.add))
                        by_length(q, m)
                        c.link(dve.tensor_tensor(k[:, m, :], q[:, m, :], k[:, m, :], ALU.mult))
                        c.link(dve.tensor_tensor_scan(q[:, m, :], keep[:, :], k[:, m, :], 0.0, ALU.mult, ALU.add))
                        by_length(q, m)
                        c.link(dve.tensor_tensor(v[:, m, :], q[:, m, :], v[:, m, :], ALU.mult))
            turn_to_tokens(chip, v, ident,
                           lambda dve, j, acc: dve.tensor_tensor(H[:, j, :], H[:, j, :], acc, ALU.add))
        layer_norm(chip, H, aT, ident, gain=(w["ln_boom_g"], w["ln_boom_b"]))
        g = sb(P, FC, T)
        jobs = []
        for h in range(2):
            for m in range(FC):
                def write(eng, acc, m=m, h=h):
                    return eng.activation(g[:, m, halves(h)], acc, ACT.Gelu, bias=bb[:, m:m + 1])
                jobs.append(([(Wb[:, c, tile(m)], aT[:, c, halves(h)]) for c in range(DC)], (P, HALF), "act", write))
        matmul_jobs(chip, jobs, [])
        jobs = []
        for j in range(NT):
            def write(eng, acc, j=j):
                eng.tensor_tensor(X[:, j, :], X[:, j, :], H[:, j, :], ALU.add).then_inc(chip.folded, 1)
                eng.wait_ge(chip.folded, j + 1)
                return eng.tensor_tensor(X[:, j, :], X[:, j, :], acc, ALU.add)
            jobs.append(([(g[:, k, tile(j)], Wu[:, k, :]) for k in range(FC)] + [(ones[:, :], bu[:, :])],
                         (P, D), "dve", write))
        matmul_jobs(chip, jobs, [])


E = 8


def peeled(eng, n, first=1, last=0):
    yield from range(first)
    if n - last > first:
        with eng.Fori(first, n - last) as i:
            yield i
    yield from range(n - last, n)


def later(step, least):
    return step >= least if isinstance(step, int) else True


def route(chip, X, xn, xnT, ident, gate, gate_bias, K, share, w, choice, chosen, loads):
    nc = chip.nc
    with ExitStack() as es:
        sb = buffers(chip, es)
        logits, ex = sb(P, NT, E), sb(P, NT, E)
        above, equal = sb(P, NT, E, E), sb(P, NT, E, E)
        lower, small = sb(P, E * E), sb(P, NT)
        ones = sb(1, P)
        begin(chip, X, xn, xnT, ident, loads + [(lower[:, :], w["lower"].partition_broadcast(P))],
              [(ones[:, :], 1.0)])
        jobs = []
        for j in range(NT):
            def write(eng, acc, j=j):
                return eng.tensor_copy(logits[:, j, :], acc)
            pairs = [(xnT[:, k, tile(j)], gate[:, k, :]) for k in range(DC)]
            if gate_bias is not None:
                pairs.append((ones[:, :], gate_bias[:, :]))
            jobs.append((pairs, (P, E), "dve", write))
        matmul_jobs(chip, jobs, [])
        with Stage(chip) as st:
            steps, shifted, exp_done = st.sems(3)
            block = st.block()

            @block.sync
            def _(sync):
                st.clear_other_set(sync)

            @block.scalar
            def _(act):
                act.wait_ge(shifted, 1)
                act.activation(ex[:, :, :], ex[:, :, :], ACT.Exp).then_inc(exp_done, 1)

            @block.vector
            def _(dve):
                c = Chain(dve, steps)
                L = logits[:, :, :]
                full = [P, NT, E, E]
                c.link(dve.tensor_reduce(small[:, :], L, AX.X, ALU.max))
                dve.tensor_tensor(ex[:, :, :], L, small[:, :].unsqueeze(2).broadcast_to([P, NT, E]),
                                  ALU.subtract).then_inc(shifted, 1)
                other = L.unsqueeze(2).broadcast_to(full)
                own = L.unsqueeze(3).broadcast_to(full)
                flat = "p j a b -> p j (a b)"
                c.link(dve.tensor_tensor(above[:, :, :, :], other, own, ALU.is_gt))
                c.link(dve.tensor_tensor(equal[:, :, :, :], other, own, ALU.is_equal))
                c.link(dve.tensor_tensor(equal[:, :, :, :].rearrange(flat), equal[:, :, :, :].rearrange(flat),
                                         lower[:, :].unsqueeze(1).broadcast_to([P, NT, E * E]), ALU.mult))
                c.link(dve.tensor_tensor(above[:, :, :, :].rearrange(flat), above[:, :, :, :].rearrange(flat),
                                         equal[:, :, :, :].rearrange(flat), ALU.add))
                c.link(dve.tensor_reduce(chosen[:, :, :], above[:, :, :, :], AX.X, ALU.add))
                c.link(dve.tensor_scalar(chosen[:, :, :], chosen[:, :, :], K - 0.5, None, ALU.is_lt))
                dve.wait_ge(exp_done, 1)
                c.link(dve.tensor_tensor(choice[:, :, :], ex[:, :, :], chosen[:, :, :], ALU.mult))
                c.link(dve.tensor_reduce(small[:, :], (ex if share == "all" else choice)[:, :, :], AX.X, ALU.add))
                c.link(dve.reciprocal(small[:, :], small[:, :]))
                c.link(dve.tensor_tensor(choice[:, :, :], choice[:, :, :],
                                         small[:, :].unsqueeze(2).broadcast_to([P, NT, E]), ALU.mult))


TILES = 26


def routing_tables(sb, w):
    tables = {"tri": sb(P, P), "lower": sb(P, E * E), "iota_slot": sb(P, P), "tile_rows": sb(P, TILES),
              "expert_no": sb(P, E), "tile_no": sb(P, TILES)}
    return tables, [(t[:, :], w[n] if n == "tri" else w[n].partition_broadcast(P)) for n, t in tables.items()]


def routed_experts(chip, X, xn, ident, choice, chosen, tables, width, gated, loads_of, bias=False):
    nc = chip.nc
    M = -(-width // P)
    last = width - (M - 1) * P
    UP = 2 if gated else 1
    with ExitStack() as es:
        sb = buffers(chip, es)
        pos, picked = sb(P, NT, E), sb(P, NT, E)
        before = sb(P, NT + 1, E)
        count, tiles, base, grid = sb(P, E), sb(P, E), sb(P, E), sb(P, TILES * E)
        tri, lower, iota, tile_rows, expert_no, tile_no = (
            tables[n] for n in ("tri", "lower", "iota_slot", "tile_rows", "expert_no", "tile_no"))
        ones, tile_expert = sb(P, P), sb(P, TILES)
        expert_int, rounds_int = sb(1, TILES, dtype=I32), sb(1, 1, dtype=I32)

        def prefixes(dve, chain):
            dve.memset(ones[:, :], 1.0)
            chain.link(dve.memset(before[:, 0, :], 0.0))
            for j in range(1, NT + 1):
                chain.link(dve.tensor_tensor(before[:, j, :], before[:, j - 1, :], chosen[:, j - 1, :], ALU.add))
        flat = "p j e -> p (j e)"
        jobs = [([(ones[:, :], before[:, NT, :])], (P, E), "dve", copy_out(count[:, :])),
                ([(tri[:, :], chosen[:, :, :].rearrange(flat)), (ones[:, :], before[:, 0:NT, :].rearrange(flat))],
                 (P, NT * E), "dve", copy_out(pos[:, :, :].rearrange(flat)))]
        matmul_jobs(chip, jobs, [], setup=prefixes)

        with Stage(chip) as st:
            steps = st.sem()
            block = st.block()

            @block.sync
            def _(sync):
                st.clear_other_set(sync)

            @block.vector
            def _(dve):
                c = Chain(dve, steps)
                square = [P, E, E]
                g = grid[:, 0:E * E].rearrange("p (a b) -> p a b", b=E)
                c.link(dve.tensor_tensor(g, count[:, :].unsqueeze(2).broadcast_to(square),
                                         tile_rows[:, 0:E].unsqueeze(1).broadcast_to(square), ALU.is_gt))
                c.link(dve.tensor_reduce(tiles[:, :], g, AX.X, ALU.add))
                c.link(dve.tensor_tensor(g, lower[:, :].rearrange("p (a b) -> p a b", b=E),
                                         tiles[:, :].unsqueeze(1).broadcast_to(square), ALU.mult))
                c.link(dve.tensor_reduce(base[:, :], g, AX.X, ALU.add))
                c.link(dve.tensor_tensor(tiles[:, :], tiles[:, :], base[:, :], ALU.add))
                c.link(dve.tensor_scalar(count[0:1, 0:1], tiles[0:1, E - 1:E], 0.5, 0.5, ALU.add, ALU.mult))
                c.link(dve.tensor_copy(rounds_int[:, :], count[0:1, 0:1]))
                g = grid[:, :].rearrange("p (a b) -> p a b", b=E)
                wide = [P, TILES, E]
                c.link(dve.tensor_tensor(g, tile_no[:, :].unsqueeze(2).broadcast_to(wide),
                                         tiles[:, :].unsqueeze(1).broadcast_to(wide), ALU.is_ge))
                c.link(dve.tensor_reduce(tile_expert[:, :], g, AX.X, ALU.add))
                c.link(dve.tensor_scalar(tile_expert[:, :], tile_expert[:, :], E - 1.0, None, ALU.min))
                c.link(dve.tensor_copy(expert_int[:, :], tile_expert[0:1, :]))
                c.link(dve.tensor_scalar(base[:, :], base[:, :], float(P), None, ALU.mult))
                c.link(dve.tensor_tensor(pos[:, :, :], pos[:, :, :], base[:, :].unsqueeze(1).broadcast_to([P, NT, E]),
                                         ALU.add))
                c.link(dve.tensor_tensor(pos[:, :, :], pos[:, :, :], chosen[:, :, :], ALU.mult))

        with Stage(chip) as st:
            Wup = [[st.sbuf(P, DC, width) for _ in range(UP)] for _ in range(2)]
            Wdn = [st.sbuf(P, M, D) for _ in range(2)]
            b_up, b_dn = [st.sbuf(P, M) for _ in range(2)], [st.sbuf(1, D) for _ in range(2)]
            hot = [st.sbuf(P, NT, P) for _ in range(2)]
            hotT = [st.sbuf(P, T) for _ in range(2)]
            own, cur = st.sbuf(P, E), st.sbuf(P, NT)
            scale = [st.sbuf(P, NT) for _ in range(2)]
            taken, given = st.sbuf(P, DC, P), [st.sbuf(P, D) for _ in range(2)]
            sil, hid = st.sbuf(P, M, P), st.sbuf(P, M, P)
            acc_take, acc_down = st.psum(P, DC, P), st.psum(P, D)
            acc_turn = [st.psum(P, HALF) for _ in range(2)]
            acc_up = [st.psum(P, UP, P) for _ in range(2)]
            acc_y = [st.psum(P, HALF) for _ in range(2)]
            weights_in = st.sems(2)
            (own_steps, hot_ready, take_filled, taken_ready, turned, turn_copied, up_filled, silu_done, hid_ready,
             down_filled, given_ready, y_filled, added) = st.sems(13)
            block = st.block()
            n_loads = UP + (1 if last == P else 2) + (2 if bias else 0)

            def size(m):
                return last if m == M - 1 else P

            def rounds_of(eng):
                return eng.value_load(rounds_int[0:1, 0:1], min_val=2, max_val=TILES // 2 - 1)

            def rounds(eng, count):
                yield 0
                with eng.Fori(1, count) as i:
                    yield i

            @block.sync
            def _(sync):
                st.clear_other_set(sync)
                for i in rounds(sync, rounds_of(sync)):
                    for x in range(2):
                        n = i * 2 + x
                        if later(n, 2):
                            sync.wait_ge(down_filled, n - 1)
                        e = sync.value_load(expert_int[0:1, bass.ds(n, 1)], min_val=0, max_val=E - 1)
                        k = 0
                        for dst, src in loads_of(x, e, Wup, Wdn, b_up, b_dn):
                            sync.dma_start(dst, src).then_inc(weights_in[x], 16)
                            k += 1
                        assert k == n_loads

            @block.tensor
            def _(pe):
                def give(n, x):
                    pe.wait_ge(given_ready, n + 1)
                    for j in range(NT):
                        if later(n * NT + j, 2):
                            pe.wait_ge(added, n * NT + j - 1)
                        pe.matmul(acc_y[j % 2][:, 0:D], hotT[x][:, tile(j)], given[x][:, :], start=True, stop=True
                                  ).then_inc(y_filled, 1)

                count = rounds_of(pe)
                for i in rounds(pe, count):
                    for x in range(2):
                        n = i * 2 + x
                        pe.wait_ge(hot_ready, n + 1)
                        if later(n, 1):
                            pe.wait_ge(taken_ready, n)
                        for c in range(DC):
                            for j in range(NT):
                                ins = pe.matmul(acc_take[:, c, :], xn[:, j, tile(c)], hot[x][:, j, :],
                                                start=(j == 0), stop=(j == NT - 1))
                        ins.then_inc(take_filled, 1)
                        for s in range(2):
                            if later(n, 1):
                                pe.wait_ge(turn_copied, n * 2 - 1 + s)
                            for q in range(4):
                                ins = pe.transpose(acc_turn[s][:, tile(q)], hot[x][:, s * 4 + q, :], ident[:, :])
                            ins.then_inc(turned, 1)
                        pe.wait_ge(weights_in[x], i * (16 * n_loads) + 16 * n_loads)
                        pe.wait_ge(taken_ready, n + 1)
                        for m in range(M):
                            if later(n * M + m, 2):
                                pe.wait_ge(hid_ready, n * M + m - 1)
                            for u in range(UP):
                                for k in range(DC):
                                    ins = pe.matmul(acc_up[m % 2][0:size(m), u, :], Wup[x][u][:, k, m * P:m * P + size(m)],
                                                    taken[:, k, :], start=(k == 0), stop=(k == DC - 1))
                            ins.then_inc(up_filled, 1)
                        if x == 1:
                            give(n - 1, 0)
                        pe.wait_ge(hid_ready, n * M + M)
                        if later(n, 1):
                            pe.wait_ge(given_ready, n)
                        for k in range(M):
                            ins = pe.matmul(acc_down[:, :], hid[0:size(k), k, :], Wdn[x][0:size(k), k, :],
                                            start=(k == 0), stop=(k == M - 1 and not bias))
                        if bias:
                            ins = pe.matmul(acc_down[:, :], ones[0:1, :], b_dn[x][:, :], start=False, stop=True)
                        ins.then_inc(down_filled, 1)
                        if x == 1:
                            give(n, 1)

            @block.scalar
            def _(act):
                for i in rounds(act, rounds_of(act)):
                    for x in range(2):
                        n = i * 2 + x
                        act.wait_ge(take_filled, n + 1)
                        if later(n, 1):
                            act.wait_ge(up_filled, n * M)
                        act.copy(taken[:, :, :], acc_take[:, :, :]).then_inc(taken_ready, 1)
                        for s in range(2):
                            act.wait_ge(turned, n * 2 + s + 1)
                            if s == 0 and later(n, 2):
                                act.wait_ge(y_filled, n * NT - NT)
                            act.copy(hotT[x][:, halves(s)], acc_turn[s][:, :]).then_inc(turn_copied, 1)
                        if bias:
                            act.wait_ge(weights_in[x], i * (16 * n_loads) + 16 * n_loads)
                        for m in range(M):
                            act.wait_ge(up_filled, n * M + m + 1)
                            if gated:
                                if m == 0 and later(n, 1):
                                    act.wait_ge(hid_ready, n * M)
                                act.activation(sil[0:size(m), m, :], acc_up[m % 2][0:size(m), 0, :], ACT.Silu
                                               ).then_inc(silu_done, 1)
                            else:
                                if m == 0 and later(n, 1):
                                    act.wait_ge(down_filled, n)
                                act.activation(hid[0:size(m), m, :], acc_up[m % 2][0:size(m), 0, :], ACT.Relu,
                                               bias=b_up[x][0:size(m), m:m + 1]).then_inc(hid_ready, 1)
                        act.wait_ge(down_filled, n + 1)
                        if later(n, 2):
                            act.wait_ge(y_filled, n * NT - NT)
                        act.copy(given[x][:, :], acc_down[:, :]).then_inc(given_ready, 1)

            @block.vector
            def _(dve):
                def prepare(n, x):
                    c = Chain(dve, own_steps, n * 6)
                    if later(n, 2):
                        dve.wait_ge(added, n * NT - NT)
                    at = bass.ds(n, 1)
                    c.link(dve.tensor_scalar(own[:, :], expert_no[:, :], tile_expert[:, at], None, ALU.is_equal))
                    mine = own[:, :].unsqueeze(1).broadcast_to([P, NT, E])
                    for src, dst in ((choice, scale[x]), (pos, cur)):
                        c.link(dve.tensor_tensor(picked[:, :, :], src[:, :, :], mine, ALU.mult))
                        c.link(dve.tensor_reduce(dst[:, :], picked[:, :, :], AX.X, ALU.add))
                    c.link(dve.tensor_scalar(cur[:, :], cur[:, :], tile_rows[:, at], None, ALU.subtract))
                    if later(n, 2):
                        dve.wait_ge(turned, n * 2 - 2)
                    dve.tensor_tensor(hot[x][:, :, :], iota[:, :].unsqueeze(1).broadcast_to([P, NT, P]),
                                      cur[:, :].unsqueeze(2).broadcast_to([P, NT, P]), ALU.is_equal
                                      ).then_inc(hot_ready, 1)
                    dve.wait_ge(hot_ready, n + 1)

                def add(n, x):
                    if later(n, 1):
                        dve.wait_ge(added, n * NT)
                    for j in range(NT):
                        dve.wait_ge(y_filled, n * NT + j + 1)
                        dve.scalar_tensor_tensor(out=X[:, j, :], in0=acc_y[j % 2][:, 0:D], scalar=scale[x][:, j:j + 1],
                                                 in1=X[:, j, :], op0=ALU.mult, op1=ALU.add).then_inc(added, 1)

                count = rounds_of(dve)
                prepare(0, 0)
                for i in rounds(dve, count):
                    for x in range(2):
                        n = i * 2 + x
                        if gated:
                            for m in range(M):
                                dve.wait_ge(silu_done, n * M + m + 1)
                                if m == 0 and later(n, 1):
                                    dve.wait_ge(down_filled, n)
                                dve.tensor_tensor(hid[0:size(m), m, :], sil[0:size(m), m, :],
                                                  acc_up[m % 2][0:size(m), 1, :], ALU.mult).then_inc(hid_ready, 1)
                        if x == 1:
                            add(n - 1, 0)
                        prepare(n + 1, 1 - x)
                        if x == 1:
                            add(n, 1)


def shared_and_routed(chip, X, xn, xnT, ident, w):
    HID, SH = 704, 384
    with ExitStack() as es:
        sb = buffers(chip, es)
        choice, chosen, gate = sb(P, NT, E), sb(P, NT, E), sb(P, DC, E)
        MS = SH // P
        s1, s3, s2 = sb(P, DC, SH), sb(P, DC, SH), sb(P, MS, D)
        tables, table_loads = routing_tables(sb, w)
        route(chip, X, xn, xnT, ident, gate, None, 2, "all", w, choice, chosen,
              [(gate[:, :, :], w["gate_w"]), (s1[:, :, :], w["sw1"]), (s3[:, :, :], w["sw3"]), (s2[:, :, :], w["sw2"])] +
              table_loads)
        FULL = HID // P

        def loads_of(x, e, Wup, Wdn, b_up, b_dn):
            one = bass.ds(e, 1)
            yield Wup[x][0][:, :, :], w["w1"][one].rearrange("o p k n -> p (o k) n")
            yield Wup[x][1][:, :, :], w["w3"][one].rearrange("o p k n -> p (o k) n")
            yield Wdn[x][:, 0:FULL, :], w["w2"][one].rearrange("o p k n -> p (o k) n")
            yield Wdn[x][0:HID - FULL * P, FULL, :], w["w2_tail"][one].rearrange("o p n -> (o p) n")
        routed_experts(chip, X, xn, ident, choice, chosen, tables, HID, True, loads_of)
        a, hid = sb(P, MS, T), sb(P, MS, T)
        jobs = []
        for h in range(2):
            for m in range(MS):
                def silu(eng, acc, m=m, h=h):
                    return eng.activation(a[:, m, halves(h)], acc, ACT.Silu)

                def copy(eng, acc, m=m, h=h):
                    return eng.tensor_copy(hid[:, m, halves(h)], acc)
                for wt, on, write in ((s1, "act", silu), (s3, "dve", copy)):
                    jobs.append(([(wt[:, k, tile(m)], xnT[:, k, halves(h)]) for k in range(DC)], (P, HALF), on, write))
        matmul_jobs(chip, jobs, [])

        def gate_hidden(dve, chain):
            for m in range(MS):
                dve.tensor_tensor(hid[:, m, :], hid[:, m, :], a[:, m, :], ALU.mult)
        jobs = []
        for j in range(NT):
            def write(eng, acc, j=j):
                return eng.tensor_tensor(X[:, j, :], X[:, j, :], acc, ALU.add)
            jobs.append(([(hid[:, k, tile(j)], s2[:, k, :]) for k in range(MS)], (P, D), "dve", write))
        matmul_jobs(chip, jobs, [], setup=gate_hidden)


def top1_experts(chip, X, xn, xnT, ident, w):
    with ExitStack() as es:
        sb = buffers(chip, es)
        choice, chosen, gate, gb = sb(P, NT, E), sb(P, NT, E), sb(P, DC, E), sb(1, E)
        tables, table_loads = routing_tables(sb, w)
        route(chip, X, xn, xnT, ident, gate, gb, 1, "all", w, choice, chosen,
              [(gate[:, :, :], w["router_W"]), (gb[:, :], w["router_b"])] + table_loads)

        def loads_of(x, e, Wup, Wdn, b_up, b_dn):
            one = bass.ds(e, 1)
            yield Wup[x][0][:, :, :], w["W1"][one].rearrange("o p k n -> p (o k) n")
            yield Wdn[x][:, :, :], w["W2"][one].rearrange("o p k n -> p (o k) n")
            yield b_up[x][:, :], w["b1"][one].rearrange("o p m -> p (o m)")
            yield b_dn[x][:, :], w["b2"][one]
        routed_experts(chip, X, xn, ident, choice, chosen, tables, 1024, False, loads_of, bias=True)


def capacity_experts(chip, X, xn, xnT, ident, w):
    HID = 1024
    M = HID // P
    CAP = int(T / E * 1.25)
    HC = CAP // 2
    with ExitStack() as es:
        sb = buffers(chip, es)
        choice, chosen, gate, gb = sb(P, NT, E), sb(P, NT, E), sb(P, DC, E), sb(1, E)
        slot, before = sb(P, NT, E), sb(P, NT, E)
        tri, ones, iota = sb(P, P), sb(P, P), sb(P, CAP)
        route(chip, X, xn, xnT, ident, gate, gb, 2, "chosen", w, choice, chosen,
              [(gate[:, :, :], w["Wg"]), (gb[:, :], w["bg"]), (tri[:, :], w["tri"]),
               (iota[:, :], w["iota"].partition_broadcast(P))])

        def prefixes(dve, chain):
            dve.memset(ones[:, :], 1.0)
            chain.link(dve.memset(before[:, 0, :], 0.0))
            for j in range(1, NT):
                chain.link(dve.tensor_tensor(before[:, j, :], before[:, j - 1, :], chosen[:, j - 1, :], ALU.add))
        flat = "p j e -> p (j e)"

        def write(eng, acc):
            return eng.tensor_tensor(slot[:, :, :].rearrange(flat), acc, chosen[:, :, :].rearrange(flat), ALU.mult)
        jobs = [([(tri[:, :], chosen[:, :, :].rearrange(flat)), (ones[:, :], before[:, :, :].rearrange(flat))],
                 (P, NT * E), "dve", write)]
        matmul_jobs(chip, jobs, [], setup=prefixes)

        with Stage(chip) as st:
            W1, W2 = ([st.sbuf(P, DC, HID) for _ in range(2)] for _ in range(2))
            W3 = [st.sbuf(P, M, D) for _ in range(2)]
            cur, scale = ([st.sbuf(P, NT) for _ in range(2)] for _ in range(2))
            hot = [st.sbuf(P, NT, CAP) for _ in range(2)]
            hotT = st.sbuf(HC, 2, T)
            taken = st.sbuf(P, DC, CAP)
            sil, hid = st.sbuf(P, M, CAP), st.sbuf(P, M, CAP)
            given = st.sbuf(HC, 2, D)
            acc_take, acc_out = st.psum(P, DC, HALF // 2), st.psum(HC, 2, D)
            acc_turn = [st.psum(P, HALF) for _ in range(2)]
            acc_up = [st.psum(P, 2, HALF // 2) for _ in range(2)]
            acc_y = [st.psum(P, HALF) for _ in range(2)]
            weights_in = st.sems(2)
            (cols_ready, cur_steps, hot_ready, take_filled, taken_ready, turned, turn_copied, up_filled, silu_done,
             hid_ready, out_filled, given_ready, y_filled, added) = st.sems(14)
            block = st.block()

            @block.sync
            def _(sync):
                st.clear_other_set(sync)
                for i in peeled(sync, E // 2):
                    for x in range(2):
                        e = i * 2 + x
                        if later(i, 1):
                            sync.wait_ge(out_filled, e - 1)
                        for dst, name in ((W1, "W1"), (W2, "W2"), (W3, "W3")):
                            sync.dma_start(dst[x][:, :, :], w[name][bass.ds(e, 1)].rearrange("o p k n -> p (o k) n")
                                           ).then_inc(weights_in[x], 16)

            @block.tensor
            def _(pe):
                for i in peeled(pe, E // 2):
                    for x in range(2):
                        e = i * 2 + x
                        pe.wait_ge(hot_ready, e + 1)
                        if later(e, 1):
                            pe.wait_ge(taken_ready, e)
                        for c in range(DC):
                            for j in range(NT):
                                ins = pe.matmul(acc_take[:, c, 0:CAP], xn[:, j, tile(c)], hot[x][:, j, :],
                                                start=(j == 0), stop=(j == NT - 1))
                        ins.then_inc(take_filled, 1)
                        for n in range(4):
                            if later(e * 4 + n, 2):
                                pe.wait_ge(turn_copied, e * 4 + n - 1)
                            for q in range(4):
                                s, j = n // 2, (n % 2) * 4 + q
                                ins = pe.transpose(acc_turn[n % 2][0:HC, q * P:(q + 1) * P],
                                                   hot[x][:, j, s * HC:(s + 1) * HC], ident[:, :])
                            ins.then_inc(turned, 1)
                        pe.wait_ge(weights_in[x], i * 48 + 48)
                        pe.wait_ge(taken_ready, e + 1)
                        for m in range(M):
                            if later(e * M + m, 2):
                                pe.wait_ge(hid_ready, e * M + m - 1)
                            for u, wt in enumerate((W1[x], W2[x])):
                                for k in range(DC):
                                    ins = pe.matmul(acc_up[m % 2][:, u, 0:CAP], wt[:, k, tile(m)], taken[:, k, :],
                                                    start=(k == 0), stop=(k == DC - 1))
                            ins.then_inc(up_filled, 1)
                        pe.wait_ge(hid_ready, e * M + M)
                        if later(e, 1):
                            pe.wait_ge(given_ready, e)
                        for s in range(2):
                            for k in range(M):
                                ins = pe.matmul(acc_out[:, s, :], hid[:, k, s * HC:(s + 1) * HC], W3[x][:, k, :],
                                                start=(k == 0), stop=(k == M - 1))
                        ins.then_inc(out_filled, 1)
                        pe.wait_ge(given_ready, e + 1)
                        pe.wait_ge(turn_copied, e * 4 + 4)
                        for j in range(NT):
                            if later(e * NT + j, 2):
                                pe.wait_ge(added, e * NT + j - 1)
                            for s in range(2):
                                ins = pe.matmul(acc_y[j % 2][:, 0:D], hotT[:, s, tile(j)], given[:, s, :],
                                                start=(s == 0), stop=(s == 1))
                            ins.then_inc(y_filled, 1)

            @block.scalar
            def _(act):
                for i in peeled(act, E // 2):
                    for x in range(2):
                        e = i * 2 + x
                        act.wait_ge(take_filled, e + 1)
                        if later(e, 1):
                            act.wait_ge(up_filled, e * M)
                        act.copy(taken[:, :, :], acc_take[:, :, 0:CAP]).then_inc(taken_ready, 1)
                        for n in range(4):
                            act.wait_ge(turned, e * 4 + n + 1)
                            if n == 0 and later(e, 1):
                                act.wait_ge(y_filled, e * NT)
                            act.copy(hotT[:, n // 2, halves(n % 2)], acc_turn[n % 2][0:HC, :]).then_inc(turn_copied, 1)
                        for m in range(M):
                            act.wait_ge(up_filled, e * M + m + 1)
                            if m == 0 and later(e, 1):
                                act.wait_ge(hid_ready, e * M)
                            act.activation(sil[:, m, :], acc_up[m % 2][:, 0, 0:CAP], ACT.Silu).then_inc(silu_done, 1)
                        act.wait_ge(out_filled, e + 1)
                        if later(e, 1):
                            act.wait_ge(y_filled, e * NT)
                        act.copy(given[:, :, :], acc_out[:, :, :]).then_inc(given_ready, 1)

            @block.vector
            def _(dve):
                def one_hot(e, x):
                    at = bass.ds(e, 1)
                    if later(e, 2):
                        dve.wait_ge(added, e * NT - NT)
                    dve.tensor_copy(cur[x][:, :], slot[:, :, at].rearrange("p j o -> p (j o)"))
                    dve.tensor_copy(scale[x][:, :], choice[:, :, at].rearrange("p j o -> p (j o)")
                                    ).then_inc(cols_ready, 1)
                    dve.wait_ge(cols_ready, e + 1)
                    if later(e, 2):
                        dve.wait_ge(turned, e * 4 - 4)
                    for j in range(NT):
                        ins = dve.tensor_scalar(hot[x][:, j, :], iota[:, :], cur[x][:, j:j + 1], None, ALU.is_equal)
                    ins.then_inc(hot_ready, 1)

                for i in peeled(dve, E // 2):
                    for x in range(2):
                        e = i * 2 + x
                        one_hot(e, x)
                        for m in range(M):
                            dve.wait_ge(silu_done, e * M + m + 1)
                            if m == 0 and later(e, 1):
                                dve.wait_ge(out_filled, e)
                            dve.tensor_tensor(hid[:, m, :], sil[:, m, :], acc_up[m % 2][:, 1, 0:CAP],
                                              ALU.mult).then_inc(hid_ready, 1)
                        if later(e, 1):
                            dve.wait_ge(added, e * NT)
                        for j in range(NT):
                            dve.wait_ge(y_filled, e * NT + j + 1)
                            dve.scalar_tensor_tensor(out=X[:, j, :], in0=acc_y[j % 2][:, 0:D],
                                                     scalar=scale[x][:, j:j + 1], in1=X[:, j, :],
                                                     op0=ALU.mult, op1=ALU.add).then_inc(added, 1)


def attend_context(chip, X, q0, q1, out0, out1, out_bias, ones, w, heads, ident):
    nc = chip.nc
    HT = min(heads, 2)
    R = HT * S
    N = heads // HT
    BL = 2 if N > 1 else 4
    U = BL * N
    PAIR = 2 * N
    ROUNDS, G = B // BL, B * N
    K1 = q1.shape[0]
    NB = 2 if N > 1 else 4
    with Stage(chip) as st:
        ctx = [st.sbuf(P, KT, CC) for _ in range(NB)]
        ct0, ct1 = [st.sbuf(P, SK) for _ in range(NB)], [st.sbuf(K1, SK) for _ in range(NB)]
        a0, a1 = [st.sbuf(P, heads, S) for _ in range(NB)], [st.sbuf(K1, heads, S) for _ in range(NB)]
        probs = [st.sbuf(R, SK) for _ in range(2)]
        probsT = [st.sbuf(P, KT, R) for _ in range(2)]
        mixed = [st.sbuf(R, CC) for _ in range(2)]
        m0, m1 = st.sbuf(P, heads, P), st.sbuf(C1, heads, P)
        negmax, total, inverse = st.sbuf(R, 4), st.sbuf(R, 4), st.sbuf(R, 4)
        acc_s = [st.psum(R, SK) for _ in range(2)]
        acc_t = st.psum(P, KT, R)
        acc_o = st.psum(R, HALF)
        acc_my = st.psum(P, HALF)
        acc_m0, acc_m1, acc_y = acc_my[:, 0:R], acc_my[0:C1, R:2 * R], acc_my[:, D:2 * D]
        ctx_in = st.sems(NB)
        (ones_ready, staged, scores_ready, max_ready, probs_ready, probs_turned, turned_copied, mixed_filled,
         inverse_ready, mixed_ready, mixed_turned, mixed_copied, y_filled, added) = st.sems(14)
        block = st.block()

        def steps(eng, body):
            for i in peeled(eng, ROUNDS, 2):
                for u in range(U):
                    body(i, u, i * U + u)
            for u in range(5):
                body(ROUNDS, u, G + u)

        def constant_wait(pe):
            if R < P:
                pe.wait_ge(ones_ready, NB)

        def live(g, lag):
            return lag <= g < G + lag if isinstance(g, int) else True

        @block.sync
        def _(sync):
            st.clear_other_set(sync)
            if K1 > C1:
                sync.wait_ge(ones_ready, NB)
            for i in peeled(sync, ROUNDS, 2):
                for b in range(BL):
                    x, n = b % NB, i * BL + b
                    if later(n, NB):
                        sync.wait_ge(mixed_filled, n * N - (NB - 1) * N)
                    one = bass.ds(n, 1)
                    sync.dma_start(ctx[x][:, :, :], w["ctx"][one].rearrange("o p k c -> p (o k) c")).then_inc(ctx_in[x], 16)
                    sync.dma_start(ct0[x][:, :], w["ctxT"][one, 0:P].rearrange("o p k -> p (o k)")).then_inc(ctx_in[x], 16)
                    sync.dma_start(ct1[x][0:C1, :], w["ctxT"][one, P:CC].rearrange("o p k -> p (o k)")
                                   ).then_inc(ctx_in[x], 16)

        @block.gpsimd
        def _(pool):
            for i in peeled(pool, ROUNDS, 2):
                for b in range(BL):
                    x, n = b % NB, i * BL + b
                    if later(n, NB):
                        pool.wait_ge(scores_ready, n * N - (NB - 1) * N)
                    pool.tensor_copy(a0[x][:, :, :], q0[:, :, bass.ds(n * S, S)]).then_inc(staged, 1)
                    pool.tensor_copy(a1[x][:, :, :], q1[:, :, bass.ds(n * S, S)]).then_inc(staged, 1)

        @block.tensor
        def _(pe):
            if K1 > C1:
                pe.wait_ge(ones_ready, NB)

            def body(i, u, g):
                ends = live(g, 4) and (u - 4) % PAIR == PAIR - 1
                p = i * (U // PAIR) + (u - 3 - PAIR) // PAIR
                if ends:
                    pe.wait_ge(mixed_copied, g - 3)
                    for h in range(heads):
                        pe.matmul(acc_y, m0[:, h, :], out0[:, h, :], start=(h == 0), stop=False)
                        pe.matmul(acc_y, m1[:, h, :], out1[:, h, :], start=False, stop=False)
                    pe.matmul(acc_y, ones[:, :], out_bias[:, :], start=False, stop=True).then_inc(y_filled, 1)
                if live(g, 0):
                    b, r = u // N, u % N
                    x = b % NB
                    if r == 0:
                        pe.wait_ge(staged, (i * BL + b) * 2 + 2)
                        pe.wait_ge(ctx_in[x], i * (48 * BL // NB) + (b // NB) * 48 + 48)
                    if later(g, 2):
                        pe.wait_ge(probs_ready, g - 1)
                    for h in range(2):
                        pe.matmul(acc_s[u % 2][:, halves(h)], a0[x][:, r * HT:(r + 1) * HT, :], ct0[x][:, halves(h)],
                                  start=True, stop=False)
                        ins = pe.matmul(acc_s[u % 2][:, halves(h)], a1[x][:, r * HT:(r + 1) * HT, :],
                                        ct1[x][:, halves(h)], start=False, stop=True)
                    ins.then_inc(scores_ready, 1)
                if live(g, 1):
                    constant_wait(pe)
                    pe.wait_ge(probs_ready, g)
                    if later(g, 2):
                        pe.wait_ge(turned_copied, g - 1)
                    for k in range(KT):
                        ins = pe.transpose(acc_t[:, k, :], probs[(u - 1) % 2][:, tile(k)], ident[0:R, 0:R])
                    ins.then_inc(probs_turned, 1)
                if ends:
                    pe.wait_ge(added, p + 1)
                if live(g, 3) and later(g, 4):
                    pe.wait_ge(mixed_copied, g - 3)
                if live(g, 2):
                    b = (u - 2) % U // N
                    pe.wait_ge(turned_copied, g - 1)
                    if later(g, 3):
                        pe.wait_ge(mixed_ready, g - 2)
                    for k in range(KT):
                        ins = pe.matmul(acc_o[:, 0:CC], probsT[u % 2][:, k, :], ctx[b % NB][:, k, :],
                                        start=(k == 0), stop=(k == KT - 1))
                    ins.then_inc(mixed_filled, 1)
                if live(g, 3):
                    constant_wait(pe)
                    pe.wait_ge(mixed_ready, g - 2)
                    pe.transpose(acc_m0, mixed[(u - 3) % 2][:, 0:P], ident[0:R, 0:R])
                    pe.transpose(acc_m1, mixed[(u - 3) % 2][:, P:CC], ident[0:R, 0:R]).then_inc(mixed_turned, 1)
            steps(pe, body)

        @block.scalar
        def _(act):
            def body(i, u, g):
                if live(g, 0):
                    act.wait_ge(max_ready, g + 1)
                    if later(g, 2):
                        act.wait_ge(probs_turned, g - 1)
                    if later(g, 4):
                        act.wait_ge(inverse_ready, g - 3)
                    act.activation(probs[u % 2][:, :], acc_s[u % 2][:, :], ACT.Exp, bias=negmax[:, u % 4:u % 4 + 1],
                                   accum_out=total[:, u % 4:u % 4 + 1]).then_inc(probs_ready, 1)
                if live(g, 3):
                    v = (u - 3) % U
                    h0, at = v % N * HT, (v // N) % 2 * S
                    act.wait_ge(mixed_turned, g - 2)
                    p = i * (U // PAIR) + (u - 3) // PAIR
                    if v % PAIR == 0 and later(p, 1):
                        act.wait_ge(y_filled, p)
                    act.copy(m0[:, h0:h0 + HT, at:at + S], acc_m0.rearrange("p (h s) -> p h s", s=S))
                    act.copy(m1[:, h0:h0 + HT, at:at + S], acc_m1.rearrange("p (h s) -> p h s", s=S)
                             ).then_inc(mixed_copied, 1)
            steps(act, body)

        @block.vector
        def _(dve):
            if K1 > C1:
                for x in range(NB):
                    dve.memset(ct1[x][C1:K1, :], 1.0).then_inc(ones_ready, 1)

            def body(i, u, g):
                if live(g, 0):
                    dve.wait_ge(scores_ready, g + 1)
                    dve.tensor_reduce(negmax[:, u % 4:u % 4 + 1], acc_s[u % 2][:, :], AX.X, ALU.max, negate=True
                                      ).then_inc(max_ready, 1)
                if live(g, 1):
                    dve.wait_ge(probs_turned, g)
                    if later(g, 3):
                        dve.wait_ge(mixed_filled, g - 2)
                    dve.tensor_copy(probsT[(u - 1) % 2][:, :, :], acc_t[:, :, :]).then_inc(turned_copied, 1)
                if live(g, 4) and (u - 4) % PAIR == PAIR - 1:
                    p = i * (U // PAIR) + (u - 3 - PAIR) // PAIR
                    at = bass.ds(p, 1)
                    dve.wait_ge(y_filled, p + 1)
                    dve.tensor_tensor(X[:, at, :].rearrange("p o d -> p (o d)"), X[:, at, :].rearrange("p o d -> p (o d)"),
                                      acc_y, ALU.add).then_inc(added, 1)
                if live(g, 2):
                    v = (u - 2) % 4
                    dve.wait_ge(probs_ready, g - 1)
                    dve.reciprocal(inverse[:, v:v + 1], total[:, v:v + 1]).then_inc(inverse_ready, 1)
                    dve.wait_ge(inverse_ready, g - 1)
                    dve.wait_ge(mixed_filled, g - 1)
                    if later(g, 4):
                        dve.wait_ge(mixed_turned, g - 3)
                    dve.tensor_scalar(mixed[u % 2][:, :], acc_o[:, 0:CC], inverse[:, v:v + 1], None, ALU.mult
                                      ).then_inc(mixed_ready, 1)
            steps(dve, body)


def one_head_xattn(chip, X, xn, xnT, ident, w):
    with ExitStack() as es:
        sb = buffers(chip, es)
        qT, q0, q1 = sb(P, DC, T), sb(P, 1, T), sb(C1 + 1, 1, T)
        Wq, Wk, bq = sb(P, DC, D), sb(P, DC, CC + 1), sb(P, DC)
        out0, out1, bv, ones = sb(P, 1, D), sb(C1, 1, D), sb(1, D), sb(1, P)
        begin(chip, X, xn, xnT, ident,
              [(Wq[:, :, :], w["Wq"]), (bq[:, :], w["bq"]), (Wk[:, :, :], w["Wk"]), (out0[:, 0, :], w["Wv"][0:P]),
               (out1[:, 0, :], w["Wv"][P:CC]), (bv[:, :], w["bv"])], [(ones[:, :], 1.0)])
        jobs = []
        for m in range(DC):
            for h in range(2):
                def write(eng, acc, m=m, h=h):
                    return eng.tensor_scalar(qT[:, m, halves(h)], acc, bq[:, m:m + 1], D ** -0.5, ALU.add, ALU.mult)
                jobs.append(([(Wq[:, k, tile(m)], xnT[:, k, halves(h)]) for k in range(DC)], (P, HALF), "dve", write))
        matmul_jobs(chip, jobs, [])
        jobs = []
        for h in range(2):
            for dst, c0, c1 in ((q0, 0, P), (q1, P, CC + 1)):
                jobs.append(([(Wk[:, k, c0:c1], qT[:, k, halves(h)]) for k in range(DC)], (c1 - c0, HALF),
                             ("act", "dve")[h], copy_out(dst[:, 0, halves(h)])))
        matmul_jobs(chip, jobs, [])
        attend_context(chip, X, q0, q1, out0, out1, bv, ones, w, 1, ident)


def eight_head_xattn(chip, X, xn, xnT, ident, w):
    HEADS, DH = 8, 64
    INNER = HEADS * DH
    MC = INNER // P
    with ExitStack() as es:
        sb = buffers(chip, es)
        q0, q1 = sb(P, HEADS, T), sb(C1, HEADS, T)
        out0, out1, bo, ones = sb(P, HEADS, D), sb(C1, HEADS, D), sb(1, D), sb(1, P)
        with ExitStack() as inner:
            ib = buffers(chip, inner)
            qT, Wq = ib(P, MC, T), ib(P, DC, INNER)
            WkT, WvT, Wo = ib(P, MC, CC), ib(P, MC, CC), ib(P, MC, D)
            begin(chip, X, xn, xnT, ident,
                  [(Wq[:, :, :], w["Wq"]), (WkT[:, :, :], w["WkT"]), (WvT[:, :, :], w["WvT"]), (Wo[:, :, :], w["Wo"]),
                   (bo[:, :], w["bo"])], [(ones[:, :], 1.0)])
            jobs = []
            for m in range(MC):
                for h in range(2):
                    def write(eng, acc, m=m, h=h):
                        dst = qT[:, m, halves(h)]
                        if is_scalar_engine(eng):
                            return eng.activation(dst, acc, ACT.Copy, scale=DH ** -0.5)
                        return eng.tensor_scalar(dst, acc, DH ** -0.5, None, ALU.mult)
                    jobs.append(([(Wq[:, k, tile(m)], xnT[:, k, halves(h)]) for k in range(DC)], (P, HALF),
                                 ("act", "dve")[h], write))
            matmul_jobs(chip, jobs, [])
            jobs = []
            for n in range(HEADS):
                at = slice((n % 2) * DH, (n % 2) * DH + DH)
                for t, (qd, od, c0, c1) in enumerate(((q0, out0, 0, P), (q1, out1, P, CC))):
                    for h in range(2):
                        jobs.append(([(WkT[at, n // 2, c0:c1], qT[at, n // 2, halves(h)])], (c1 - c0, HALF),
                                     ("act", "dve")[h], copy_out(qd[:, n, halves(h)])))
                    jobs.append(([(WvT[at, n // 2, c0:c1], Wo[at, n // 2, :])], (c1 - c0, D),
                                 ("act", "dve")[t], copy_out(od[:, n, :])))
            matmul_jobs(chip, jobs, [])
        attend_context(chip, X, q0, q1, out0, out1, bo, ones, w, HEADS, ident)


def sixteen_head_xattn(chip, X, xn, xnT, ident, w):
    nc = chip.nc
    HEADS, DH = 16, 16
    N = HEADS // 2
    G = B * N
    BL = 2
    U = BL * N
    R = N // DC
    RING = 2 * R
    LAST = R + 4
    ROUNDS = B // BL
    with ExitStack() as es:
        sb = buffers(chip, es)
        qT, Wq, bq = sb(P, DC, T), sb(P, DC, D), sb(P, DC)
        Wk0, Wk1, bk = sb(P, D), sb(C1, D), sb(P, DC)
        Wv0, Wv1 = sb(P, D), sb(C1 + 1, D)
        Wo, bo, ones = sb(P, DC, D), sb(1, D), sb(1, P)
        pairs_mask = sb(P, N // DC, 2)
        own = sb(P, 2 * DH)
        begin(chip, X, xn, xnT, ident,
              [(Wq[:, :, :], w["Wq"]), (bq[:, :], w["bq"]), (Wk0[:, :], w["Wk"][0:P]), (Wk1[:, :], w["Wk"][P:CC]),
               (bk[:, :], w["bk"]), (Wv0[:, :], w["Wv"][0:P]), (Wv1[:, :], w["Wv"][P:CC + 1]), (Wo[:, :, :], w["Wo"]),
               (bo[:, :], w["bo"]), (pairs_mask[:, :, :], w["pairs_mask"]), (own[:, :], w["own_channels"])],
              [(ones[:, :], 1.0)])
        jobs = []
        for m in range(DC):
            for h in range(2):
                def write(eng, acc, m=m, h=h):
                    return eng.tensor_scalar(qT[:, m, halves(h)], acc, bq[:, m:m + 1], DH ** -0.5, ALU.add, ALU.mult)
                jobs.append(([(Wq[:, k, tile(m)], xnT[:, k, halves(h)]) for k in range(DC)], (P, HALF), "dve", write))
        matmul_jobs(chip, jobs, [])
        with Stage(chip) as st:
            ct0, ct1 = [st.sbuf(P, SK) for _ in range(2)], [st.sbuf(C1 + 1, SK) for _ in range(2)]
            kT = [st.sbuf(P, DC, SK) for _ in range(2)]
            v = [st.sbuf(P, KT, D) for _ in range(2)]
            a = [st.sbuf(P, N, 2, S) for _ in range(2)]
            probs = [st.sbuf(P, SK) for _ in range(2)]
            probsT = st.sbuf(P, RING, KT, P)
            total, inverse = st.sbuf(P, RING), st.sbuf(P, R)
            spread = st.sbuf(P, P)
            scale, scaled = st.sbuf(P, P), st.sbuf(P, P)
            mT = st.sbuf(P, DC, P)
            negmax = st.sbuf(P, 2)
            acc_s = [st.psum(P, SK) for _ in range(2)]
            acc_t = [st.psum(P, HALF) for _ in range(2)]
            acc_kv = st.psum(P, HALF)
            acc_o = st.psum(P, HALF)
            acc_scale = acc_o[:, P:2 * P]
            acc_y = acc_t[1][:, 0:D]
            ctx_in = st.sems(2)
            (ones_ready, staged, scores_ready, max_ready, probs_ready, probs_turned, turned_copied, mixed_filled,
             inverse_ready, spread_ready, scale_ready, scaled_ready, mixed_ready, y_filled, added, kv_filled, kv_ready
             ) = st.sems(17)
            block = st.block()

            def steps(eng, body):
                for i in peeled(eng, ROUNDS, 2, 1):
                    for u in range(U):
                        body(i, u, i * U + u)
                for u in range(LAST - R + 2):
                    body(ROUNDS, u, G + u)

            def live(g, lag):
                return lag <= g < G + lag if isinstance(g, int) else True

            def group(i, u, lag):
                return i * (U // R) + (u - lag) // R

            def q_slot(u):
                return (u - R - 1) % RING // R * R

            def is_first(u, lag):
                return (u - lag) % R == 0

            @block.sync
            def _(sync):
                st.clear_other_set(sync)
                sync.wait_ge(ones_ready, 2)
                for i in peeled(sync, ROUNDS):
                    for x in range(BL):
                        n = i * BL + x
                        if later(n, 2):
                            sync.wait_ge(kv_filled, n * 8 - 8)
                        one = bass.ds(n, 1)
                        sync.dma_start(ct0[x][:, :], w["ctxT"][one, 0:P].rearrange("o p k -> p (o k)")
                                       ).then_inc(ctx_in[x], 16)
                        sync.dma_start(ct1[x][0:C1, :], w["ctxT"][one, P:CC].rearrange("o p k -> p (o k)")
                                       ).then_inc(ctx_in[x], 16)

            @block.gpsimd
            def _(pool):
                def stage(i, x):
                    n = i * BL + x
                    if later(n, 2):
                        pool.wait_ge(scores_ready, n * N - N)
                    for c in range(DC):
                        for s in range(2):
                            pool.tensor_tensor(
                                a[x][:, c * R:(c + 1) * R, s, :],
                                qT[:, c:c + 1, bass.ds(n * S, S)].broadcast_to([P, R, S]),
                                pairs_mask[:, :, s:s + 1].broadcast_to([P, R, S]), ALU.mult).then_inc(staged, 1)

                def body(i, u, g):
                    if u % N == 4 and (not isinstance(g, int) or g < G - N):
                        stage(i + (u // N + 1) // BL, 1 - u // N)
                    if is_first(u, R + 1) and live(g, R + 1):
                        q = group(i, u, R + 1)
                        if later(q, 1):
                            pool.wait_ge(mixed_filled, q)
                        pool.wait_ge(inverse_ready, q + 1)
                        pool.tensor_tensor(spread[:, :].rearrange("p (r d) -> p r d", r=R),
                                           inverse[:, :].unsqueeze(2).broadcast_to([P, R, 2 * DH]),
                                           own[:, :].unsqueeze(1).broadcast_to([P, R, 2 * DH]), ALU.mult
                                           ).then_inc(spread_ready, 1)
                stage(0, 0)
                steps(pool, body)

            def project(pe, x, t, done):
                if t < 4:
                    m, h = t // 2, t % 2
                    pe.matmul(acc_kv[:, :], Wk0[:, tile(m)], ct0[x][:, halves(h)], start=True, stop=False)
                    ins = pe.matmul(acc_kv[:, :], Wk1[:, tile(m)], ct1[x][0:C1, halves(h)], start=False, stop=True)
                else:
                    for s in range(2):
                        k = (t - 4) * 2 + s
                        pe.matmul(acc_kv[:, s * D:(s + 1) * D], ct0[x][:, tile(k)], Wv0[:, :], start=True, stop=False)
                        ins = pe.matmul(acc_kv[:, s * D:(s + 1) * D], ct1[x][:, tile(k)], Wv1[:, :],
                                        start=False, stop=True)
                ins.then_inc(kv_filled, 1)

            def project_out(act, x, t):
                if t < 4:
                    m, h = t // 2, t % 2
                    return act.activation(kT[x][:, m, halves(h)], acc_kv[:, :], ACT.Identity, bias=bk[:, m:m + 1])
                k = (t - 4) * 2
                return act.copy(v[x][:, k:k + 2, :], acc_kv[:, :].rearrange("p (k d) -> p k d", k=2))

            @block.tensor
            def _(pe):
                pe.wait_ge(ones_ready, 2)
                pe.wait_ge(ctx_in[0], 32)
                for t in range(8):
                    if t:
                        pe.wait_ge(kv_ready, t)
                    project(pe, 0, t, t)

                def body(i, u, g):
                    x, r = u // N, u % N
                    if live(g, 0):
                        if r == 0:
                            pe.wait_ge(staged, (i * BL + x) * 4 + 4)
                            pe.wait_ge(kv_ready, (i * BL + x) * 8 + 8)
                        if later(g, 2):
                            pe.wait_ge(probs_ready, g - 1)
                        for h in range(2):
                            ins = pe.matmul(acc_s[u % 2][:, halves(h)], a[x][:, r, :, :], kT[x][:, r // 4, halves(h)],
                                            start=True, stop=True)
                        ins.then_inc(scores_ready, 1)
                    if live(g, 1):
                        pe.wait_ge(probs_ready, g)
                        for s in range(2):
                            if later(g, 2):
                                pe.wait_ge(turned_copied, 2 * g - 3 + s)
                            if s == 1 and (u - LAST - 2) % U == U - R and later(g, U + LAST - R + 2):
                                pe.wait_ge(added, i + (u - LAST - 2 - (U - R)) // U + 1)
                            for k in range(4):
                                ins = pe.transpose(acc_t[s][:, tile(k)], probs[(u - 1) % 2][:, tile(4 * s + k)],
                                                   ident[:, :])
                            ins.then_inc(probs_turned, 1)
                    if live(g, R + 1):
                        j, q = (u - R - 1) % R, group(i, u, R + 1)
                        slot, xq = q_slot(u), (u - R - 1) % U // N
                        if j == 0:
                            pe.wait_ge(turned_copied, 2 * g - 2)
                            if later(q, 1):
                                pe.wait_ge(mixed_ready, q)
                        for k in range(2 * j, 2 * j + 2):
                            for t in range(R):
                                c0 = (u - R - 1) % N // R * P + t * 2 * DH
                                ins = pe.matmul(acc_o[t * 2 * DH:(t + 1) * 2 * DH, 0:P], v[xq][:, k, c0:c0 + 2 * DH],
                                                probsT[:, slot + t, k, :], start=(k == 0), stop=(k == KT - 1))
                        if j == R - 1:
                            pe.wait_ge(spread_ready, q + 1)
                            ins = pe.matmul(acc_scale, spread[:, :], ident[:, :], start=True, stop=True)
                            ins.then_inc(mixed_filled, 1)
                    if live(g, 0) and (not isinstance(g, int) or g < G - N):
                        if r == 0:
                            pe.wait_ge(ctx_in[1 - x], (i + (1 if x == 1 else 0)) * 32 + 32)
                        pe.wait_ge(kv_ready, g + 8)
                        project(pe, 1 - x, r, g)
                    if (u - LAST - 1) % U == U - R and live(g, LAST + 1 + U - R):
                        p = i + (u - LAST - 1 - (U - R)) // U
                        pe.wait_ge(mixed_ready, p * (U // R) + U // R)
                        if live(g, 1):
                            pe.wait_ge(turned_copied, 2 * g)
                        for c in range(DC):
                            pe.matmul(acc_y, mT[:, c, :], Wo[:, c, :], start=(c == 0), stop=False)
                        pe.matmul(acc_y, ones[:, :], bo[:, :], start=False, stop=True).then_inc(y_filled, 1)
                steps(pe, body)

            @block.scalar
            def _(act):
                for t in range(8):
                    act.wait_ge(kv_filled, t + 1)
                    project_out(act, 0, t).then_inc(kv_ready, 1)

                def body(i, u, g):
                    x, r = u // N, u % N
                    if live(g, 0):
                        act.wait_ge(max_ready, g + 1)
                        if later(g, 2):
                            act.wait_ge(probs_turned, 2 * g - 2)
                        if u % R == 0 and later(g, RING):
                            act.wait_ge(inverse_ready, group(i, u, RING) + 1)
                        act.activation(probs[u % 2][:, :], acc_s[u % 2][:, :], ACT.Exp,
                                       bias=negmax[:, u % 2:u % 2 + 1], accum_out=total[:, u % RING:u % RING + 1]
                                       ).then_inc(probs_ready, 1)
                    if live(g, 0) and (not isinstance(g, int) or g < G - N):
                        act.wait_ge(kv_filled, g + 9)
                        if later(g, N):
                            if r < 4:
                                act.wait_ge(scores_ready, i * U + x * N)
                            elif r == 4:
                                act.wait_ge(mixed_filled, (i * BL + x) * (N // R))
                        project_out(act, 1 - x, r).then_inc(kv_ready, 1)
                steps(act, body)

            @block.vector
            def _(dve):
                for x in range(2):
                    dve.memset(ct1[x][C1:C1 + 1, :], 1.0).then_inc(ones_ready, 1)

                def body(i, u, g):
                    if live(g, 0):
                        dve.wait_ge(scores_ready, g + 1)
                        if later(g, 2):
                            dve.wait_ge(probs_ready, g - 1)
                        dve.tensor_reduce(negmax[:, u % 2:u % 2 + 1], acc_s[u % 2][:, :], AX.X, ALU.max, negate=True
                                          ).then_inc(max_ready, 1)
                    if live(g, 1):
                        for s in range(2):
                            dve.wait_ge(probs_turned, 2 * g - 1 + s)
                            if is_first(u, 1) and later(g, RING + 1) and s == 0:
                                dve.wait_ge(mixed_filled, group(i, u, RING + 1) + 1)
                            dve.tensor_copy(probsT[:, (u - 1) % RING, 4 * s:4 * s + 4, :],
                                            acc_t[s][:, :].rearrange("p (k r) -> p k r", r=P)
                                            ).then_inc(turned_copied, 1)
                    if is_first(u, R + 1) and live(g, R + 1):
                        q = group(i, u, R + 1)
                        c = (u - R - 1) % RING
                        dve.wait_ge(probs_ready, q * R + R)
                        if later(q, 1):
                            dve.wait_ge(spread_ready, q)
                        dve.reciprocal(inverse[:, :], total[:, c:c + R]).then_inc(inverse_ready, 1)
                    if is_first(u, LAST) and live(g, LAST):
                        q = group(i, u, LAST)
                        c, xb = (u - LAST) % N // R, (u - LAST) % U // N
                        dve.wait_ge(mixed_filled, q + 1)
                        dve.tensor_copy(scale[:, :], acc_scale).then_inc(scale_ready, 1)
                        dve.wait_ge(scale_ready, q + 1)
                        dve.tensor_tensor(scaled[:, :], acc_o[:, 0:P], scale[:, :], ALU.mult).then_inc(scaled_ready, 1)
                        dve.wait_ge(scaled_ready, q + 1)
                        dve.tensor_tensor(mT[:, c, xb * S:(xb + 1) * S], scaled[:, 0:S], scaled[:, S:2 * S], ALU.add
                                          ).then_inc(mixed_ready, 1)
                    if (u - LAST - 1) % U == U - R and live(g, LAST + 1 + U - R):
                        p = i + (u - LAST - 1 - (U - R)) // U
                        at = bass.ds(p, 1)
                        dve.wait_ge(y_filled, p + 1)
                        dve.tensor_tensor(X[:, at, :].rearrange("p o d -> p (o d)"),
                                          X[:, at, :].rearrange("p o d -> p (o d)"), acc_y, ALU.add
                                          ).then_inc(added, 1)
                steps(dve, body)


def log1p_coefficients():
    import numpy as np
    n = 64
    e = (1 - np.cos((np.arange(n) + 0.5) * np.pi / n)) / 2
    fit = np.polynomial.Polynomial.fit(e, np.log1p(e) / e, 9, domain=[0, 1]).convert()
    return [float(c) for c in fit.coef]


def selective_scan(chip, X, xn, xnT, ident, w):
    nc = chip.nc
    CH, NS = 512, 16
    C = CH // P
    with ExitStack() as es:
        sb = buffers(chip, es)
        u, gate, delta, du = (sb(P, C, T) for _ in range(4))
        A, Dp, cw, cb, dtb = sb(P, NS, C), sb(P, C), sb(P, C, 3), sb(P, C), sb(P, C)
        Wo = sb(P, C, D)
        early = es.enter_context(ExitStack())
        Wx, Wdt = (buffers(chip, early)(P, C, n) for n in (CH + 2 * NS, CH))
        rows_dram = nc.dram_tensor("state_rows", [2 * NS, T], F32, kind="Internal").ap()

        with ExitStack() as inner:
            ib = buffers(chip, inner)
            up, Win = ib(P, C, B, S + 2), ib(P, DC, 2 * CH)
            begin(chip, X, xn, xnT, ident,
                  [(Win[:, :, :], w["in_proj_w"]), (cw[:, :, :], w["conv_w"]), (cb[:, :], w["conv_b"]),
                   (A[:, :, :], w["A_log"]), (Dp[:, :], w["D_param"]), (dtb[:, :], w["dt_proj_b"]),
                   (Wx[:, :, :], w["x_proj_w"]), (Wdt[:, :, :], w["dt_proj_w"]), (Wo[:, :, :], w["out_proj_w"])],
                  [(up[:, :, :, 0:1], 0.0), (up[:, :, :, S + 1:S + 2], 0.0)])
            jobs = []
            for m in range(2 * C):
                for h in range(2):
                    def write(eng, acc, m=m, h=h):
                        if m < C:
                            return eng.tensor_copy(up[:, m, 8 * h:8 * h + 8, 1:S + 1],
                                                   acc.rearrange("p (b s) -> p b s", s=S))
                        return eng.activation(gate[:, m - C, halves(h)], acc, ACT.Silu)
                    jobs.append(([(Win[:, k, tile(m)], xnT[:, k, halves(h)]) for k in range(DC)], (P, HALF),
                                 "dve" if m < C else "act", write))

            def convolve(dve, done):
                c = Chain(dve, done["steps"])
                c.link(dve.engine_nop())
                for m in range(C):
                    t = delta[:, m, :].rearrange("p (b s) -> p b s", s=S)
                    c.link(dve.tensor_scalar(t, up[:, m, :, 0:S], cw[:, m, 0:1], cb[:, m:m + 1], ALU.mult, ALU.add))
                    for k in (1, 2):
                        c.link(dve.scalar_tensor_tensor(out=t, in0=up[:, m, :, k:k + S], scalar=cw[:, m, k:k + 1],
                                                        in1=t, op0=ALU.mult, op1=ALU.add))

            def activate(act, done):
                for m in range(C):
                    act.wait_ge(done["steps"], 3 * m + 4)
                    act.activation(u[:, m, :], delta[:, m, :], ACT.Silu)
                act.activation(A[:, :, :], A[:, :, :], ACT.Exp).then_inc(done["act_steps"], 1)
                act.wait_ge(done["act_steps"], 1)
                act.activation(A[:, :, :], A[:, :, :], ACT.Copy, scale=-1.0)
            matmul_jobs(chip, jobs, [], then={"dve": convolve, "act": activate})

        with ExitStack() as inner:
            ib = buffers(chip, inner)
            low, bc = ib(P, C, T), ib(2 * NS, T)
            jobs = []
            for h in range(2):
                for m in range(C + 1):
                    r = P if m < C else 2 * NS
                    dst = low[:, m, halves(h)] if m < C else bc[:, halves(h)]
                    jobs.append(([(Wx[:, k, m * P:m * P + r], u[:, k, halves(h)]) for k in range(C)], (r, HALF),
                                 ("act", "dve")[m % 2], copy_out(dst)))
            matmul_jobs(chip, jobs, [])
            e, p = (ib(P, C, T) for _ in range(2))
            coef = log1p_coefficients()
            jobs = []
            for m in range(C):
                for h in range(2):
                    def write(eng, acc, m=m, h=h):
                        b = dtb[:, m:m + 1]
                        em = e[:, m, halves(h)]
                        eng.activation(delta[:, m, halves(h)], acc, ACT.Identity, bias=b)
                        eng.activation(em, acc, ACT.Abs, bias=b).then_inc(chip.abs_ready, 1)
                        eng.wait_ge(chip.abs_ready, 2 * m + h + 1)
                        return eng.activation(em, em, ACT.Exp, scale=-1.0)
                    jobs.append(([(Wdt[:, k, tile(m)], low[:, k, halves(h)]) for k in range(C)], (P, HALF), "act",
                                 write))

            def softplus(eng, chain, done, m, at):
                def both(out, in0, scalar, in1, op0, op1):
                    if eng.engine == mybir.EngineType.Pool:
                        chain.link(eng.tensor_scalar(out, in0, scalar, None, op0))
                        chain.link(eng.tensor_tensor(out, out, in1, op1))
                    else:
                        chain.link(eng.scalar_tensor_tensor(out=out, in0=in0, scalar=scalar, in1=in1, op0=op0, op1=op1))
                em, pm, z = (t[:, m, at] for t in (e, p, delta))
                eng.wait_ge(done["act"], 2 * m + 2)
                chain.link(eng.tensor_scalar(pm, em, coef[-1], None, ALU.mult))
                for k in coef[-2::-1]:
                    both(pm, pm, k, em, ALU.add, ALU.mult)
                both(z, z, 0.0, pm, ALU.max, ALU.add)

            SPLIT = 1
            LINKS = len(coef) + 1

            def by_vector(dve, done):
                chain = Chain(dve, done["steps"])
                for m in range(C):
                    softplus(dve, chain, done, m, halves(0) if m == SPLIT else slice(0, T))

            def by_pool(pool, done):
                chain = Chain(pool, done["pool_steps"])
                softplus(pool, chain, done, SPLIT, halves(1))
                for m in range(C):
                    pool.wait_ge(done["steps"], LINKS * (m + 1))
                    chain.link(pool.tensor_tensor(du[:, m, :], delta[:, m, :], u[:, m, :], ALU.mult))
            matmul_jobs(chip, jobs, [(rows_dram, bc[:, :])], then={"dve": by_vector, "pool": by_pool})
        early.close()

        ROUNDS = NS // 2
        with Stage(chip) as st:
            brow, crow = ([st.sbuf(P, T) for _ in range(2)] for _ in range(2))
            acur = [st.sbuf(P, C) for _ in range(2)]
            decay, drive, state, out = ([st.sbuf(P, T) for _ in range(C)] for _ in range(4))
            acc = [[st.psum(P, HALF) for _ in range(2)] for _ in range(C)]
            rows_in = st.sems(2)
            a_ready, exp_done, decay_ready, drive_ready, scanned, out_ready, summed, y_steps = st.sems(8)
            block = st.block()

            def rounds(eng):
                for i in peeled(eng, ROUNDS, 1, 1):
                    for x in range(2):
                        for c in range(C):
                            yield i, x, i * 2 + x, c, (i * 2 + x) * C + c

            @block.sync
            def _(sync):
                st.clear_other_set(sync)
                for i in peeled(sync, ROUNDS, 1, 1):
                    for x in range(2):
                        s = i * 2 + x
                        if later(s, 2):
                            sync.wait_ge(out_ready, s * C - C)
                        for dst, base in ((brow, 0), (crow, NS)):
                            sync.dma_start(dst[x][:, :], rows_dram[bass.ds(s + base, 1), :].broadcast_to([P, T])
                                           ).then_inc(rows_in[x], 16)

            @block.gpsimd
            def _(pool):
                for i, x, s, c, n in rounds(pool):
                    if c == 0:
                        pool.wait_ge(rows_in[x], i * 32 + 32)
                    pool.wait_ge(scanned, n + 1)
                    if later(n, C):
                        pool.wait_ge(summed, n - C + 1)
                    pool.tensor_tensor(out[c][:, :], state[c][:, :], crow[x][:, :], ALU.mult).then_inc(out_ready, 1)

            @block.scalar
            def _(act):
                for i, x, s, c, n in rounds(act):
                    if c == 0:
                        act.copy(acur[x][:, :], A[:, bass.ds(s, 1), :].rearrange("p o c -> p (o c)")
                                 ).then_inc(a_ready, 1)
                        act.wait_ge(a_ready, s + 1)
                    if later(n, C):
                        act.wait_ge(scanned, n - C + 1)
                    act.activation(decay[c][:, :], delta[:, c, :], ACT.Exp, scale=acur[x][:, c:c + 1]
                                   ).then_inc(exp_done, 1)

            @block.vector
            def _(dve):
                def make_drive(i, x, c, n):
                    if c == 0:
                        dve.wait_ge(rows_in[x], i * 32 + 32)
                    if later(n, C):
                        dve.wait_ge(scanned, n - C + 1)
                    dve.tensor_tensor(drive[c][:, :], du[:, c, :], brow[x][:, :], ALU.mult).then_inc(drive_ready, 1)

                make_drive(0, 0, 0, 0)
                for i, x, s, c, n in rounds(dve):
                    dve.wait_ge(exp_done, n + 1)
                    dve.memset(decay[c][:, :].rearrange("p (b s) -> p b s", s=S)[:, :, 0:1], 0.0
                               ).then_inc(decay_ready, 1)
                    if not isinstance(n, int) or n < NS * C - 1:
                        step = x * C + c + 1
                        make_drive(i + step // (2 * C), step // C % 2, step % C, n + 1)
                    dve.wait_ge(drive_ready, n + 1)
                    dve.wait_ge(decay_ready, n + 1)
                    if later(n, C):
                        dve.wait_ge(out_ready, n - C + 1)
                    dve.tensor_tensor_scan(state[c][:, :], decay[c][:, :], drive[c][:, :], 0.0,
                                           ALU.mult, ALU.add).then_inc(scanned, 1)
                dve.wait_ge(summed, NS * C)
                ch = Chain(dve, y_steps)
                for c in range(C):
                    for h in range(2):
                        t = u[:, c, halves(h)]
                        ch.link(dve.scalar_tensor_tensor(out=t, in0=t, scalar=Dp[:, c:c + 1], in1=acc[c][h][:, :],
                                                         op0=ALU.mult, op1=ALU.add))
                    dve.tensor_tensor(u[:, c, :], u[:, c, :], gate[:, c, :], ALU.mult)

            @block.tensor
            def _(pe):
                for i, x, s, c, n in rounds(pe):
                    pe.wait_ge(out_ready, n + 1)
                    first = isinstance(s, int) and s == 0
                    last = isinstance(s, int) and s == NS - 1
                    for h in range(2):
                        ins = pe.matmul(acc[c][h][:, :], ident[:, :], out[c][:, halves(h)], start=first, stop=last)
                    ins.then_inc(summed, 1)

        jobs = []
        for j in range(NT):
            def write(eng, acc, j=j):
                return eng.tensor_tensor(X[:, j, :], X[:, j, :], acc, ALU.add)
            jobs.append(([(u[:, k, tile(j)], Wo[:, k, :]) for k in range(C)], (P, D), "dve", write))
        matmul_jobs(chip, jobs, [])


def turn_to_features(chip, pairs, ident):
    with Stage(chip) as st:
        banks = [st.psum(P, HALF) for _ in range(6)]
        turned, act_done, dve_done = st.sems(3)
        block = st.block()
        units = [(src, dst, c, h) for src, dst in pairs for c in range(DC) for h in range(2)]

        @block.sync
        def _(sync):
            st.clear_other_set(sync)

        @block.tensor
        def _(pe):
            for n, (src, dst, c, h) in enumerate(units):
                if n >= 6:
                    pe.wait_ge((act_done, dve_done)[n % 2], (n - 6) // 2 + 1)
                for q in range(4):
                    ins = pe.transpose(banks[n % 6][:, tile(q)], src[:, 4 * h + q, tile(c)], ident[:, :])
                ins.then_inc(turned, 1)

        @block.scalar
        def _(act):
            for n, (src, dst, c, h) in enumerate(units):
                if n % 2 == 0:
                    act.wait_ge(turned, n + 1)
                    act.copy(dst[:, c, halves(h)], banks[n % 6][:, :]).then_inc(act_done, 1)

        @block.vector
        def _(dve):
            for n, (src, dst, c, h) in enumerate(units):
                if n % 2 == 1:
                    dve.wait_ge(turned, n + 1)
                    dve.tensor_copy(dst[:, c, halves(h)], banks[n % 6][:, :]).then_inc(dve_done, 1)


def local_attention(chip, X, xn, xnT, ident, w):
    nc = chip.nc
    DH = 16
    N = D // DH // 2
    BL = 2
    ROUNDS = B // BL
    with ExitStack() as es:
        sb = buffers(chip, es)
        v = sb(S, B, D)
        qT, kT, Wp = sb(P, DC, T), sb(P, DC, T), sb(P, DC, D)
        pairs_mask, own, causal = sb(P, N // DC, 2), sb(P, 2 * DH), sb(P, S)
        with ExitStack() as inner:
            ib = buffers(chip, inner)
            W, lnw = ib(P, DC, 3 * D), ib(P, D)
            qk = [ib(P, NT, D) for _ in range(2)]
            sq = ib(P, NT, D)
            ms, std = ib(P, 2, NT), ib(P, 2, NT)
            begin(chip, X, xn, xnT, ident,
                  [(W[:, :, :], w["w_qkv"]), (Wp[:, :, :], w["w_proj"]), (lnw[:, :], w["ln_w"].partition_broadcast(P)),
                   (pairs_mask[:, :, :], w["pairs_mask"]), (own[:, :], w["own_channels"]),
                   (causal[:, :], w["causal"])])
            jobs = []
            for n in range(2):
                for j in range(NT):
                    jobs.append(([(xnT[:, k, tile(j)], W[:, k, n * D:(n + 1) * D]) for k in range(DC)], (P, D),
                                 ("act", "dve")[n], copy_out(qk[n][:, j, :])))
            for b in range(B):
                jobs.append(([(xnT[:, k, b * S:(b + 1) * S], W[:, k, 2 * D:]) for k in range(DC)], (S, D),
                             "act", copy_out(v[:, b, :])))

            def normalise(dve, done):
                c = Chain(dve, done["steps"])
                c.link(dve.engine_nop())
                dve.wait_ge(done["act"], 2 * NT)
                for n in range(2):
                    c.link(dve.tensor_tensor(sq[:, :, :], qk[n][:, :, :], qk[n][:, :, :], ALU.mult))
                    c.link(dve.tensor_reduce(ms[:, n, :], sq[:, :, :], AX.X, ALU.add))
                c.link(dve.tensor_scalar(ms[:, :, :], ms[:, :, :], 1.0 / D, 1e-6, ALU.mult, ALU.add))
                dve.wait_ge(done["act_steps"], 1)
                c.link(dve.reciprocal(std[:, :, :], std[:, :, :]))
                for n in range(2):
                    c.link(dve.tensor_tensor(qk[n][:, :, :], qk[n][:, :, :],
                                             std[:, n, :].unsqueeze(2).broadcast_to([P, NT, D]), ALU.mult))
                    dve.tensor_tensor(qk[n][:, :, :], qk[n][:, :, :],
                                      lnw[:, :].unsqueeze(1).broadcast_to([P, NT, D]), ALU.mult)

            def root(act, done):
                act.wait_ge(done["steps"], 6)
                act.activation(std[:, :, :], ms[:, :, :], ACT.Sqrt).then_inc(done["act_steps"], 1)
            matmul_jobs(chip, jobs, [], then={"dve": normalise, "act": root})
            turn_to_features(chip, ((qk[0], qT), (qk[1], kT)), ident)

        with Stage(chip) as st:
            a = [st.sbuf(P, N, 2, S) for _ in range(2)]
            sc = [st.sbuf(P, N, S) for _ in range(2)]
            probsT = [st.sbuf(S, N, P) for _ in range(2)]
            mx, total = ([st.sbuf(P, N) for _ in range(2)] for _ in range(2))
            spread = [st.sbuf(P, D) for _ in range(2)]
            values = [st.sbuf(S, D) for _ in range(2)]
            scale, scaled = st.sbuf(P, D), st.sbuf(P, D)
            mT = st.sbuf(P, DC, P)
            acc_s = [st.psum(P, N, S) for _ in range(2)]
            acc_t = st.psum(S, N, P)
            acc_o, acc_y = st.psum(P, HALF), st.psum(P, HALF)
            acc_mixed, acc_scale = acc_o[:, 0:D], acc_o[:, D:2 * D]
            (always, staged, scored, shifted, exp_done, turned, turned_copied, mixed_filled, mixed_ready,
             values_ready, spread_ready, scale_ready, scaled_ready, y_filled, added, score_steps, norm_steps
             ) = st.sems(17)
            block = st.block()

            def steps(eng, body):
                for i in peeled(eng, ROUNDS, 3):
                    for x in range(BL):
                        body(i, x, i * BL + x)
                for x in range(2):
                    body(ROUNDS, x, B + x)

            def live(g, lag):
                return lag <= g < B + lag if isinstance(g, int) else True

            @block.sync
            def _(sync):
                st.clear_other_set(sync)

            @block.gpsimd
            def _(pool):
                def body(i, x, g):
                    if live(g, 0):
                        if later(g, 2):
                            pool.wait_ge(scored, g - 1)
                        for c in range(DC):
                            for s in range(2):
                                q = N // DC
                                pool.tensor_tensor(
                                    a[x][:, c * q:(c + 1) * q, s, :],
                                    qT[:, c:c + 1, bass.ds(g * S, S)].broadcast_to([P, q, S]),
                                    pairs_mask[:, :, s:s + 1].broadcast_to([P, q, S]), ALU.mult).then_inc(staged, 1)
                    if live(g, 1):
                        if later(g, 3):
                            pool.wait_ge(mixed_filled, g - 2)
                        pool.tensor_copy(values[(x + 1) % 2][:, :], v[:, bass.ds(g - 1, 1), :].rearrange(
                            "p o d -> p (o d)")).then_inc(values_ready, 1)
                steps(pool, body)

            @block.tensor
            def _(pe):
                pe.wait_ge(always, 1)

                def body(i, x, g):
                    if live(g, 0):
                        pe.wait_ge(staged, g * 4 + 4)
                        if later(g, 2):
                            pe.wait_ge(shifted, g - 1)
                        for r in range(N):
                            ins = pe.matmul(acc_s[x % 2][:, r, :], a[x % 2][:, r, :, :],
                                            kT[:, r // 4, bass.ds(g * S, S)], start=True, stop=True)
                        ins.then_inc(scored, 1)
                    if live(g, 1):
                        pe.wait_ge(always, 1)
                        pe.wait_ge(exp_done, g)
                        if later(g, 2):
                            pe.wait_ge(turned_copied, g - 1)
                        for r in range(N):
                            ins = pe.transpose(acc_t[:, r, :], sc[(x + 1) % 2][:, r, :], ident[:, :])
                        ins.then_inc(turned, 1)
                    if live(g, 2):
                        pe.wait_ge(turned_copied, g - 1)
                        if later(g, 3):
                            pe.wait_ge(mixed_ready, g - 2)
                        pe.wait_ge(values_ready, g - 1)
                        pe.wait_ge(spread_ready, g - 1)
                        for c in range(DC):
                            pe.matmul(acc_scale[:, tile(c)], spread[x % 2][:, tile(c)], ident[:, :],
                                      start=True, stop=True)
                        for c in range(DC):
                            for t in range(N // DC):
                                r = c * (N // DC) + t
                                ins = pe.matmul(acc_mixed[t * 2 * DH:(t + 1) * 2 * DH, tile(c)],
                                                values[x % 2][:, r * 2 * DH:(r + 1) * 2 * DH],
                                                probsT[x % 2][:, r, :], start=True, stop=True)
                        ins.then_inc(mixed_filled, 1)
                        if x % 2 == 1:
                            pe.wait_ge(mixed_ready, g - 1)
                            if later(g, 4):
                                pe.wait_ge(added, i - 1)
                            for c in range(DC):
                                ins = pe.matmul(acc_y[:, 0:D], mT[:, c, :], Wp[:, c, :], start=(c == 0),
                                                stop=(c == DC - 1))
                            ins.then_inc(y_filled, 1)
                steps(pe, body)

            @block.scalar
            def _(act):
                def body(i, x, g):
                    if live(g, 0):
                        act.wait_ge(shifted, g + 1)
                        act.activation(sc[x % 2][:, :, :], sc[x % 2][:, :, :], ACT.Exp).then_inc(exp_done, 1)
                    if live(g, 1):
                        act.wait_ge(turned, g)
                        if later(g, 3):
                            act.wait_ge(mixed_filled, g - 2)
                        act.copy(probsT[(x + 1) % 2][:, :, :], acc_t[:, :, :]).then_inc(turned_copied, 1)
                steps(act, body)

            @block.vector
            def _(dve):
                dve.memset(total[0][:, :], 0.0).then_inc(always, 1)

                def body(i, x, g):
                    if live(g, 0):
                        t, m = sc[x % 2], mx[x % 2]
                        c = Chain(dve, score_steps, g * 2)
                        dve.wait_ge(scored, g + 1)
                        if later(g, 2):
                            dve.wait_ge(turned, g - 1)
                        c.link(dve.scalar_tensor_tensor(out=t[:, :, :], in0=acc_s[x % 2][:, :, :], scalar=DH ** -0.5,
                                                        in1=causal[:, :].unsqueeze(1).broadcast_to([P, N, S]),
                                                        op0=ALU.mult, op1=ALU.add))
                        c.link(dve.tensor_reduce(m[:, :], t[:, :, :], AX.X, ALU.max))
                        dve.tensor_tensor(t[:, :, :], t[:, :, :], m[:, :].unsqueeze(2).broadcast_to([P, N, S]),
                                          ALU.subtract).then_inc(shifted, 1)
                    if live(g, 1):
                        y = (x + 1) % 2
                        c = Chain(dve, norm_steps, g * 2 - 2)
                        dve.wait_ge(exp_done, g)
                        c.link(dve.tensor_reduce(total[y][:, :], sc[y][:, :, :], AX.X, ALU.add))
                        c.link(dve.reciprocal(total[y][:, :], total[y][:, :]))
                        if later(g, 3):
                            dve.wait_ge(mixed_filled, g - 2)
                        dve.tensor_tensor(spread[y][:, :].rearrange("p (r d) -> p r d", r=N),
                                          total[y][:, :].unsqueeze(2).broadcast_to([P, N, 2 * DH]),
                                          own[:, :].unsqueeze(1).broadcast_to([P, N, 2 * DH]), ALU.mult
                                          ).then_inc(spread_ready, 1)
                    if live(g, 2):
                        y = x % 2
                        dve.wait_ge(mixed_filled, g - 1)
                        dve.tensor_copy(scale[:, :], acc_scale).then_inc(scale_ready, 1)
                        dve.wait_ge(scale_ready, g - 1)
                        dve.tensor_tensor(scaled[:, :], acc_mixed, scale[:, :], ALU.mult).then_inc(scaled_ready, 1)
                        dve.wait_ge(scaled_ready, g - 1)
                        if y == 0 and later(g, 4):
                            dve.wait_ge(y_filled, i - 1)
                        by_side = scaled[:, :].rearrange("p (c x s) -> p c x s", c=DC, x=2)
                        dve.tensor_tensor(mT[:, :, y * S:(y + 1) * S], by_side[:, :, 0, :], by_side[:, :, 1, :], ALU.add
                                          ).then_inc(mixed_ready, 1)
                        if y == 1:
                            at = bass.ds(i - 1, 1)
                            dve.wait_ge(y_filled, i)
                            dve.tensor_tensor(X[:, at, :].rearrange("p o d -> p (o d)"),
                                              X[:, at, :].rearrange("p o d -> p (o d)"), acc_y[:, 0:D], ALU.add
                                              ).then_inc(added, 1)
                steps(dve, body)


def program(nc, w, out, stages):
    chip = Chip(nc)
    with ExitStack() as es:
        X = es.enter_context(nc.sbuf_tensor("x_tokens", [P, NT, D], F32))
        xn = es.enter_context(nc.sbuf_tensor("xn_tokens", [P, NT, D], F32))
        xnT = es.enter_context(nc.sbuf_tensor("xn_features", [P, DC, T], F32))
        ident = es.enter_context(nc.sbuf_tensor("identity", [P, P], F32))
        with Stage(chip) as st:
            loaded = st.sem()
            block = st.block()

            @block.sync
            def _(sync):
                st.clear_other_set(sync)
                sync.dma_start(X[:, :, :], w["x"]).then_inc(loaded, 16)
                sync.dma_start(ident[:, :], w["identity"]).then_inc(loaded, 16)
                sync.wait_ge(loaded, 32)

        def sub(prefix):
            own = {k[len(prefix):]: v for k, v in w.items() if k.startswith(prefix)}
            return {**own, "ctx": w["ctx"], "ctxT": w["ctxT"]}

        for s in stages:
            LAYERS[s](chip, X, xn, xnT, ident, sub(s + "_"))

        with Stage(chip) as st:
            stored = nc.alloc_semaphore("x_stored")
            block = st.block()

            @block.sync
            def _(sync):
                st.clear_other_set(sync)
                sync.dma_start(out, X[:, :, :]).then_inc(stored, 16)
                sync.wait_ge(stored, 16)


LAYERS = {"L0_attn": local_attention, "L3_attn": selective_scan, "L1_xattn": sixteen_head_xattn, "L0_xattn": one_head_xattn, "L2_xattn": eight_head_xattn, "L3_xattn": eight_head_xattn, "L0_ffn": shared_and_routed, "L1_ffn": top1_experts, "L2_ffn": capacity_experts, "L2_attn": lru, "L3_ffn": binary_mlp, "L1_attn": conv_pool_mlp}
STAGES = ["L0_xattn", "L0_attn", "L0_ffn", "L1_xattn", "L1_attn", "L1_ffn", "L2_xattn", "L2_attn", "L2_ffn", "L3_xattn", "L3_attn", "L3_ffn"]


def layouts(inputs):
    import numpy as np
    a = {k: np.asarray(v) for k, v in inputs.items()}

    def kpn(m):
        return m.reshape(-1, P, m.shape[-1]).transpose(1, 0, 2)

    o = {"x": kpn(a["x"].reshape(T, D)), "identity": np.eye(P, dtype=np.float32)}
    for n in ("theta_log", "nu_log", "gamma_log"):
        o["L2_attn_" + n] = a["L2_attn_" + n].reshape(P, 1)
    for n in ("B_re", "B_im"):
        o["L2_attn_" + n] = kpn(a["L2_attn_" + n].T)
    for n in ("C_re", "C_im"):
        o["L2_attn_" + n] = a["L2_attn_" + n].T
    o["L2_attn_D"] = a["L2_attn_D"]
    for n in ("k0", "k1", "k2"):
        o["L3_ffn_" + n] = np.ascontiguousarray(kpn(a["L3_ffn_" + n])).view(np.int32)
    for n in ("s0", "s1", "s2"):
        o["L3_ffn_" + n] = a["L3_ffn_" + n].reshape(1)

    def cols(v):
        return v.reshape(-1, P).T

    p = "L1_attn_"
    o[p + "conv_w"] = a[p + "conv_w"].reshape(4, 64, 64, 4).transpose(0, 2, 3, 1)
    o[p + "conv_b"] = cols(a[p + "conv_b"])
    for n in ("conv", "attn", "boom"):
        for x in "gb":
            o[f"{p}ln_{n}_{x}"] = cols(a[f"{p}ln_{n}_{x}"])
    for x in "qkv":
        o[p + "W" + x] = kpn(a[p + "W" + x].T)
        o[p + "b" + x] = cols(a[p + "b" + x])
    o[p + "inv_len"] = (1.0 / np.arange(1, S + 1)).astype(np.float32)
    o[p + "Wb"], o[p + "Wu"] = kpn(a[p + "Wb"].T), kpn(a[p + "Wu"].T)
    o[p + "bb"], o[p + "bu"] = cols(a[p + "bb"]), a[p + "bu"].reshape(1, D)
    c = a["ctx_768"]
    o["ctx"], o["ctxT"] = c.reshape(B, KT, P, CC).transpose(0, 2, 1, 3), c.transpose(0, 2, 1)
    p = "L0_xattn_"
    o[p + "Wq"], o[p + "bq"] = kpn(a[p + "Wq"].T), cols(a[p + "bq"])
    o[p + "Wk"] = kpn(np.concatenate([a[p + "Wk"], a[p + "bk"].reshape(D, 1)], axis=1))
    o[p + "Wv"], o[p + "bv"] = a[p + "Wv"].T, a[p + "bv"].reshape(1, D)
    for p in ("L2_xattn_", "L3_xattn_"):
        o[p + "Wq"], o[p + "Wo"], o[p + "bo"] = kpn(a[p + "Wq"]), kpn(a[p + "Wo"]), a[p + "bo"].reshape(1, D)
        o[p + "WkT"], o[p + "WvT"] = kpn(a[p + "Wk"].T), kpn(a[p + "Wv"].T)
    p = "L1_xattn_"
    H1, DH = 16, 16
    o[p + "Wq"], o[p + "bq"] = kpn(a[p + "Wq"].T), cols(a[p + "bq"])
    wkv, bkv = a[p + "Wkv"].reshape(H1, 2, DH, CC), a[p + "bkv"].reshape(H1, 2, DH)
    o[p + "Wk"], o[p + "bk"] = wkv[:, 0].reshape(D, CC).T, cols(bkv[:, 0].reshape(D))
    o[p + "Wv"] = np.concatenate([wkv[:, 1].reshape(D, CC).T, bkv[:, 1].reshape(1, D)])
    o[p + "Wo"], o[p + "bo"] = kpn(a[p + "Wo"].T), a[p + "bo"].reshape(1, D)
    o[p + "pairs_mask"] = (np.arange(P)[:, None] // DH == np.arange(P // DH)[None]).astype(np.float32).reshape(P, 4, 2)
    own = (np.arange(P)[:, None] // S == np.arange(2)[None]).astype(np.float32)
    o[p + "own_channels"] = np.repeat(own, DH, axis=1)
    q = "L0_attn_"
    for n in ("pairs_mask", "own_channels"):
        o[q + n] = o[p + n]
    o[q + "causal"] = np.where(np.arange(S)[None] <= np.arange(P)[:, None] % S, 0.0, -1e30).astype(np.float32)
    o[q + "w_qkv"], o[q + "w_proj"], o[q + "ln_w"] = kpn(a[q + "w_qkv"]), kpn(a[q + "w_proj"]), a[q + "ln_w"]
    p = "L3_attn_"
    for n in ("in_proj_w", "x_proj_w", "dt_proj_w", "out_proj_w"):
        o[p + n] = kpn(a[p + n])
    for n in ("conv_b", "dt_proj_b", "D_param"):
        o[p + n] = cols(a[p + n])
    o[p + "conv_w"] = a[p + "conv_w"].reshape(4, P, 3).transpose(1, 0, 2)
    o[p + "A_log"] = a[p + "A_log"].reshape(4, P, 16).transpose(1, 2, 0)
    lower = np.tril(np.ones((E, E), np.float32), -1).reshape(E * E)

    def per_expert(m):
        return m.reshape(E, -1, P, m.shape[-1]).transpose(0, 2, 1, 3)

    p = "L0_ffn_"
    o[p + "lower"] = o["L1_ffn_lower"] = o["L2_ffn_lower"] = lower
    o[p + "gate_w"] = kpn(a[p + "gate_w"].T)
    o[p + "w1"], o[p + "w3"] = per_expert(a[p + "w1"]), per_expert(a[p + "w3"])
    whole = a[p + "w2"].shape[1] // P * P
    o[p + "w2"], o[p + "w2_tail"] = per_expert(a[p + "w2"][:, :whole]), a[p + "w2"][:, whole:]
    for n in ("sw1", "sw2", "sw3"):
        o[p + n] = kpn(a[p + n])
    p = "L1_ffn_"
    o[p + "router_W"], o[p + "router_b"] = kpn(a[p + "router_W"]), a[p + "router_b"].reshape(1, E)
    o[p + "W1"], o[p + "W2"] = per_expert(a[p + "W1"]), per_expert(a[p + "W2"])
    o[p + "b1"] = a[p + "b1"].reshape(E, -1, P).transpose(0, 2, 1)
    o[p + "b2"] = a[p + "b2"]
    p = "L2_ffn_"
    o[p + "Wg"], o[p + "bg"] = kpn(a[p + "Wg"]), a[p + "bg"].reshape(1, E)
    for n in ("W1", "W2", "W3"):
        o[p + n] = per_expert(a[p + n])
    o[p + "tri"] = np.triu(np.ones((P, P), np.float32))
    o[p + "iota"] = np.arange(1, int(T / E * 1.25) + 1, dtype=np.float32)
    for q in ("L0_ffn_", "L1_ffn_"):
        o[q + "tri"], o[q + "iota_slot"] = o[p + "tri"], np.arange(1, P + 1, dtype=np.float32)
        o[q + "tile_rows"] = P * np.arange(TILES, dtype=np.float32)
        o[q + "tile_no"], o[q + "expert_no"] = np.arange(TILES, dtype=np.float32), np.arange(E, dtype=np.float32)
    return o


def kernel(**inputs):
    import numpy as np
    import concourse.bacc as bacc
    from concourse.bass_utils import run_bass_kernel_spmd as run

    nc = bacc.Bacc("TRN2", target_bir_lowering=False, num_devices=1)
    arrays, w = {}, {}
    for name, a in layouts(inputs).items():
        a = np.ascontiguousarray(a)
        arrays[f"in_{name}"] = a
        w[name] = nc.dram_tensor(f"in_{name}", a.shape, mybir.dt.from_np(a.dtype), kind="ExternalInput").ap()
    out = nc.dram_tensor("out_0", (P, NT, D), F32, kind="ExternalOutput").ap()
    program(nc, w, out, STAGES)
    r = run(nc, [arrays], core_ids=[0])
    got = np.asarray(r.results[0]["out_0"])
    return got.transpose(1, 0, 2).reshape(B, S, D)
```
